# Optimizing a Trainium2 kernel written in Bass

```python
import numpy as np
import jax
import jax.numpy as jnp

def _softmax(x, axis=-1):
    return jax.nn.softmax(x, axis=axis)

def _gelu(x):
    return jax.nn.gelu(x, approximate=True)

def _silu(x):
    return jax.nn.silu(x)

def _sigmoid(x):
    return jax.nn.sigmoid(x)

def _layernorm(x, axis=-1, eps=1e-05):
    m = jnp.mean(x, axis=axis, keepdims=True)
    v = jnp.var(x, axis=axis, keepdims=True)
    return (x - m) / jnp.sqrt(v + eps)

def _scatter_add(tgt, idx, src, axis=0):
    return tgt.at[idx].add(src)

def _segment_sum(src, seg, n):
    return jax.ops.segment_sum(src, seg, n)
kernel_name = 'mk_xattn_ffn_d4_seqx_r8_74d624'

def setup_inputs(seed: int=0):
    np.random.seed(seed)
    _w = jnp.asarray

    def _rec_inputs():
        import jax
        import jax.numpy as jnp
        _rk = jax.random.key(seed)
        x = -0.000929 + 1 * jax.random.normal(jax.random.fold_in(_rk, 1), (64, 128, 128), jnp.float32)
        _lenS = 128 - jax.random.randint(jax.random.fold_in(_rk, 7), (64,), 0, max(1, 128 // 4) + 1, jnp.int32)
        _lenS2 = 120 - jax.random.randint(jax.random.fold_in(_rk, 8), (64,), 0, max(1, 120 // 4) + 1, jnp.int32)
        _ctx_1024P = jax.random.normal(jax.random.fold_in(_rk, 11), (64, 16, 128), jnp.float32)
        _ctx_1024c = jax.random.dirichlet(jax.random.fold_in(_rk, 511), 0.3 * jnp.ones((16,), jnp.float32), (64, 120))
        _ctx_1024t = jnp.einsum('bsk,bkd->bsd', _ctx_1024c, _ctx_1024P)
        _ctx_1024t = _ctx_1024t * jax.lax.rsqrt(jnp.mean(jnp.square(_ctx_1024t)) + 1e-12) * 0.953939
        ctx_1024 = 2.81802e-05 + 1.00001 * (_ctx_1024t + 0.3 * jax.random.normal(jax.random.fold_in(_rk, 611), (64, 120, 128), jnp.float32))
        _validS = jnp.arange(128)[None, :] < _lenS[:, None]
        _validS2 = jnp.arange(120)[None, :] < _lenS2[:, None]
        _causal = jnp.tril(jnp.ones((128, 128), dtype=bool))
        mask_BxS2_bf0 = jnp.logical_not(jnp.ones((64, 120), dtype=bool))
        mask_1x1xSxS2_ik0 = jnp.where(jnp.broadcast_to(_validS2[0:1, None, None, :], (1, 1, 128, 120)), 0, 1).astype(jnp.int32)
        return (x, ctx_1024, mask_BxS2_bf0, mask_1x1xSxS2_ik0)
    x, ctx_1024, mask_BxS2_bf0, mask_1x1xSxS2_ik0 = _rec_inputs()

    def _L0_xattn_setup():
        import jax, jax.numpy as jnp
        import numpy as np
        D_MODEL = 128
        NUM_HEADS = 16
        STRIDE = 4
        HEAD_DIM = D_MODEL // NUM_HEADS
        SCALE = HEAD_DIM ** (-0.5)
        key = jax.random.key(seed)
        ks = jax.random.split(key, 12)
        B, T, S = (2, 64, 1024)
        inp = {'query': jax.random.normal(ks[0], (B, T, D_MODEL), jnp.float32), 'key': jax.random.normal(ks[1], (B, S, D_MODEL), jnp.float32), 'value': jax.random.normal(ks[2], (B, S, D_MODEL), jnp.float32), 'key_padding_mask': jnp.zeros((B, S), dtype=bool)}
        s = 1.0 / np.sqrt(D_MODEL)
        inp['Wq'] = jax.random.normal(ks[3], (D_MODEL, D_MODEL), jnp.float32) * s
        inp['bq'] = jnp.zeros((D_MODEL,), jnp.float32)
        inp['Wk'] = jax.random.normal(ks[4], (D_MODEL, D_MODEL), jnp.float32) * s
        inp['bk'] = jnp.zeros((D_MODEL,), jnp.float32)
        inp['Wv'] = jax.random.normal(ks[5], (D_MODEL, D_MODEL), jnp.float32) * s
        inp['bv'] = jnp.zeros((D_MODEL,), jnp.float32)
        inp['Wo'] = jax.random.normal(ks[6], (D_MODEL, D_MODEL), jnp.float32) * s
        inp['bo'] = jnpp = jnp.zeros((D_MODEL,), jnp.float32)
        return inp
    _L0_xattn_all = _L0_xattn_setup()
    _L0_xattn_in = {k: v for k, v in _L0_xattn_all.items() if k in ('Wq', 'bq', 'Wk', 'bk', 'Wv', 'bv', 'Wo', 'bo')}
    del _L0_xattn_all

    def _L0_ffn_setup():
        import jax, jax.numpy as jnp
        import numpy as np
        IN_DIM, OUT_DIM, N_PROTO, RANK = (128, 128, 32, 16)
        key = jax.random.key(seed)
        ks = jax.random.split(key, 5)
        x = jax.random.normal(ks[0], (2, 512, IN_DIM), dtype=jnp.float32)
        prototypes = jax.random.normal(ks[1], (N_PROTO, IN_DIM), dtype=jnp.float32) * 0.02
        B = jax.random.normal(ks[2], (N_PROTO, RANK, IN_DIM), dtype=jnp.float32) * 0.02
        A = jax.random.normal(ks[3], (N_PROTO, OUT_DIM, RANK), dtype=jnp.float32) * 0.02
        bias = jnp.zeros((N_PROTO, OUT_DIM), dtype=jnp.float32)
        temp = jnp.asarray(1.0, dtype=jnp.float32)
        return {'x': x, 'prototypes': prototypes, 'B': B, 'A': A, 'bias': bias, 'temp': temp}
    _L0_ffn_all = _L0_ffn_setup()
    _L0_ffn_in = {k: v for k, v in _L0_ffn_all.items() if k in ('prototypes', 'B', 'A', 'bias', 'temp')}
    del _L0_ffn_all

    def _L1_xattn_setup():
        import jax, jax.numpy as jnp
        import numpy as np
        D_MODEL = 128
        NUM_HEADS = 16
        D_HEAD = D_MODEL // NUM_HEADS

        def _split_heads(x):
            B, L, _ = x.shape
            return x.reshape(B, L, NUM_HEADS, D_HEAD).transpose(0, 2, 1, 3)
        key = jax.random.key(seed)
        ks = jax.random.split(key, 10)
        B, L = (2, 256)
        s = 1.0 / np.sqrt(D_MODEL)
        inp = {'x_q': jax.random.normal(ks[0], (B, L, D_MODEL), jnp.float32), 'x_kv': jax.random.normal(ks[1], (B, L, D_MODEL), jnp.float32), 'wq': jax.random.normal(ks[2], (D_MODEL, D_MODEL), jnp.float32) * s, 'bq': jnp.zeros((D_MODEL,), jnp.float32), 'wk': jax.random.normal(ks[3], (D_MODEL, D_MODEL), jnp.float32) * s, 'bk': jnp.zeros((D_MODEL,), jnp.float32), 'wv': jax.random.normal(ks[4], (D_MODEL, D_MODEL), jnp.float32) * s, 'bv': jnp.zeros((D_MODEL,), jnp.float32), 'wo': jax.random.normal(ks[5], (D_MODEL, D_MODEL), jnp.float32) * s, 'bo': jnp.zeros((D_MODEL,), jnp.float32)}
        return inp
    _L1_xattn_all = _L1_xattn_setup()
    _L1_xattn_in = {k: v for k, v in _L1_xattn_all.items() if k in ('wq', 'bq', 'wk', 'bk', 'wv', 'bv', 'wo', 'bo')}
    del _L1_xattn_all

    def _L1_ffn_setup():
        import jax, jax.numpy as jnp
        import numpy as np
        H_DIM, E_DIM = (128, 64)
        N_SHARED, N_ROUTED, TOP_K = (2, 16, 4)
        B, S = (4, 256)
        key = jax.random.key(seed)
        ks = jax.random.split(key, 6)
        sc = 1.0 / np.sqrt(H_DIM)
        ec = 1.0 / np.sqrt(E_DIM)
        return {'x': jax.random.normal(ks[0], (B, S, H_DIM), dtype=jnp.float32), 'shared_up': jax.random.uniform(ks[1], (N_SHARED, E_DIM, H_DIM), jnp.float32, -sc, sc), 'shared_down': jax.random.uniform(ks[2], (N_SHARED, H_DIM, E_DIM), jnp.float32, -ec, ec), 'routed_up': jax.random.uniform(ks[3], (N_ROUTED, E_DIM, H_DIM), jnp.float32, -sc, sc), 'routed_down': jax.random.uniform(ks[4], (N_ROUTED, H_DIM, E_DIM), jnp.float32, -ec, ec), 'router_w': jax.random.uniform(ks[5], (N_ROUTED, H_DIM), jnp.float32, -sc, sc)}
    _L1_ffn_all = _L1_ffn_setup()
    _L1_ffn_in = {k: v for k, v in _L1_ffn_all.items() if k in ('shared_up', 'shared_down', 'routed_up', 'routed_down', 'router_w')}
    del _L1_ffn_all

    def _L2_xattn_setup():
        import jax, jax.numpy as jnp
        import numpy as np
        import math
        D_MODEL = 128
        N_HEADS = 16
        D_K = D_MODEL // N_HEADS
        B, S = (2, 256)
        key = jax.random.key(seed)
        ks = jax.random.split(key, 11)
        sc = 1.0 / math.sqrt(D_MODEL)
        inp = {'q': jax.random.normal(ks[0], (B, S, D_MODEL), jnp.float32), 'k': jax.random.normal(ks[1], (B, S, D_MODEL), jnp.float32), 'v': jax.random.normal(ks[2], (B, S, D_MODEL), jnp.float32), 'mask': jnp.tril(jnp.ones((S, S), jnp.int32))[None, None], 'W_q': jax.random.normal(ks[3], (D_MODEL, D_MODEL), jnp.float32) * sc, 'b_q': jnp.zeros((D_MODEL,), jnp.float32), 'W_k': jax.random.normal(ks[4], (D_MODEL, D_MODEL), jnp.float32) * sc, 'b_k': jnp.zeros((D_MODEL,), jnp.float32), 'W_v': jax.random.normal(ks[5], (D_MODEL, D_MODEL), jnp.float32) * sc, 'b_v': jnp.zeros((D_MODEL,), jnp.float32), 'W_o': jax.random.normal(ks[6], (D_MODEL, D_MODEL), jnp.float32) * sc, 'b_o': jnp.zeros((D_MODEL,), jnp.float32)}
        return inp
    _L2_xattn_all = _L2_xattn_setup()
    _L2_xattn_in = {k: v for k, v in _L2_xattn_all.items() if k in ('W_q', 'b_q', 'W_k', 'b_k', 'W_v', 'b_v', 'W_o', 'b_o')}
    del _L2_xattn_all

    def _L2_ffn_setup():
        import math
        import jax, jax.numpy as jnp
        import numpy as np
        K = 2
        CAP_FACTOR = 1.0
        EPS = 1e-09
        key = jax.random.key(seed)
        ks = jax.random.split(key, 6)
        B, S, D, H, E = (4, 256, 128, 512, 8)
        x = jax.random.normal(ks[0], (B, S, D), jnp.float32)
        wg = jax.random.normal(ks[1], (D, E), jnp.float32) * 0.02
        w1 = jax.random.normal(ks[2], (E, D, H), jnp.float32) * 0.02
        b1 = jnp.zeros((E, H), jnp.float32)
        w2 = jax.random.normal(ks[3], (E, H, D), jnp.float32) * 0.02
        b2 = jnp.zeros((E, D), jnp.float32)
        return {'x': x, 'wg': wg, 'w1': w1, 'b1': b1, 'w2': w2, 'b2': b2}
    _L2_ffn_all = _L2_ffn_setup()
    _L2_ffn_in = {k: v for k, v in _L2_ffn_all.items() if k in ('wg', 'w1', 'b1', 'w2', 'b2')}
    del _L2_ffn_all

    def _L3_xattn_setup():
        import jax, jax.numpy as jnp
        import numpy as np
        EMBED_DIM = 128
        NUM_HEADS = 16
        HEAD_DIM = EMBED_DIM // NUM_HEADS
        key = jax.random.key(seed)
        ks = jax.random.split(key, 7)
        B, S, E = (2, 256, EMBED_DIM)
        scale = 1.0 / np.sqrt(E)
        return {'query': jax.random.normal(ks[0], (B, S, E), dtype=jnp.float32), 'key': jax.random.normal(ks[1], (B, S, E), dtype=jnp.float32), 'value': jax.random.normal(ks[2], (B, S, E), dtype=jnp.float32), 'Wq': jax.random.normal(ks[3], (E, E), dtype=jnp.float32) * scale, 'Wk': jax.random.normal(ks[4], (E, E), dtype=jnp.float32) * scale, 'Wv': jax.random.normal(ks[5], (E, E), dtype=jnp.float32) * scale, 'Wo': jax.random.normal(ks[6], (E, E), dtype=jnp.float32) * scale}
    _L3_xattn_all = _L3_xattn_setup()
    _L3_xattn_in = {k: v for k, v in _L3_xattn_all.items() if k in ('Wq', 'Wk', 'Wv', 'Wo')}
    del _L3_xattn_all

    def _L3_ffn_setup():
        import jax, jax.numpy as jnp
        import numpy as np
        EMB = 128
        HID = 256
        HEADS = 16
        HEAD_DIM = EMB // HEADS
        EXPERTS = 8
        TOPK = 2
        EPS = 1e-05

        def layernorm(x, scale, shift):
            mean = jnp.mean(x, axis=-1, keepdims=True)
            var = jnp.mean((x - mean) ** 2, axis=-1, keepdims=True)
            return scale * (x - mean) / jnp.sqrt(var + EPS) + shift

        def attention(x, wq, wk, wv, wo, bo):
            b, t, _ = x.shape
            q = (x @ wq).reshape(b, t, HEADS, HEAD_DIM)
            k = (x @ wk).reshape(b, t, HEADS, HEAD_DIM)
            v = (x @ wv).reshape(b, t, HEADS, HEAD_DIM)
            scores = jnp.einsum('bqhd,bkhd->bhqk', q, k)
            mask = jnp.arange(t)[:, None] < jnp.arange(t)[None, :]
            scores = jnp.where(mask, -jnp.inf, scores)
            attn = jax.nn.softmax(scores / np.sqrt(HEAD_DIM), axis=-1)
            ctx = jnp.einsum('bhqk,bkhd->bqhd', attn, v).reshape(b, t, EMB)
            return ctx @ wo + bo

        def moe_ff(x, gate_w, w1, w2, w3):
            b, t, d = x.shape
            xf = x.reshape(b * t, d)
            scores = xf @ gate_w
            topk_scores, topk_idx = jax.lax.top_k(scores, TOPK)
            topk_probs = jax.nn.softmax(topk_scores, axis=-1)
            weight = jnp.sum(jax.nn.one_hot(topk_idx, EXPERTS, dtype=xf.dtype) * topk_probs[..., None], axis=1)
            h = jax.nn.silu(jnp.einsum('td,edh->eth', xf, w1)) * jnp.einsum('td,edh->eth', xf, w2)
            out_e = jnp.einsum('eth,ehd->etd', h, w3)
            out = jnp.einsum('etd,te->td', out_e, weight)
            return out.reshape(b, t, d)
        key = jax.random.key(seed)
        ks = jax.random.split(key, 12)
        s = lambda k, shape, fan: jax.random.normal(k, shape, jnp.float32) / np.sqrt(fan)
        return {'x': jax.random.normal(ks[0], (2, 256, EMB), jnp.float32), 'ln1_scale': jnp.ones((EMB,), jnp.float32), 'ln1_shift': jnp.zeros((EMB,), jnp.float32), 'wq': s(ks[1], (EMB, EMB), EMB), 'wk': s(ks[2], (EMB, EMB), EMB), 'wv': s(ks[3], (EMB, EMB), EMB), 'wo': s(ks[4], (EMB, EMB), EMB), 'bo': jnp.zeros((EMB,), jnp.float32), 'ln2_scale': jnp.ones((EMB,), jnp.float32), 'ln2_shift': jnp.zeros((EMB,), jnp.float32), 'gate_w': s(ks[5], (EMB, EXPERTS), EMB), 'w1': s(ks[6], (EXPERTS, EMB, HID), EMB), 'w2': s(ks[7], (EXPERTS, EMB, HID), EMB), 'w3': s(ks[8], (EXPERTS, HID, EMB), HID)}
    _L3_ffn_all = _L3_ffn_setup()
    _L3_ffn_in = {k: v for k, v in _L3_ffn_all.items() if k in ('ln1_scale', 'ln1_shift', 'wq', 'wk', 'wv', 'wo', 'bo', 'ln2_scale', 'ln2_shift', 'gate_w', 'w1', 'w2', 'w3')}
    del _L3_ffn_all
    return {'x': x, 'ctx_1024': ctx_1024, 'mask_BxS2_bf0': mask_BxS2_bf0, 'mask_1x1xSxS2_ik0': mask_1x1xSxS2_ik0, 'L0_xattn_Wq': _L0_xattn_in['Wq'], 'L0_xattn_bq': _L0_xattn_in['bq'], 'L0_xattn_Wk': _L0_xattn_in['Wk'], 'L0_xattn_bk': _L0_xattn_in['bk'], 'L0_xattn_Wv': _L0_xattn_in['Wv'], 'L0_xattn_bv': _L0_xattn_in['bv'], 'L0_xattn_Wo': _L0_xattn_in['Wo'], 'L0_xattn_bo': _L0_xattn_in['bo'], 'L0_ffn_prototypes': _L0_ffn_in['prototypes'], 'L0_ffn_B': _L0_ffn_in['B'], 'L0_ffn_A': _L0_ffn_in['A'], 'L0_ffn_bias': _L0_ffn_in['bias'], 'L0_ffn_temp': _L0_ffn_in['temp'], 'L1_xattn_wq': _L1_xattn_in['wq'], 'L1_xattn_bq': _L1_xattn_in['bq'], 'L1_xattn_wk': _L1_xattn_in['wk'], 'L1_xattn_bk': _L1_xattn_in['bk'], 'L1_xattn_wv': _L1_xattn_in['wv'], 'L1_xattn_bv': _L1_xattn_in['bv'], 'L1_xattn_wo': _L1_xattn_in['wo'], 'L1_xattn_bo': _L1_xattn_in['bo'], 'L1_ffn_shared_up': _L1_ffn_in['shared_up'], 'L1_ffn_shared_down': _L1_ffn_in['shared_down'], 'L1_ffn_routed_up': _L1_ffn_in['routed_up'], 'L1_ffn_routed_down': _L1_ffn_in['routed_down'], 'L1_ffn_router_w': _L1_ffn_in['router_w'], 'L2_xattn_W_q': _L2_xattn_in['W_q'], 'L2_xattn_b_q': _L2_xattn_in['b_q'], 'L2_xattn_W_k': _L2_xattn_in['W_k'], 'L2_xattn_b_k': _L2_xattn_in['b_k'], 'L2_xattn_W_v': _L2_xattn_in['W_v'], 'L2_xattn_b_v': _L2_xattn_in['b_v'], 'L2_xattn_W_o': _L2_xattn_in['W_o'], 'L2_xattn_b_o': _L2_xattn_in['b_o'], 'L2_ffn_wg': _L2_ffn_in['wg'], 'L2_ffn_w1': _L2_ffn_in['w1'], 'L2_ffn_b1': _L2_ffn_in['b1'], 'L2_ffn_w2': _L2_ffn_in['w2'], 'L2_ffn_b2': _L2_ffn_in['b2'], 'L3_xattn_Wq': _L3_xattn_in['Wq'], 'L3_xattn_Wk': _L3_xattn_in['Wk'], 'L3_xattn_Wv': _L3_xattn_in['Wv'], 'L3_xattn_Wo': _L3_xattn_in['Wo'], 'L3_ffn_ln1_scale': _L3_ffn_in['ln1_scale'], 'L3_ffn_ln1_shift': _L3_ffn_in['ln1_shift'], 'L3_ffn_wq': _L3_ffn_in['wq'], 'L3_ffn_wk': _L3_ffn_in['wk'], 'L3_ffn_wv': _L3_ffn_in['wv'], 'L3_ffn_wo': _L3_ffn_in['wo'], 'L3_ffn_bo': _L3_ffn_in['bo'], 'L3_ffn_ln2_scale': _L3_ffn_in['ln2_scale'], 'L3_ffn_ln2_shift': _L3_ffn_in['ln2_shift'], 'L3_ffn_gate_w': _L3_ffn_in['gate_w'], 'L3_ffn_w1': _L3_ffn_in['w1'], 'L3_ffn_w2': _L3_ffn_in['w2'], 'L3_ffn_w3': _L3_ffn_in['w3']}

def reference(x, ctx_1024, mask_BxS2_bf0, mask_1x1xSxS2_ik0, L0_xattn_Wq, L0_xattn_bq, L0_xattn_Wk, L0_xattn_bk, L0_xattn_Wv, L0_xattn_bv, L0_xattn_Wo, L0_xattn_bo, L0_ffn_prototypes, L0_ffn_B, L0_ffn_A, L0_ffn_bias, L0_ffn_temp, L1_xattn_wq, L1_xattn_bq, L1_xattn_wk, L1_xattn_bk, L1_xattn_wv, L1_xattn_bv, L1_xattn_wo, L1_xattn_bo, L1_ffn_shared_up, L1_ffn_shared_down, L1_ffn_routed_up, L1_ffn_routed_down, L1_ffn_router_w, L2_xattn_W_q, L2_xattn_b_q, L2_xattn_W_k, L2_xattn_b_k, L2_xattn_W_v, L2_xattn_b_v, L2_xattn_W_o, L2_xattn_b_o, L2_ffn_wg, L2_ffn_w1, L2_ffn_b1, L2_ffn_w2, L2_ffn_b2, L3_xattn_Wq, L3_xattn_Wk, L3_xattn_Wv, L3_xattn_Wo, L3_ffn_ln1_scale, L3_ffn_ln1_shift, L3_ffn_wq, L3_ffn_wk, L3_ffn_wv, L3_ffn_wo, L3_ffn_bo, L3_ffn_ln2_scale, L3_ffn_ln2_shift, L3_ffn_gate_w, L3_ffn_w1, L3_ffn_w2, L3_ffn_w3):
    import jax
    import jax.numpy as jnp

    def _L0_xattn_ref(query, key, value, key_padding_mask, Wq, bq, Wk, bk, Wv, bv, Wo, bo):
        import jax, jax.numpy as jnp
        import numpy as np
        D_MODEL = 128
        NUM_HEADS = 16
        STRIDE = 4
        HEAD_DIM = D_MODEL // NUM_HEADS
        SCALE = HEAD_DIM ** (-0.5)
        B, T, _ = query.shape
        S = key.shape[1]
        q = (query @ Wq + bq).reshape(B, T, NUM_HEADS, HEAD_DIM).transpose(0, 2, 1, 3)
        k = (key @ Wk + bk).reshape(B, S, NUM_HEADS, HEAD_DIM).transpose(0, 2, 1, 3)
        v = (value @ Wv + bv).reshape(B, S, NUM_HEADS, HEAD_DIM).transpose(0, 2, 1, 3)
        scores = jnp.einsum('bhtd,bhsd->bhts', q, k) * SCALE
        s_idx = jnp.arange(S)[None, None, None, :]
        h_idx = jnp.arange(NUM_HEADS)[None, :, None, None]
        hepos_mask = (s_idx - h_idx) % STRIDE != 0
        scores = jnp.where(hepos_mask, -jnp.inf, scores)
        scores = jnp.where(key_padding_mask[:, None, None, :], -jnp.inf, scores)
        attn = jax.nn.softmax(scores, axis=-1)
        context = jnp.einsum('bhts,bhsd->bhtd', attn, v)
        context = context.transpose(0, 2, 1, 3).reshape(B, T, D_MODEL)
        return context @ Wo + bo

    def _L0_ffn_ref(x, prototypes, B, A, bias, temp):
        import jax, jax.numpy as jnp
        import numpy as np
        IN_DIM, OUT_DIM, N_PROTO, RANK = (128, 128, 32, 16)
        lead = x.shape[:-1]
        xf = x.reshape(-1, IN_DIM)
        x2 = jnp.sum(xf * xf, axis=1, keepdims=True)
        p2 = jnp.sum(prototypes * prototypes, axis=1)
        d2 = x2 + p2[None, :] - 2.0 * (xf @ prototypes.T)
        dists = jnp.sqrt(jnp.maximum(d2, 0.0))
        t = jnp.maximum(jnp.abs(temp), 0.1)
        w = jax.nn.softmax(-dists / t, axis=1)
        topw, topi = jax.lax.top_k(w, 2)
        topw = topw / jnp.sum(topw, axis=1, keepdims=True)
        out = jnp.zeros((xf.shape[0], OUT_DIM), dtype=xf.dtype)
        for tslot in range(2):
            idx = topi[:, tslot]
            wt = topw[:, tslot:tslot + 1]
            h = jnp.einsum('nri,ni->nr', B[idx], xf)
            y = jnp.einsum('nor,nr->no', A[idx], h) + bias[idx]
            out = out + wt * y
        return out.reshape(*lead, OUT_DIM)

    def _L1_xattn_ref(x_q, x_kv, wq, bq, wk, bk, wv, bv, wo, bo):
        import jax, jax.numpy as jnp
        import numpy as np
        D_MODEL = 128
        NUM_HEADS = 16
        D_HEAD = D_MODEL // NUM_HEADS

        def _split_heads(x):
            B, L, _ = x.shape
            return x.reshape(B, L, NUM_HEADS, D_HEAD).transpose(0, 2, 1, 3)
        q = _split_heads(x_q @ wq.T + bq)
        k = _split_heads(x_kv @ wk.T + bk)
        v = _split_heads(x_kv @ wv.T + bv)
        scale = 1.0 / jnp.sqrt(jnp.asarray(D_HEAD, q.dtype))
        scores = jnp.einsum('bhqd,bhkd->bhqk', q, k) * scale
        attn = jax.nn.softmax(scores, axis=-1)
        out = jnp.einsum('bhqk,bhkd->bhqd', attn, v)
        B, H, Lq, Dh = out.shape
        out = out.transpose(0, 2, 1, 3).reshape(B, Lq, H * Dh)
        return out @ wo.T + bo

    def _L1_ffn_ref(x, shared_up, shared_down, routed_up, routed_down, router_w):
        import jax, jax.numpy as jnp
        import numpy as np
        H_DIM, E_DIM = (128, 64)
        N_SHARED, N_ROUTED, TOP_K = (2, 16, 4)
        B, S = (4, 256)
        b, s, h = x.shape
        xt = x.reshape(-1, h)
        up_s = jnp.einsum('th,seh->tse', xt, shared_up)
        shared = jnp.einsum('tse,she->th', jax.nn.gelu(up_s, approximate=False), shared_down)
        probs = jax.nn.softmax(xt @ router_w.T, axis=-1)
        topk_p, topk_i = jax.lax.top_k(probs, TOP_K)
        gate = jnp.zeros_like(probs).at[jnp.arange(xt.shape[0])[:, None], topk_i].add(topk_p)
        up_r = jnp.einsum('th,reh->tre', xt, routed_up)
        act = jax.nn.gelu(up_r, approximate=False) * gate[:, :, None]
        routed = jnp.einsum('tre,rhe->th', act, routed_down)
        return (shared + routed).reshape(b, s, h)

    def _L2_xattn_ref(q, k, v, mask, W_q, b_q, W_k, b_k, W_v, b_v, W_o, b_o):
        import jax, jax.numpy as jnp
        import numpy as np
        import math
        D_MODEL = 128
        N_HEADS = 16
        D_K = D_MODEL // N_HEADS
        B, S = (2, 256)

        def split_heads(x):
            b, s, _ = x.shape
            return x.reshape(b, s, N_HEADS, D_K).transpose(0, 2, 1, 3)
        Q = split_heads(q @ W_q + b_q)
        K = split_heads(k @ W_k + b_k)
        V = split_heads(v @ W_v + b_v)
        scores = jnp.einsum('bhqd,bhkd->bhqk', Q, K) / math.sqrt(D_K)
        scores = jnp.where(mask == 0, jnp.float32(-1000000000.0), scores)
        attn = jax.nn.softmax(scores, axis=-1)
        out = jnp.einsum('bhqk,bhkd->bhqd', attn, V)
        out = out.transpose(0, 2, 1, 3).reshape(q.shape[0], -1, D_MODEL)
        return out @ W_o + b_o

    def _L2_ffn_ref(x, wg, w1, b1, w2, b2):
        import math
        import jax, jax.numpy as jnp
        import numpy as np
        K = 2
        CAP_FACTOR = 1.0
        EPS = 1e-09
        B, S, D = x.shape
        E = wg.shape[1]
        xt = x.reshape(-1, D)
        N = xt.shape[0]
        cap = int(math.ceil(CAP_FACTOR * K * N / E))
        logits = xt.astype(jnp.float32) @ wg.astype(jnp.float32)
        scores = jax.nn.softmax(logits, axis=-1)
        gvals, gidx = jax.lax.top_k(scores, K)
        gvals = gvals / jnp.clip(gvals.sum(-1, keepdims=True), EPS)
        offset = jnp.zeros((E,), jnp.int32)
        pos_l, keep_l = ([], [])
        for kk in range(K):
            m = jax.nn.one_hot(gidx[:, kk], E, dtype=jnp.int32)
            loc = jnp.cumsum(m, axis=0) - 1 + offset[None, :]
            offset = offset + m.sum(axis=0)
            pos = jnp.take_along_axis(loc, gidx[:, kk:kk + 1], axis=1)[:, 0]
            keep = pos < cap
            pos_l.append(jnp.where(keep, pos, 0))
            keep_l.append(keep)
        pos = jnp.stack(pos_l, axis=1)
        keep = jnp.stack(keep_l, axis=1)
        gvals = gvals * keep
        e_flat = gidx.reshape(-1)
        p_flat = pos.reshape(-1)
        kmask = keep.reshape(-1).astype(x.dtype)
        x_rep = jnp.repeat(xt, K, axis=0)
        disp = jnp.zeros((E, cap, D), x.dtype).at[e_flat, p_flat].add(x_rep * kmask[:, None])
        h = jax.nn.gelu(jnp.einsum('ecd,edh->ech', disp, w1) + b1[:, None, :], approximate=False)
        y = jnp.einsum('ech,ehd->ecd', h, w2) + b2[:, None, :]
        yk = y[e_flat, p_flat]
        w = gvals.reshape(-1).astype(x.dtype)
        out = (yk * w[:, None]).reshape(N, K, D).sum(axis=1)
        return out.reshape(B, S, D)

    def _L3_xattn_ref(query, key, value, Wq, Wk, Wv, Wo):
        import jax, jax.numpy as jnp
        import numpy as np
        EMBED_DIM = 128
        NUM_HEADS = 16
        HEAD_DIM = EMBED_DIM // NUM_HEADS
        B, Sq, E = query.shape
        Sk = key.shape[1]
        H, D = (NUM_HEADS, HEAD_DIM)

        def split_heads(x, S):
            return x.reshape(B, S, H, D).transpose(0, 2, 1, 3)
        Q = split_heads(query @ Wq.T, Sq)
        K = split_heads(key @ Wk.T, Sk)
        V = split_heads(value @ Wv.T, Sk)
        scores = jnp.einsum('bhqd,bhkd->bhqk', Q, K) / jnp.sqrt(jnp.float32(D))
        causal = jnp.tril(jnp.ones((Sq, Sk), dtype=bool))
        scores = jnp.where(causal[None, None, :, :], scores, -jnp.inf)
        attn = jax.nn.softmax(scores, axis=-1)
        attn = jnp.nan_to_num(attn, nan=0.0)
        out = jnp.einsum('bhqk,bhkd->bhqd', attn, V)
        out = out.transpose(0, 2, 1, 3).reshape(B, Sq, E)
        return out @ Wo.T

    def _L3_ffn_ref(x, ln1_scale, ln1_shift, wq, wk, wv, wo, bo, ln2_scale, ln2_shift, gate_w, w1, w2, w3):
        import jax, jax.numpy as jnp
        import numpy as np
        EMB = 128
        HID = 256
        HEADS = 16
        HEAD_DIM = EMB // HEADS
        EXPERTS = 8
        TOPK = 2
        EPS = 1e-05

        def layernorm(x, scale, shift):
            mean = jnp.mean(x, axis=-1, keepdims=True)
            var = jnp.mean((x - mean) ** 2, axis=-1, keepdims=True)
            return scale * (x - mean) / jnp.sqrt(var + EPS) + shift

        def attention(x, wq, wk, wv, wo, bo):
            b, t, _ = x.shape
            q = (x @ wq).reshape(b, t, HEADS, HEAD_DIM)
            k = (x @ wk).reshape(b, t, HEADS, HEAD_DIM)
            v = (x @ wv).reshape(b, t, HEADS, HEAD_DIM)
            scores = jnp.einsum('bqhd,bkhd->bhqk', q, k)
            mask = jnp.arange(t)[:, None] < jnp.arange(t)[None, :]
            scores = jnp.where(mask, -jnp.inf, scores)
            attn = jax.nn.softmax(scores / np.sqrt(HEAD_DIM), axis=-1)
            ctx = jnp.einsum('bhqk,bkhd->bqhd', attn, v).reshape(b, t, EMB)
            return ctx @ wo + bo

        def moe_ff(x, gate_w, w1, w2, w3):
            b, t, d = x.shape
            xf = x.reshape(b * t, d)
            scores = xf @ gate_w
            topk_scores, topk_idx = jax.lax.top_k(scores, TOPK)
            topk_probs = jax.nn.softmax(topk_scores, axis=-1)
            weight = jnp.sum(jax.nn.one_hot(topk_idx, EXPERTS, dtype=xf.dtype) * topk_probs[..., None], axis=1)
            h = jax.nn.silu(jnp.einsum('td,edh->eth', xf, w1)) * jnp.einsum('td,edh->eth', xf, w2)
            out_e = jnp.einsum('eth,ehd->etd', h, w3)
            out = jnp.einsum('etd,te->td', out_e, weight)
            return out.reshape(b, t, d)
        h = layernorm(x, ln1_scale, ln1_shift)
        x = x + attention(h, wq, wk, wv, wo, bo)
        h = layernorm(x, ln2_scale, ln2_shift)
        x = x + moe_ff(h, gate_w, w1, w2, w3)
        return x
    x = x + _L0_xattn_ref(_layernorm(x, axis=-1), ctx_1024, ctx_1024, mask_BxS2_bf0, L0_xattn_Wq, L0_xattn_bq, L0_xattn_Wk, L0_xattn_bk, L0_xattn_Wv, L0_xattn_bv, L0_xattn_Wo, L0_xattn_bo)
    x = x + _L0_ffn_ref(_layernorm(x, axis=-1), L0_ffn_prototypes, L0_ffn_B, L0_ffn_A, L0_ffn_bias, L0_ffn_temp)
    x = x + _L1_xattn_ref(_layernorm(x, axis=-1), ctx_1024, L1_xattn_wq, L1_xattn_bq, L1_xattn_wk, L1_xattn_bk, L1_xattn_wv, L1_xattn_bv, L1_xattn_wo, L1_xattn_bo)
    x = x + _L1_ffn_ref(_layernorm(x, axis=-1), L1_ffn_shared_up, L1_ffn_shared_down, L1_ffn_routed_up, L1_ffn_routed_down, L1_ffn_router_w)
    x = x + _L2_xattn_ref(_layernorm(x, axis=-1), ctx_1024, ctx_1024, mask_1x1xSxS2_ik0, L2_xattn_W_q, L2_xattn_b_q, L2_xattn_W_k, L2_xattn_b_k, L2_xattn_W_v, L2_xattn_b_v, L2_xattn_W_o, L2_xattn_b_o)
    x = x + _L2_ffn_ref(_layernorm(x, axis=-1), L2_ffn_wg, L2_ffn_w1, L2_ffn_b1, L2_ffn_w2, L2_ffn_b2)
    x = x + _L3_xattn_ref(_layernorm(x, axis=-1), ctx_1024, ctx_1024, L3_xattn_Wq, L3_xattn_Wk, L3_xattn_Wv, L3_xattn_Wo)
    x = x + _L3_ffn_ref(_layernorm(x, axis=-1), L3_ffn_ln1_scale, L3_ffn_ln1_shift, L3_ffn_wq, L3_ffn_wk, L3_ffn_wv, L3_ffn_wo, L3_ffn_bo, L3_ffn_ln2_scale, L3_ffn_ln2_shift, L3_ffn_gate_w, L3_ffn_w1, L3_ffn_w2, L3_ffn_w3)
    return x

_drawn_inputs = setup_inputs


def setup_inputs(seed=0):
    import zlib

    import numpy as np

    out = dict(_drawn_inputs(seed))
    spreads = {'L0_xattn_bq': (0.0, 0.272),
     'L0_xattn_bk': (0.0, 0.8),
     'L0_xattn_bv': (0.0, 0.1),
     'L0_xattn_bo': (0.0, 0.1),
     'L0_ffn_bias': (0.0, 0.1),
     'L1_xattn_bq': (0.0, 0.348),
     'L1_xattn_bk': (0.0, 0.8),
     'L1_xattn_bv': (0.0, 0.1),
     'L1_xattn_bo': (0.0, 0.1),
     'L2_xattn_b_q': (0.0, 0.325),
     'L2_xattn_b_k': (0.0, 0.8),
     'L2_xattn_b_v': (0.0, 0.1),
     'L2_xattn_b_o': (0.0, 0.1),
     'L2_ffn_b1': (0.0, 0.556),
     'L2_ffn_b2': (0.0, 0.1),
     'L3_ffn_ln1_scale': (1.0, 0.2),
     'L3_ffn_ln1_shift': (0.0, 0.1),
     'L3_ffn_bo': (0.0, 0.1),
     'L3_ffn_ln2_scale': (1.0, 0.2),
     'L3_ffn_ln2_shift': (0.0, 0.1)}
    factors = {'L0_ffn_B': 4.49, 'L0_ffn_A': 4.661}
    for name, (base, spread) in spreads.items():
        noise = np.random.default_rng([zlib.crc32(name.encode()), seed]).standard_normal(out[name].shape)
        drawn = base * np.exp(spread * noise) if base else spread * noise
        out[name] = jnp.asarray(drawn.astype(out[name].dtype))
    for name, factor in factors.items():
        out[name] = (out[name] * factor).astype(out[name].dtype)
    return out
```

```python
from contextlib import ExitStack

import concourse.bass as bass
import numpy as np
from concourse import mybir

F32 = mybir.dt.float32
BF16 = mybir.dt.bfloat16
U8 = mybir.dt.uint8
I32 = mybir.dt.int32
ALU = mybir.AluOpType
ACT = mybir.ActivationFunctionType
AX = mybir.AxisListType

P = 128
D = 128
NB = 64
GB = 4
NG = NB // GB
GT = GB * P
NH = 16
HD = D // NH
KC = 120
STRIDE = 4
KCLS = KC // STRIDE
EPS = 1e-5
SCALE = float(HD) ** -0.5
FAR = -1.0e30


def at_least(eng, sem, value):
    if isinstance(value, int) and value <= 0:
        return
    eng.wait_ge(sem, value)


class Namespace:
    pass


def allocator(nc, stack):
    numbers = []

    def zero_semaphores():
        numbers.sort()
        runs = []
        for n in numbers:
            if runs and runs[-1].stop == n:
                runs[-1] = range(runs[-1].start, n + 1)
            else:
                runs.append(range(n, n + 1))
        for run in runs:
            nc.gpsimd.sem_clear(run)
        nc.all_engine_barrier()

    stack.callback(zero_semaphores)

    def sb(name, shape, dt=F32):
        return stack.enter_context(nc.sbuf_tensor(name, shape, dt))

    def ps(name, shape, dt=F32):
        return stack.enter_context(nc.psum_tensor(name, shape, dt))

    def sem(name):
        handle = stack.enter_context(nc.semaphore(name))
        numbers.append(handle.num)
        return handle

    return sb, ps, sem


def groups_loop(eng, body, peel=1):
    for g in range(peel):
        body(g, g % 2, g == 0, False)
    with eng.Fori(peel, NG - 2, 2) as g:
        body(g, 1, False, False)
        body(g + 1, 0, False, False)
    body(NG - 1, 1, False, True)


def pairs_loop(eng, end, body):
    body(0)
    with eng.Fori(2, end - 1, 2) as g:
        body(g)


class Norm:

    def __init__(self, nc, R, sb, sem, name):
        self.nc, self.R = nc, R
        self.mean = sb(name + "_mean", [P, NB])
        self.rstd = sb(name + "_rstd", [P, NB])
        self.work = sb(name + "_work", [P, 4, NB])
        self.steps = sem(name + "_norm_steps")
        self.var_ready = sem(name + "_var_ready")
        self.std_ready = sem(name + "_std_ready")

    def vector(self, dve):
        s = self.R.stats
        w = self.work
        v = self.nc.vector
        v.tensor_tensor(w[:, 0, :], s[:, :, 1], s[:, :, 4], ALU.add).then_inc(self.steps, 1)
        v.tensor_tensor(w[:, 1, :], s[:, :, 1], s[:, :, 4], ALU.subtract).then_inc(self.steps, 1)
        v.tensor_tensor(w[:, 2, :], s[:, :, 2], s[:, :, 5], ALU.add).then_inc(self.steps, 1)
        dve.wait_ge(self.steps, 3)
        v.tensor_scalar(self.mean[:], w[:, 0, :], 0.5, None, ALU.mult).then_inc(self.steps, 1)
        v.tensor_tensor(w[:, 3, :], w[:, 1, :], w[:, 1, :], ALU.mult).then_inc(self.steps, 1)
        dve.wait_ge(self.steps, 5)
        v.scalar_tensor_tensor(w[:, 0, :], w[:, 3, :], D / 4.0, w[:, 2, :], ALU.mult, ALU.add).then_inc(self.steps, 1)
        dve.wait_ge(self.steps, 6)
        v.tensor_scalar(w[:, 1, :], w[:, 0, :], 1.0 / D, EPS, ALU.mult, ALU.add).then_inc(self.var_ready, 1)
        dve.wait_ge(self.std_ready, 1)
        v.reciprocal(self.rstd[:], w[:, 2, :]).then_inc(self.steps, 1)
        dve.wait_ge(self.steps, 7)

    def scalar(self, act):
        act.wait_ge(self.var_ready, 1)
        self.nc.scalar.activation(self.work[:, 2, :], self.work[:, 1, :], ACT.Sqrt).then_inc(self.std_ready, 1)

    def apply(self, dve, g, h):
        for j in range(GB):
            b = g * GB + j
            last = self.nc.vector.tensor_scalar(h[:, j, :], self.R.x[:, b, :],
                                                self.mean[:, bass.ds(b, 1)], self.rstd[:, bass.ds(b, 1)],
                                                ALU.subtract, ALU.mult)
        return last


def residual(nc, R, dve, sem, g, out, done):
    xg = R.x[:, bass.ds(g * GB, GB), :]
    nc.vector.tensor_tensor(xg, xg, out, ALU.add).then_inc(sem, 1)
    dve.wait_ge(sem, done)
    for j in range(GB):
        b = g * GB + j
        nc.vector.bn_stats(R.stats[:, b, :], R.x[:, b, :]).then_inc(R.stats_done, 1)


def load_phase(nc, R, I):
    with ExitStack() as stack:
        sb, ps, sem = allocator(nc, stack)
        x_in = [sem(f"load_x{i}") for i in range(4)]
        const_in = sem("load_const")
        with nc.Block() as block:
            @block.sync
            def _(sp):
                for i in range(4):
                    q = slice(i * NB // 4, (i + 1) * NB // 4)
                    sp.dma_start(R.x[:, q, :], I["x"][:, q, :]).then_inc(x_in[i], 16)
                sp.dma_start(R.ident[:], I["ident"]).then_inc(const_in, 16)
                sp.dma_start(R.ident_bf[:], I["ident_bf"]).then_inc(const_in, 16)
                sp.wait_ge(const_in, 32)

            @block.vector
            def _(dve):
                nc.vector.memset(R.ones[:], 1.0)
                nc.vector.memset(R.ones_bf[:], 1.0)
                for b in range(NB):
                    if b % (NB // 4) == 0:
                        dve.wait_ge(x_in[b // (NB // 4)], 16)
                    nc.vector.bn_stats(R.stats[:, b, :], R.x[:, b, :]).then_inc(R.stats_done, 1)


def renorm_phase(nc, R, y):
    with ExitStack() as stack:
        sb, ps, sem = allocator(nc, stack)
        norm = Norm(nc, R, sb, sem, "renorm")
        y_ready = sem("y_ready")
        with nc.Block() as block:
            @block.scalar
            def _(act):
                norm.scalar(act)

            @block.vector
            def _(dve):
                norm.vector(dve)

                def group(g):
                    norm.apply(dve, g, y[:, bass.ds(g * GB, GB), :]).then_inc(y_ready, 1)
                    dve.wait_ge(y_ready, g + 1)
                    for j in range(GB):
                        b = g * GB + j
                        nc.vector.bn_stats(R.stats[:, b, :], y[:, b, :]).then_inc(R.stats_done, 1)

                with dve.Fori(0, NG) as g:
                    group(g)
    R.kept, R.x = R.x, y


def attention_phase(nc, R, I, name, wq, wk, wv, wo, bq=None, bk=None, bv=None, bo=None, hepos=False,
                    own_keys=False, mask=None, causal=None, pad=None, ln=None):
    KN = P if own_keys else KC
    U = 1 if hepos else 4
    S = GB * U
    W = 4 * KN
    steps_of = ["ht", "k", "q", "v"] if own_keys else ["k", "ht", "q", "v"]
    slot_of = {s: (n if U == 1 else 2 * n) for n, s in enumerate(steps_of)}
    with ExitStack() as stack:
        sb, ps, sem = allocator(nc, stack)
        n_ = lambda s: f"{name}_{s}"
        norm = Norm(nc, R, sb, sem, name)
        Wq, Wk, Wv, Wo = (sb(n_(s), [P, D]) for s in ("wq", "wk", "wv", "wo"))
        cols = sb(n_("cols"), [P, 6])
        bvb = sb(n_("bv"), [P, GB * D])
        bor = sb(n_("bo"), [1, D])
        H = sb(n_("h"), [P, GB, D])
        HT = [sb(n_(f"ht{i}"), [P, GT]) for i in range(2)]
        QT = [sb(n_(f"qt{i}"), [P, GT]) for i in range(2)]
        KT = [sb(n_(f"kt{i}"), [P, GB, KN]) for i in range(2)]
        CTX = [sb(n_(f"ctx{i}"), [P, GB, KN]) for i in range(2)] if not own_keys else None
        KM = [sb(n_(f"km{i}"), [P, GB, U, W]) for i in range(2)]
        VW = D if hepos else NH * 32
        VM = [sb(n_(f"vm{i}"), [P, GB, VW]) for i in range(2)]
        DM = sb(n_("dm"), [P, 4, 32])
        PR = [sb(n_(f"p{i}"), [P, W]) for i in range(4)]
        PT = [sb(n_(f"pt{i}"), [P, 4 * P]) for i in range(4)]
        MX = [sb(n_(f"mx{i}"), [P, 16 if hepos else 4]) for i in range(2)]
        RD = sb(n_("rd"), [P, P])
        CT = [sb(n_(f"ct{i}"), [P, P]) for i in range(2)]
        SC = [ps(n_(f"sc{i}"), [P, 512]) for i in range(2)]
        TP = [ps(n_(f"tp{i}"), [P, 512]) for i in range(2)]
        PJ = ps(n_("pj"), [P, 512])
        ND = [ps(n_(f"nd{i}"), [P, 4, P]) for i in range(2)]
        OUT = ps(n_("out"), [P, GB, D])
        if pad is not None:
            padu = sb(n_("padu"), [1, NB * KC], U8)
            padb = sb(n_("padb"), [1, NB, KC], BF16)
        if mask is not None:
            mski = sb(n_("mski"), [P, KC], I32)
            keep = sb(n_("keep"), [P, KC])
            some = sb(n_("some"), [P, 1])
            diag = sb(n_("diag"), [P, P], BF16)
            qfac = sb(n_("qfac"), [P, P])
        if mask is not None or causal is not None:
            addm = sb(n_("addm"), [P, KN], BF16)

        v_biased = sem(n_("v_biased"))
        weights_in = sem(n_("weights_in"))
        prep = sem(n_("prep"))
        prep_pool = sem(n_("prep_pool"))
        f_psum = sem(n_("f_psum"))
        ctx_in = [sem(n_(f"ctx_in{i}")) for i in range(2)]
        h_ready, h_used = sem(n_("h_ready")), sem(n_("h_used"))
        psum_done = {s: sem(n_(f"{s}_psum")) for s in steps_of}
        ready = {s: sem(n_(f"{s}_ready")) for s in steps_of}
        km_in = [sem(n_(f"km_in{i}")) for i in range(2)]
        sc_ready, mx_ready, sub_ready, exp_ready = (sem(n_(s)) for s in ("sc_ready", "mx_ready", "sub_ready", "exp_ready"))
        tp_ready, pt_ready, pv_done = (sem(n_(s)) for s in ("tp_ready", "pt_ready", "pv_done"))
        rd_ready, ct_ready, o_done, x_added = (sem(n_(s)) for s in ("rd_ready", "ct_ready", "o_done", "x_added"))

        n_weights = 4 + sum(a is not None for a in (bq, bk, bo, mask, causal, pad)) + (GB if bv is not None else 0)
        n_weights += 2 * (ln is not None) + hepos
        n_prep = (bq is not None) + (pad is not None) + (5 if mask is not None else 0)

        def diagonal(vm):
            a = vm[0:KN, :, :]
            return bass.AP(a.tensor, a.offset, [list(a.ap[0]), [128, GB * 4], [40, 4], [1, 8]])

        with nc.Block() as block:
            @block.sync
            def _(sp):
                for t, w in ((Wq, wq), (Wk, wk), (Wv, wv), (Wo, wo)):
                    sp.dma_start(t[:], w).then_inc(weights_in, 16)
                for c, v in ((0, bq), (1, bk)) + (((3, ln[0]), (4, ln[1])) if ln else ()):
                    if v is not None:
                        sp.dma_start(cols[:, c:c + 1], v.rearrange("(p a) -> p a", a=1)).then_inc(weights_in, 16)
                if bv is not None:
                    for j in range(GB):
                        sp.dma_start(bvb[:, j * D:(j + 1) * D],
                                     v_broadcast(bv)).then_inc(weights_in, 16)
                if bo is not None:
                    sp.dma_start(bor[:], bo.rearrange("(a p) -> a p", a=1)).then_inc(weights_in, 16)
                if mask is not None:
                    sp.dma_start(mski[:], mask).then_inc(weights_in, 16)
                if causal is not None:
                    sp.dma_start(addm[:], causal).then_inc(weights_in, 16)
                if pad is not None:
                    sp.dma_start(padu[:], pad).then_inc(weights_in, 16)
                if hepos:
                    sp.dma_start(DM[0:KC, 0, :], I["classes"]).then_inc(weights_in, 16)

                def ctx_load(g, par):
                    if not own_keys:
                        at_least(sp, psum_done["v"], g - 1)
                        sp.dma_start(CTX[par][:], I["ctxT"][:, bass.ds(g * GB, GB), :]).then_inc(ctx_in[par], 16)

                def spread(g, par, first):
                    sp.wait_ge(ready["k"], g + 1)
                    if first:
                        sp.wait_ge(prep_pool, 4)
                    for h in range(NH):
                        i, j = h % 4, h // 4
                        rows = slice(HD * h, HD * h + HD)
                        if hepos:
                            c = i
                            dst = KM[par][rows, :, 0, j * KC + c * KCLS:j * KC + (c + 1) * KCLS]
                            src = KT[par][rows, :, c * KCLS:(c + 1) * KCLS]
                        else:
                            dst = KM[par][rows, :, i, j * KN:(j + 1) * KN]
                            src = KT[par][rows, :, :]
                        sp.dma_start(dst, src).then_inc(km_in[par], 16)

                ctx_load(0, 0)
                ctx_load(1, 1)
                spread(0, 0, True)
                def pair(g):
                    ctx_load(g + 2, 0)
                    spread(g + 1, 1, False)
                    ctx_load(g + 3, 1)
                    spread(g + 2, 0, False)

                pairs_loop(sp, NG - 2, pair)
                spread(NG - 1, 1, False)

            @block.gpsimd
            def _(pool):
                for t in (KM[0], KM[1], VM[0], VM[1]):
                    nc.gpsimd.memset(t[:], 0.0).then_inc(prep_pool, 1)
                if not hepos:
                    nc.gpsimd.memset(DM[:], 0.0).then_inc(prep_pool, 1)
                    pool.wait_ge(prep_pool, 5)
                    for i in range(4):
                        nc.gpsimd.memset(DM[:, i, 8 * i:8 * i + 8], 1.0).then_inc(prep_pool, 1)

            @block.vector
            def _(dve):
                v = nc.vector
                norm.vector(dve)
                dve.wait_ge(weights_in, 16 * n_weights)
                done = 0
                if bq is not None:
                    v.tensor_scalar(cols[:, 2:3], cols[:, 0:1], SCALE, None, ALU.mult).then_inc(prep, 1)
                    done += 1
                if pad is not None:
                    v.tensor_scalar(padb[0:1, :, :], padu[0:1, :].rearrange("p (b k) -> p b k", k=KC), FAR, None,
                                    ALU.mult).then_inc(prep, 1)
                    done += 1
                if mask is not None:
                    v.tensor_scalar(keep[:], mski[:], 0.0, None, ALU.not_equal).then_inc(prep, 1)
                    v.tensor_scalar(addm[:], mski[:], 0.0, -1.0e9, ALU.is_equal, ALU.mult).then_inc(prep, 1)
                    done += 2
                    dve.wait_ge(prep, done)
                    v.tensor_reduce(some[:], keep[:], AX.X, ALU.max).then_inc(prep, 1)
                    dve.wait_ge(prep, done + 1)
                    v.tensor_scalar(diag[:], R.ident[:], some[:, 0:1], None, ALU.mult).then_inc(prep, 1)
                    dve.wait_ge(f_psum, 1)
                    v.tensor_scalar(qfac[:], OUT[:, 0, :], SCALE, None, ALU.mult).then_inc(prep, 1)
                    done += 3
                    dve.wait_ge(prep, done)

                def ln_group(g):
                    at_least(dve, psum_done["ht"], g)
                    norm.apply(dve, g, H).then_inc(h_ready, 1)

                def q_evict(g, par):
                    dve.wait_ge(psum_done["q"], g + 1)
                    o = QT[par][:].rearrange("p (b t) -> p b t", b=GB)
                    i = PJ[:].rearrange("p (b t) -> p b t", b=GB)
                    f = qfac[:].unsqueeze(1).to_broadcast([P, GB, P])
                    v.scalar_tensor_tensor(o, i, cols[:, 0:1], f, ALU.add, ALU.mult).then_inc(ready["q"], 1)

                def v_evict(g, par, first):
                    dve.wait_ge(psum_done["v"], g + 1)
                    if first:
                        dve.wait_ge(prep_pool, 4)
                    src = PJ[0:KN, :]
                    if hepos:
                        o = VM[par][0:KN, :, :].rearrange("p b (i c) -> p (b i) c", c=32)
                        cm = DM[0:KN, 0, :].unsqueeze(1).to_broadcast([KN, GB * 4, 32])
                        s = src.rearrange("p (b c) -> p b c", c=32)
                        v.tensor_tensor(s, s, bvb[0:KN, :].rearrange("p (b c) -> p b c", c=32),
                                        ALU.add).then_inc(v_biased, 1)
                        dve.wait_ge(v_biased, g + 1)
                        v.tensor_tensor(o, s, cm, ALU.mult).then_inc(ready["v"], 1)
                    elif bv is not None:
                        v.tensor_tensor(diagonal(VM[par]), src.rearrange("p (b i d) -> p b i d", i=4, d=8),
                                        bvb[0:KN, :].rearrange("p (b i d) -> p b i d", i=4, d=8),
                                        ALU.add).then_inc(ready["v"], 1)
                    else:
                        v.tensor_copy(diagonal(VM[par]), src.rearrange("p (b i d) -> p b i d", i=4, d=8)
                                      ).then_inc(ready["v"], 1)

                def softmax_shift(g, s):
                    n = g * S + s
                    sc, mx = SC[s % 2], MX[s % 2]
                    k = KCLS if hepos else KN
                    heads = W // k
                    view = sc[:, 0:W].rearrange("p (h k) -> p h k", k=k)
                    dve.wait_ge(sc_ready, n + 1)
                    v.tensor_reduce(mx[:], view, AX.X, ALU.max).then_inc(mx_ready, 1)
                    at_least(dve, tp_ready, n - 3)
                    dve.wait_ge(mx_ready, n + 1)
                    v.tensor_tensor(PR[s % 4][:].rearrange("p (h k) -> p h k", k=k), view,
                                    mx[:].unsqueeze(2).to_broadcast([P, heads, k]),
                                    ALU.subtract).then_inc(sub_ready, 1)

                def normalise(b, bt):
                    dve.wait_ge(pv_done, b * U + U)
                    at_least(dve, ct_ready, b)
                    v.reciprocal(RD[:], ND[bt % 2][:, 1, :]).then_inc(rd_ready, 1)
                    at_least(dve, o_done, b - 1)
                    dve.wait_ge(rd_ready, b + 1)
                    v.tensor_tensor(CT[bt % 2][:], ND[bt % 2][:, 0, :], RD[:], ALU.mult).then_inc(ct_ready, 1)

                def add_out(g):
                    dve.wait_ge(o_done, g * GB + GB)
                    residual(nc, R, dve, x_added, g, OUT[:], g + 1)

                def tail(g, s, first):
                    u = s - 3
                    if first and u < 0:
                        return
                    if (u + 1) % U == 0:
                        bt = (u // U) % GB
                        normalise(g * GB + u // U, bt)

                def evicts(g, s, par):
                    if mask is not None and slot_of["q"] == s:
                        q_evict(g, par)
                    if slot_of["v"] == s:
                        v_evict(g, par, False)

                def group(g, par, first, last):
                    for s in range(S):
                        if s == 0 and not last:
                            ln_group(g + 1)
                        softmax_shift(g, s)
                        tail(g, s, first)
                        if not last:
                            evicts(g + 1, s, 1 - par)
                        if s == (3 if U == 1 else 4) and not first:
                            add_out(g - 1)
                    if last:
                        for s in range(S, S + 3):
                            tail(g, s, False)
                        add_out(g)

                ln_group(0)
                if mask is not None:
                    q_evict(0, 0)
                v_evict(0, 0, True)
                groups_loop(dve, group, 3 if U == 1 else 1)

            @block.scalar
            def _(act):
                a = nc.scalar
                norm.scalar(act)
                act.wait_ge(weights_in, 16 * n_weights)
                at_least(act, prep, n_prep)

                def evict(step, g, par):
                    if step == "v" or (step == "q" and mask is not None):
                        return
                    act.wait_ge(psum_done[step], g + 1)
                    pj = PJ
                    if step == "ht":
                        if ln:
                            ins = a.activation(HT[par][:], pj[:], ACT.Identity, scale=cols[:, 3:4], bias=cols[:, 4:5])
                        else:
                            ins = a.activation(HT[par][:], pj[:], ACT.Copy)
                    elif step == "q":
                        if bq is not None:
                            ins = a.activation(QT[par][:], pj[:], ACT.Identity, scale=SCALE, bias=cols[:, 2:3])
                        else:
                            ins = a.activation(QT[par][:], pj[:], ACT.Copy, scale=SCALE)
                    else:
                        at_least(act, km_in[par], km_count(g - 2, par))
                        k_in = pj[:, 0:W].rearrange("p (b k) -> p b k", k=KN)
                        if bk is not None:
                            ins = a.activation(KT[par][:], k_in, ACT.Identity, bias=cols[:, 1:2])
                        else:
                            ins = a.activation(KT[par][:], k_in, ACT.Copy)
                    ins.then_inc(ready[step], 1)

                def exponentials(g, s):
                    n = g * S + s
                    act.wait_ge(sub_ready, n + 1)
                    a.activation(PR[s % 4][:], PR[s % 4][:], ACT.Exp).then_inc(exp_ready, 1)

                def turned(g, s):
                    n = g * S + s
                    act.wait_ge(tp_ready, n + 1)
                    at_least(act, pv_done, n - 3)
                    a.activation(PT[s % 4][0:KN, :], TP[s % 2][0:KN, :], ACT.Copy).then_inc(pt_ready, 1)

                def group(g, par, first, last):
                    for s in range(S):
                        if not (first and s < 2):
                            turned(g, s - 2)
                        exponentials(g, s)
                        if not last:
                            for step in steps_of:
                                if slot_of[step] == s:
                                    evict(step, g + 1, 1 - par)
                    if last:
                        turned(g, S - 2)
                        turned(g, S - 1)

                for step in steps_of:
                    evict(step, 0, 0)
                groups_loop(act, group, 3 if U == 1 else 1)

            @block.tensor
            def _(pe):
                t = nc.tensor
                pe.wait_ge(weights_in, 16 * n_weights)
                at_least(pe, prep, n_prep - 1 if mask is not None else n_prep)
                if mask is not None:
                    t.matmul(OUT[:, 0, :], R.ones_bf[:], diag[:], start=True, stop=True).then_inc(f_psum, 1)
                pe.wait_ge(prep_pool, 4 if hepos else 9)

                def project(step, g, par):
                    pj = PJ
                    n = steps_of.index(step)
                    at_least(pe, ready[steps_of[n - 1]], g + 1 if n else g)
                    if step == "ht":
                        pe.wait_ge(h_ready, g + 1)
                        for j in range(GB):
                            last = t.transpose(pj[:, j * P:(j + 1) * P], H[:, j, :], R.ident[:])
                    elif step == "q":
                        pe.wait_ge(ready["ht"], g + 1)
                        last = t.matmul(pj[:], Wq[:], HT[par][:], start=True, stop=True)
                    elif step == "k":
                        keys_there(g, par)
                        src = HT[par][:] if own_keys else CTX[par][:].rearrange("p b k -> p (b k)")
                        last = t.matmul(pj[:, 0:W], Wk[:], src, start=True, stop=True)
                    else:
                        keys_there(g, par)
                        for j in range(GB):
                            src = HT[par][:, j * P:(j + 1) * P] if own_keys else CTX[par][:, j, :]
                            last = t.matmul(pj[0:KN, j * D:(j + 1) * D], src, Wv[:], start=True, stop=True)
                    last.then_inc(psum_done[step], 1)

                def keys_there(g, par):
                    if own_keys:
                        pe.wait_ge(ready["ht"], g + 1)
                    else:
                        pe.wait_ge(ctx_in[par], ctx_count(g, par))

                def scores(g, s, par):
                    n = g * S + s
                    j, i = s // U, s % U
                    if s == 0:
                        pe.wait_ge(km_in[par], km_count(g, par))
                        pe.wait_ge(ready["q"], g + 1)
                    at_least(pe, sub_ready, n - 1)
                    masked = addm_there = mask is not None or causal is not None or pad is not None
                    last = t.matmul(SC[s % 2][:, 0:W], QT[par][:, j * P:(j + 1) * P], KM[par][:, j, i, :],
                                    start=True, stop=not masked)
                    if pad is not None:
                        b = g * GB + j
                        rows = padb[0:1, b, :].unsqueeze(1).to_broadcast([1, 4, KC])
                        last = t.matmul(SC[s % 2][:, 0:W], R.ones_bf[0:1, :], rows, start=False, stop=True)
                    elif masked:
                        last = t.matmul(SC[s % 2][:, 0:W], R.ident_bf[:],
                                        addm[:].unsqueeze(1).to_broadcast([P, 4, KN]), start=False, stop=True)
                    last.then_inc(sc_ready, 1)

                def turn(g, s):
                    n = g * S + s
                    pe.wait_ge(exp_ready, n + 1)
                    at_least(pe, pt_ready, n - 1)
                    for q in range(4):
                        last = t.transpose(TP[s % 2][0:KN, q * P:(q + 1) * P], PR[s % 4][:, q * KN:(q + 1) * KN],
                                           R.ident[:])
                    last.then_inc(tp_ready, 1)

                def values(g, s, par):
                    n = g * S + s
                    j, i = (s // U) % GB, s % U
                    if s % S == 0:
                        pe.wait_ge(ready["v"], g + s // S + 1)
                    pe.wait_ge(pt_ready, n + 1)
                    if i == 0:
                        at_least(pe, ct_ready, g * GB + s // U - 1)
                    for what in range(2):
                        for q in range(4):
                            if what == 1:
                                w = DM[0:KN, i, :]
                            elif hepos:
                                w = VM[par][0:KN, j, 32 * q:32 * q + 32]
                            else:
                                h = 4 * q + i
                                w = VM[par][0:KN, j, 32 * h:32 * h + 32]
                            last = t.matmul(ND[j % 2][32 * q:32 * q + 32, what, :], w,
                                            PT[s % 4][0:KN, q * P:(q + 1) * P],
                                            start=(what == 0 and i == 0), stop=(i == U - 1), skip_group_check=True,
                                            tile_position=(0, 32 * q))
                    last.then_inc(pv_done, 1)

                def output(g, b, bt):
                    pe.wait_ge(ct_ready, b + 1)
                    if bt == 0:
                        at_least(pe, x_added, g)
                    last = t.matmul(OUT[:, bt, :], CT[bt % 2][:], Wo[:], start=True, stop=bo is None)
                    if bo is not None:
                        last = t.matmul(OUT[:, bt, :], R.ones[0:1, :], bor[:], start=False, stop=True)
                    last.then_inc(o_done, 1)

                def behind(g, s, par, first):
                    if not (first and s < 2) and s - 2 < S:
                        turn(g, s - 2)
                    if not (first and s < 3) and s - 3 < S:
                        values(g, s - 3, par if s >= 3 else 1 - par)
                    u = s - 4
                    if not (first and u < 0) and (u + 1) % U == 0:
                        gg = g if u >= 0 else g - 1
                        output(gg, g * GB + u // U, (u // U) % GB)

                def group(g, par, first, last):
                    for s in range(S):
                        scores(g, s, par)
                        behind(g, s, par, first)
                        if not last:
                            for step in steps_of:
                                if slot_of[step] == s:
                                    project(step, g + 1, 1 - par)
                    if last:
                        for s in range(S, S + 4):
                            behind(g, s, par, False)

                for step in steps_of:
                    project(step, 0, 0)
                groups_loop(pe, group, 3 if U == 1 else 1)


def ctx_count(g, par):
    return (g + 2 - par) * 8


def km_count(g, par):
    return (g + 2 - par) * (8 * NH)


def v_broadcast(v):
    return v.rearrange("(a p) -> a p", a=1).to_broadcast([P, D])


class Experts:

    def __init__(self, nc, R, sb, sem, name, E):
        self.E = E
        self.ht = sb(name + "_htall", [P, NB * P])
        self.logits = sb(name + "_logits", [P, NB, E])
        self.gates = sb(name + "_gates", [P, NB, E])


def top_choices(nc, v, link, X, cur, scratch, rank, E, k, chosen, each=None):
    m, eq, r = scratch
    bc = lambda a: a.unsqueeze(2).to_broadcast([P, NB, E])
    for it in range(k):
        link(v.tensor_reduce(m[:], cur, AX.X, ALU.max))
        link(v.tensor_tensor(eq[:], cur, bc(m[:]), ALU.is_equal))
        link(v.tensor_tensor(eq[:], eq[:], rank[:].unsqueeze(1).to_broadcast([P, NB, E]), ALU.mult))
        link(v.tensor_reduce(r[:], eq[:], AX.X, ALU.max))
        one = each[it] if each is not None else eq[:]
        link(v.tensor_tensor(one, eq[:], bc(r[:]), ALU.is_equal))
        if it == 0:
            link(v.tensor_copy(chosen, one))
        else:
            link(v.tensor_tensor(chosen, chosen, one, ALU.add))
        if it < k - 1:
            link(v.scalar_tensor_tensor(cur, one, -3.0e38, cur, ALU.mult, ALU.add))


def routing_part(nc, R, I, name, X, kind, wr, loads, extra):
    E = X.E
    TOP = {"proto": 2, "shared": 4, "capacity": 2, "swiglu": 2}[kind]
    with ExitStack() as stack:
        sb, ps, sem = allocator(nc, stack)
        n_ = lambda s: f"{name}r_{s}"
        norm = Norm(nc, R, sb, sem, n_("n"))
        WR = sb(n_("wr"), [P, E])
        rank = sb(n_("rank"), [P, E])
        H = [sb(n_(f"h{i}"), [P, GB, D]) for i in range(2)]
        HS = [sb(n_(f"hs{i}"), [P, GT]) for i in range(2)]
        m, r = sb(n_("m"), [P, NB]), sb(n_("r"), [P, NB])
        eq = sb(n_("eq"), [P, NB, E])
        ex = sb(n_("ex"), [P, NB, E])
        dist = sb(n_("dist"), [P, NB, E])
        TR = [ps(n_(f"tr{i}"), [P, 512]) for i in range(2)]
        LG = [ps(n_(f"lg{i}"), [P, GB, E]) for i in range(2)]
        small_in, big_in = sem(n_("small_in")), sem(n_("big_in"))
        h_ready, tr_ready, hs_ready, lg_ready, l_ready = (sem(n_(s)) for s in
                                                         ("h_ready", "tr_ready", "hs_ready", "lg_ready", "l_ready"))
        ht_in, chain, act_step, pe_step = [sem(n_(f"ht_in{i}")) for i in range(2)], sem(n_("chain")), sem(n_("act_step")), sem(n_("pe_step"))
        act_go, pe_go, scans, x2_ready = (sem(n_(s)) for s in ("act_go", "pe_go", "scans", "x2_ready"))
        if kind == "proto":
            psq = sb(n_("psq"), [P, E])
            protoT2 = sb(n_("protoT2"), [P, E])
            x2 = sb(n_("x2"), [P, NB])
            junk = sb(n_("junk"), [P, 2, GB, D])
            temp = sb(n_("temp"), [P, 2])
            PQ = ps(n_("pq"), [P, E])
        if kind == "swiglu":
            lnc = sb(n_("lnc"), [P, 2])
        if kind == "capacity":
            one = [sb(n_(f"one{i}"), [P, NB, E]) for i in range(2)]
            oneb = [sb(n_(f"oneb{i}"), [P, NB, E], BF16) for i in range(2)]
            tri = sb(n_("tri"), [P, P], BF16)
            total = [sb(n_(f"total{i}"), [P, NB, E]) for i in range(2)]
            run = [sb(n_(f"run{i}"), [P, NB, E]) for i in range(2)]
            ones64 = sb(n_("ones64"), [P, NB])
            CUM = [ps(n_(f"cum{i}"), [P, NB * E]) for i in range(2)]
            TOT = [ps(n_("tot0"), [P, NB * E]), ps(n_("tot1"), [P, NB * E])]
        n_small = 2 + {"proto": 1, "shared": 0, "capacity": 1, "swiglu": 2}[kind]

        with nc.Block() as block:
            @block.sync
            def _(sp):
                sp.dma_start(WR[:], wr).then_inc(small_in, 16)
                sp.dma_start(rank[:], extra["rank"].to_broadcast([P, E])).then_inc(small_in, 16)
                if kind == "proto":
                    sp.dma_start(temp[:, 0:1], extra["temp"].to_broadcast([P, 1])).then_inc(small_in, 16)
                if kind == "swiglu":
                    for c in range(2):
                        sp.dma_start(lnc[:, c:c + 1], extra["ln"][c].rearrange("(p a) -> p a", a=1)).then_inc(small_in, 16)
                if kind == "capacity":
                    sp.dma_start(tri[:], I["tri"]).then_inc(small_in, 16)
                for t, w in loads:
                    sp.dma_start(t, w).then_inc(big_in, 16)

                def keep(g, par):
                    sp.wait_ge(hs_ready, g + 1)
                    sp.dma_start(X.ht[:, bass.ds(g * GT, GT)], HS[par][:]).then_inc(ht_in[par], 16)

                def pair(g):
                    keep(g, 0)
                    keep(g + 1, 1)

                pairs_loop(sp, NG, pair)
                for i in range(2):
                    sp.wait_ge(ht_in[i], 8 * NG)
                sp.wait_ge(big_in, 16 * len(loads))

            @block.tensor
            def _(pe):
                t = nc.tensor
                pe.wait_ge(small_in, 16 * n_small)
                if kind == "proto":
                    pe.wait_ge(chain, 1)
                    t.matmul(PQ[:], R.ones[:], protoT2[:], start=True, stop=True).then_inc(pe_step, 1)

                def turn(g, par):
                    pe.wait_ge(h_ready, g + 1)
                    at_least(pe, hs_ready, g - 1)
                    for j in range(GB):
                        last = t.transpose(TR[par][:, j * P:(j + 1) * P], H[par][:, j, :], R.ident[:])
                    last.then_inc(tr_ready, 1)

                def scores(g, par):
                    pe.wait_ge(hs_ready, g + 1)
                    at_least(pe, l_ready, g - 1)
                    for j in range(GB):
                        last = t.matmul(LG[par][:, j, :], HS[par][:, j * P:(j + 1) * P], WR[:], start=True, stop=True)
                    last.then_inc(lg_ready, 1)

                turn(0, 0)
                def pair(g):
                    turn(g + 1, 1)
                    scores(g, 0)
                    turn(g + 2, 0)
                    scores(g + 1, 1)

                pairs_loop(pe, NG - 2, pair)
                turn(NG - 1, 1)
                scores(NG - 2, 0)
                scores(NG - 1, 1)
                if kind == "capacity":
                    for i in range(2):
                        pe.wait_ge(pe_go, i + 1)
                        flat = oneb[i][:].rearrange("p b e -> p (b e)")
                        t.matmul(CUM[i][:], tri[:], flat, start=True, stop=True)
                        t.matmul(TOT[i][:], R.ones_bf[:], flat, start=True, stop=True).then_inc(pe_step, 1)

            @block.scalar
            def _(act):
                a = nc.scalar
                norm.scalar(act)
                act.wait_ge(small_in, 16 * n_small)

                def hs(g, par):
                    act.wait_ge(tr_ready, g + 1)
                    at_least(act, ht_in[par], (g - par) * 8)
                    at_least(act, lg_ready, g - 1)
                    if kind == "swiglu":
                        ins = a.activation(HS[par][:], TR[par][:], ACT.Identity, scale=lnc[:, 0:1], bias=lnc[:, 1:2])
                    else:
                        ins = a.activation(HS[par][:], TR[par][:], ACT.Copy)
                    ins.then_inc(hs_ready, 1)

                def lg(g, par):
                    act.wait_ge(lg_ready, g + 1)
                    a.activation(X.logits[:, bass.ds(g * GB, GB), :], LG[par][:], ACT.Copy).then_inc(l_ready, 1)

                hs(0, 0)
                def pair(g):
                    hs(g + 1, 1)
                    lg(g, 0)
                    hs(g + 2, 0)
                    lg(g + 1, 1)

                pairs_loop(act, NG - 2, pair)
                hs(NG - 1, 1)
                lg(NG - 2, 0)
                lg(NG - 1, 1)
                if kind == "proto":
                    act.wait_ge(act_go, 1)
                    a.activation(dist[:], dist[:], ACT.Sqrt).then_inc(act_step, 1)
                    act.wait_ge(act_go, 2)
                    a.activation(ex[:], ex[:], ACT.Exp, scale=temp[:, 1:2]).then_inc(act_step, 1)
                else:
                    act.wait_ge(act_go, 1)
                    a.activation(ex[:], ex[:], ACT.Exp).then_inc(act_step, 1)

            @block.vector
            def _(dve):
                v = nc.vector
                count = [0]

                def link(ins):
                    count[0] += 1
                    ins.then_inc(chain, 1)
                    dve.wait_ge(chain, count[0])

                norm.vector(dve)
                dve.wait_ge(small_in, 16 * n_small)
                if kind == "proto":
                    link(v.tensor_tensor(protoT2[:], WR[:], WR[:], ALU.mult))
                    dve.wait_ge(pe_step, 1)
                    link(v.tensor_copy(psq[:], PQ[:]))
                    link(v.tensor_scalar(temp[:, 1:2], temp[:, 0:1], -1.0, None, ALU.mult))
                    link(v.tensor_tensor(temp[:, 0:1], temp[:, 0:1], temp[:, 1:2], ALU.max))
                    link(v.tensor_scalar(temp[:, 0:1], temp[:, 0:1], 0.1, None, ALU.max))
                    link(v.reciprocal(temp[:, 1:2], temp[:, 0:1]))
                    link(v.tensor_scalar(temp[:, 1:2], temp[:, 1:2], -1.0, None, ALU.mult))

                def ln_group(g, par):
                    at_least(dve, tr_ready, g - 1)
                    norm.apply(dve, g, H[par]).then_inc(h_ready, 1)
                    if kind == "proto":
                        dve.wait_ge(h_ready, g + 1)
                        at_least(dve, x2_ready, (g - 1) * GB)
                        for j in range(GB):
                            b = g * GB + j
                            v.scalar_tensor_tensor(junk[:, par, j, :], H[par][:, j, :], 1.0, H[par][:, j, :], ALU.mult, ALU.mult,
                                                   accum_out=x2[:, bass.ds(b, 1)]).then_inc(x2_ready, 1)

                def pair(g):
                    ln_group(g, 0)
                    ln_group(g + 1, 1)

                pairs_loop(dve, NG, pair)
                dve.wait_ge(l_ready, NG)
                bc = lambda a: a.unsqueeze(2).to_broadcast([P, NB, E])
                L = X.logits
                scratch = (m, eq, r)
                if kind == "proto":
                    dve.wait_ge(x2_ready, NB)
                    link(v.tensor_copy(eq[:], psq[:].unsqueeze(1).to_broadcast([P, NB, E])))
                    link(v.tensor_tensor(eq[:], eq[:], bc(x2[:]), ALU.add))
                    link(v.scalar_tensor_tensor(L[:], L[:], -2.0, eq[:], ALU.mult, ALU.add))
                    v.tensor_scalar(dist[:], L[:], 0.0, None, ALU.max).then_inc(chain, 1)
                    count[0] += 1
                    link(v.tensor_scalar(eq[:], L[:], 0.0, -1.0, ALU.max, ALU.mult))
                    v.tensor_copy(L[:], eq[:]).then_inc(act_go, 1)
                    dve.wait_ge(act_go, 1)
                    top_choices(nc, v, link, X, L[:], scratch, rank, E, TOP, X.gates[:])
                    dve.wait_ge(act_step, 1)
                    link(v.tensor_reduce(m[:], dist[:], AX.X, ALU.min))
                    v.tensor_tensor(ex[:], dist[:], bc(m[:]), ALU.subtract).then_inc(act_go, 1)
                    dve.wait_ge(act_step, 2)
                else:
                    link(v.tensor_reduce(m[:], L[:], AX.X, ALU.max))
                    v.tensor_tensor(ex[:], L[:], bc(m[:]), ALU.subtract).then_inc(act_go, 1)
                    dve.wait_ge(act_go, 1)
                    top_choices(nc, v, link, X, L[:], scratch, rank, E, TOP, X.gates[:],
                                [o[:] for o in one] if kind == "capacity" else None)
                    dve.wait_ge(act_step, 1)
                G = X.gates[:]
                if kind == "shared":
                    link(v.tensor_reduce(m[:], ex[:], AX.X, ALU.add))
                    link(v.tensor_tensor(G, G, ex[:], ALU.mult))
                else:
                    link(v.tensor_tensor(G, G, ex[:], ALU.mult))
                    link(v.tensor_reduce(m[:], G, AX.X, ALU.add))
                link(v.reciprocal(r[:], m[:]))
                link(v.tensor_tensor(G, G, bc(r[:]), ALU.mult))
                if kind == "capacity":
                    link(v.memset(ones64[:], 1.0))
                    for i in range(2):
                        v.tensor_copy(oneb[i][:], one[i][:]).then_inc(pe_go, 1)
                    for i in range(2):
                        dve.wait_ge(pe_step, i + 1)
                        link(v.tensor_copy(total[i][:], TOT[i][:].rearrange("p (b e) -> p b e", e=E)))
                        for e in range(E):
                            ins = v.tensor_tensor_scan(run[i][:, :, e], ones64[:], total[i][:, :, e], 0.0, ALU.mult,
                                                       ALU.add)
                            if e == E - 1:
                                link(ins)
                            else:
                                ins.then_inc(scans, 1)
                        dve.wait_ge(scans, (E - 1) * (i + 1))
                        link(v.tensor_tensor(total[i][:], run[i][:], total[i][:], ALU.subtract))
                        link(v.tensor_tensor(total[i][:], CUM[i][:].rearrange("p (b e) -> p b e", e=E), total[i][:],
                                             ALU.add))
                        if i == 1:
                            link(v.tensor_tensor(total[1][:], total[1][:],
                                                 run[0][:, NB - 1, :].unsqueeze(1).to_broadcast([P, NB, E]), ALU.add))
                        link(v.scalar_tensor_tensor(one[i][:], total[i][:], float(extra["cap"]) + 0.5, one[i][:],
                                                    ALU.is_lt, ALU.mult))
                    link(v.tensor_tensor(one[0][:], one[0][:], one[1][:], ALU.add))
                    link(v.tensor_tensor(G, G, one[0][:], ALU.mult))


def gated_rows_phase(nc, R, I, name, kind):
    E = 32 if kind == "proto" else 16
    BL = 4 if kind == "proto" else 9
    UNG = 0 if kind == "proto" else 1
    AR = 4 if kind == "proto" else 3
    TERMS = 96 // E
    K3 = TERMS * E
    with ExitStack() as stack:
        sb, ps, sem = allocator(nc, stack)
        n_ = lambda s: f"{name}_{s}"
        X = Experts(nc, R, sb, sem, name, E)
        UP = sb(n_("up"), [P, BL * P])
        DN = sb(n_("dn"), [P, BL, D])
        SEL = sb(n_("sel"), [K3, BL - UNG, P], BF16)
        loads = [(UP[:], I[n_("up")]), (DN[:], I[n_("down")]), (SEL[:], I[n_("sel")])]
        if kind == "proto":
            BI = sb(n_("bias"), [E, D])
            loads.append((BI[:], I[n_("bias")]))
        extra = {"rank": I[f"rank{E}"], "temp": I["temp"] if kind == "proto" else None}
        routing_part(nc, R, I, name, X, kind, I[n_("router")], loads, extra)

        g3 = sb(n_("g3"), [P, NB, TERMS, E], BF16)
        rest = sb(n_("rest"), [P, NB, E])
        GS = [sb(n_(f"gs{i}"), [P, GB, K3], BF16) for i in range(2)]
        G3T = [sb(n_(f"g3t{i}"), [K3, GT], BF16) for i in range(2)]
        if kind == "proto":
            GF = [sb(n_(f"gf{i}"), [P, GB, E]) for i in range(2)]
            GFT = [sb(n_(f"gft{i}"), [E, GT]) for i in range(2)]
        A = [sb(n_(f"a{i}"), [P, GT]) for i in range(2)]
        AG = [sb(n_(f"ag{i}"), [P, GT]) for i in range(AR)]
        PU = [ps(n_(f"pu{i}"), [P, 512]) for i in range(2)]
        PG = [ps(n_(f"pg{i}"), [P, 512]) for i in range(2)]
        PO = [ps(n_(f"po{i}"), [P, GB, D]) for i in range(2)]
        PT3 = ps(n_("pt3"), [K3, GT], BF16)
        PTF = ps(n_("ptf"), [E, GT]) if kind == "proto" else None
        names = ("split", "gs_ready", "gt_psum", "gt_ready", "up_ready", "ge_ready", "a_ready", "ag_ready", "ag0_ready",
                 "dn_ready", "x_added", "zeroed")
        Z = {s: sem(n_(s)) for s in names}
        func = ACT.Copy if kind == "proto" else ACT.Gelu
        GBL = BL - UNG

        with nc.Block() as block:
            @block.gpsimd
            def _(pool):
                pool.wait_ge(Z["split"], 5)
                if TERMS > 3:
                    pool.wait_ge(Z["zeroed"], 1)

                def stage(g, par):
                    at_least(pool, Z["gt_psum"], g - 1)
                    src = g3[:, bass.ds(g * GB, GB), :, :].rearrange("p b t e -> p b (t e)")
                    ins = nc.gpsimd.tensor_copy(GS[par][:], src)
                    if kind == "proto":
                        ins.then_inc(Z["gs_ready"], 1)
                        ins = nc.gpsimd.tensor_copy(GF[par][:], X.gates[:, bass.ds(g * GB, GB), :])
                    ins.then_inc(Z["gs_ready"], 1)

                def pair(g):
                    stage(g, 0)
                    stage(g + 1, 1)

                pairs_loop(pool, NG, pair)

            @block.vector
            def _(dve):
                v = nc.vector
                if TERMS > 3:
                    v.memset(g3[:, :, 3:TERMS, :], 0.0).then_inc(Z["zeroed"], 1)
                v.tensor_copy(g3[:, :, 0, :], X.gates[:]).then_inc(Z["split"], 1)
                dve.wait_ge(Z["split"], 1)
                v.tensor_tensor(rest[:], X.gates[:], g3[:, :, 0, :], ALU.subtract).then_inc(Z["split"], 1)
                dve.wait_ge(Z["split"], 2)
                v.tensor_copy(g3[:, :, 1, :], rest[:]).then_inc(Z["split"], 1)
                dve.wait_ge(Z["split"], 3)
                v.tensor_tensor(rest[:], rest[:], g3[:, :, 1, :], ALU.subtract).then_inc(Z["split"], 1)
                dve.wait_ge(Z["split"], 4)
                v.tensor_copy(g3[:, :, 2, :], rest[:]).then_inc(Z["split"], 1)

                def gate(g, c, par):
                    if c < UNG:
                        return
                    n = g * BL + c
                    gn = g * GBL + c - UNG
                    q = par * BL + c
                    dve.wait_ge(Z["a_ready"], gn + 1)
                    dve.wait_ge(Z["ge_ready"], gn + 1)
                    at_least(dve, Z["dn_ready"], n - AR + 1)
                    v.tensor_tensor(AG[q % AR][:], A[(par * GBL + c - UNG) % 2][:], PG[(par * GBL + c - UNG) % 2][:],
                                    ALU.mult).then_inc(Z["ag_ready"], 1)

                def group(g, par, first, last):
                    for c in range(BL):
                        gate(g, c, par)
                        if c == 2 and not first:
                            add(g - 1, 1 - par)
                    if last:
                        add(g, par)

                def add(g, par):
                    dve.wait_ge(Z["dn_ready"], g * BL + BL)
                    residual(nc, R, dve, Z["x_added"], g, PO[par][:], g + 1)

                groups_loop(dve, group, 3)

            @block.scalar
            def _(act):
                a = nc.scalar

                def gates_in(g, par):
                    act.wait_ge(Z["gt_psum"], g + 1)
                    ins = a.activation(G3T[par][:], PT3[:], ACT.Copy)
                    if kind == "proto":
                        ins.then_inc(Z["gt_ready"], 1)
                        ins = a.activation(GFT[par][:], PTF[:], ACT.Copy)
                    ins.then_inc(Z["gt_ready"], 1)

                def rows(g, c, par):
                    n = g * BL + c
                    q = par * BL + c
                    act.wait_ge(Z["up_ready"], n + 1)
                    if c < UNG:
                        at_least(act, Z["dn_ready"], n - AR + 1)
                        a.activation(AG[q % AR][:], PU[q % 2][:], func).then_inc(Z["ag0_ready"], 1)
                    else:
                        gn = g * GBL + c - UNG
                        at_least(act, Z["ag_ready"], gn - 1)
                        a.activation(A[(par * GBL + c - UNG) % 2][:], PU[q % 2][:], func).then_inc(Z["a_ready"], 1)

                def group(g, par, first, last):
                    for c in range(BL):
                        rows(g, c, par)
                        if c == 1 and not last:
                            gates_in(g + 1, 1 - par)

                gates_in(0, 0)
                groups_loop(act, group, 3)

            @block.tensor
            def _(pe):
                t = nc.tensor

                def gates_turn(g, par):
                    many = 2 if kind == "proto" else 1
                    pe.wait_ge(Z["gs_ready"], (g + 1) * many)
                    at_least(pe, Z["gt_ready"], g * many)
                    for j in range(GB):
                        last = t.transpose(PT3[:, j * P:(j + 1) * P], GS[par][:, j, :], R.ident_bf[:])
                    if kind == "proto":
                        for j in range(GB):
                            last = t.transpose(PTF[:, j * P:(j + 1) * P], GF[par][:, j, :], R.ident[:])
                    last.then_inc(Z["gt_psum"], 1)

                def up(g, c, par):
                    n = g * BL + c
                    q = par * BL + c
                    if UNG:
                        if c == 0:
                            at_least(pe, Z["a_ready"], g * GBL - 1)
                        elif c == 1:
                            at_least(pe, Z["a_ready"], g * GBL)
                        elif c == 2:
                            pe.wait_ge(Z["ag0_ready"], g + 1)
                        else:
                            at_least(pe, Z["a_ready"], g * GBL + c - 2)
                    else:
                        at_least(pe, Z["a_ready"], n - 1)
                    t.matmul(PU[q % 2][:], UP[:, c * P:(c + 1) * P], X.ht[:, bass.ds(g * GT, GT)], start=True,
                             stop=True).then_inc(Z["up_ready"], 1)
                    if c >= UNG:
                        gn = g * GBL + c - UNG
                        if c == UNG:
                            pe.wait_ge(Z["gt_ready"], (g + 1) * (2 if kind == "proto" else 1))
                        at_least(pe, Z["ag_ready"], gn - 1)
                        t.matmul(PG[(par * GBL + c - UNG) % 2][:], SEL[:, c - UNG, :], G3T[par][:], start=True,
                                 stop=True).then_inc(Z["ge_ready"], 1)

                def down(g, c, par):
                    q = par * BL + c
                    if c == 0:
                        at_least(pe, Z["x_added"], g - 1)
                    if c < UNG:
                        pe.wait_ge(Z["ag0_ready"], g + 1)
                    else:
                        pe.wait_ge(Z["ag_ready"], g * GBL + c - UNG + 1)
                    if c == 0 and kind == "proto":
                        for j in range(GB):
                            t.matmul(PO[par][:, j, :], GFT[par][:, j * P:(j + 1) * P], BI[:], start=(j == 0), stop=False,
                                     skip_group_check=True)
                    for j in range(GB):
                        last = t.matmul(PO[par][:, j, :], AG[q % AR][:, j * P:(j + 1) * P], DN[:, c, :],
                                        start=(c == 0 and j == 0 and kind != "proto"), stop=(c == BL - 1),
                                        skip_group_check=True)
                    last.then_inc(Z["dn_ready"], 1)

                def group(g, par, first, last):
                    for c in range(BL):
                        up(g, c, par)
                        if c >= 2:
                            down(g, c - 2, par)
                        elif not first:
                            down(g - 1, BL - 2 + c, 1 - par)
                        if c == 0 and not last:
                            gates_turn(g + 1, 1 - par)
                    if last:
                        down(g, BL - 2, par)
                        down(g, BL - 1, par)

                gates_turn(0, 0)
                groups_loop(pe, group, 3)


def gated_outputs_phase(nc, R, I, name, kind):
    E = 8
    HB = 4 if kind == "capacity" else 2
    N = E * HB
    two = kind == "swiglu"
    with ExitStack() as stack:
        sb, ps, sem = allocator(nc, stack)
        n_ = lambda s: f"{name}_{s}"
        X = Experts(nc, R, sb, sem, name, E)
        W1 = sb(n_("w1"), [P, N * P])
        W2 = sb(n_("w2"), [P, N * P]) if two else None
        WD = sb(n_("wd"), [P, N, D])
        loads = [(W1[:], I[n_("w1")]), (WD[:], I[n_("wd")])]
        if two:
            loads.append((W2[:], I[n_("w2")]))
        else:
            B1, B2 = sb(n_("b1"), [P, N]), sb(n_("b2"), [E, D])
            loads += [(B1[:], I[n_("b1")]), (B2[:], I[n_("b2")])]
        extra = {"rank": I["rank8"], "cap": 2 * NB * P // E, "ln": (I["ln2_scale"], I["ln2_shift"]) if two else None}
        routing_part(nc, R, I, name, X, kind, I[n_("router")], loads, extra)

        A = [sb(n_(f"a{i}"), [P, GT]) for i in range(4)]
        S = [sb(n_(f"s{i}"), [P, GT]) for i in range(2)] if two else None
        PU = [ps(n_(f"pu{i}"), [P, 512]) for i in range(2)]
        PV = [ps(n_(f"pv{i}"), [P, 512]) for i in range(2)] if two else None
        PY = [ps(n_(f"py{i}"), [P, GB, D]) for i in range(2)]
        if not two:
            GF = [sb(n_(f"gf{i}"), [P, GB, E]) for i in range(2)]
            GFT = [sb(n_(f"gft{i}"), [E, GT]) for i in range(2)]
            PTF = ps(n_("ptf"), [E, GT])
            PB = ps(n_("pb"), [P, GB, D])
        Z = {s: sem(n_(s)) for s in ("gs_ready", "gt_psum", "gt_ready", "up_ready", "s_ready", "a_ready", "dn_ready",
                                     "y_used", "b_ready", "x_added")}

        with nc.Block() as block:
            if not two:
                @block.gpsimd
                def _(pool):
                    def stage(g, par):
                        at_least(pool, Z["gt_psum"], g - 1)
                        nc.gpsimd.tensor_copy(GF[par][:], X.gates[:, bass.ds(g * GB, GB), :]).then_inc(Z["gs_ready"], 1)

                    def pair(g):
                        stage(g, 0)
                        stage(g + 1, 1)

                    pairs_loop(pool, NG, pair)

            @block.vector
            def _(dve):
                v = nc.vector

                def product(g, s):
                    n = g * N + s
                    dve.wait_ge(Z["s_ready"], n + 1)
                    dve.wait_ge(Z["up_ready"], n + 1)
                    at_least(dve, Z["dn_ready"], n - 3)
                    v.tensor_tensor(A[s % 4][:], S[s % 2][:], PV[s % 2][:], ALU.mult).then_inc(Z["a_ready"], 1)

                def weigh(g, e):
                    dve.wait_ge(Z["dn_ready"], (g * E + e + 1) * HB)
                    at_least(dve, Z["y_used"], (g * E + e) * GB)
                    for j in range(GB):
                        b = g * GB + j
                        xb = R.x[:, b, :]
                        v.scalar_tensor_tensor(xb, PY[e % 2][:, j, :], X.gates[:, b, bass.ds(e, 1)], xb, ALU.mult,
                                               ALU.add).then_inc(Z["y_used"], 1)

                def finish(g):
                    dve.wait_ge(Z["y_used"], (g + 1) * E * GB)
                    if two:
                        for j in range(GB):
                            b = g * GB + j
                            v.bn_stats(R.stats[:, b, :], R.x[:, b, :]).then_inc(R.stats_done, 1)
                    else:
                        dve.wait_ge(Z["b_ready"], g + 1)
                        residual(nc, R, dve, Z["x_added"], g, PB[:], g + 1)

                def group(g, par, first, last):
                    for s in range(N):
                        if two:
                            product(g, s)
                        if s >= 2 and (s - 1) % HB == 0:
                            weigh(g, (s - 1) // HB - 1)
                        if s == 1 and not first:
                            weigh(g - 1, E - 1)
                            finish(g - 1)
                    if last:
                        weigh(g, E - 1)
                        finish(g)

                groups_loop(dve, group)

            @block.scalar
            def _(act):
                a = nc.scalar

                def rows(g, s):
                    n = g * N + s
                    act.wait_ge(Z["up_ready"], n + 1)
                    if two:
                        at_least(act, Z["a_ready"], n - 1)
                        a.activation(S[s % 2][:], PU[s % 2][:], ACT.Silu).then_inc(Z["s_ready"], 1)
                    else:
                        at_least(act, Z["dn_ready"], n - 3)
                        a.activation(A[s % 4][:], PU[s % 2][:], ACT.Gelu, bias=B1[:, s:s + 1]).then_inc(Z["a_ready"], 1)

                def gates_in(g, par):
                    act.wait_ge(Z["gt_psum"], g + 1)
                    a.activation(GFT[par][:], PTF[:], ACT.Copy).then_inc(Z["gt_ready"], 1)

                def group(g, par, first, last):
                    for s in range(N):
                        rows(g, s)
                        if s == 4 and not two:
                            gates_in(g, par)

                groups_loop(act, group)

            @block.tensor
            def _(pe):
                t = nc.tensor

                def up(g, s):
                    n = g * N + s
                    at_least(pe, Z["a_ready"], n - 1)
                    rhs = X.ht[:, bass.ds(g * GT, GT)]
                    last = t.matmul(PU[s % 2][:], W1[:, s * P:(s + 1) * P], rhs, start=True, stop=True)
                    if two:
                        last = t.matmul(PV[s % 2][:], W2[:, s * P:(s + 1) * P], rhs, start=True, stop=True)
                    last.then_inc(Z["up_ready"], 1)

                def down(g, s):
                    n = g * N + s
                    e, c = s // HB, s % HB
                    pe.wait_ge(Z["a_ready"], n + 1)
                    if c == 0:
                        at_least(pe, Z["y_used"], (g * E + e - 1) * GB)
                    for j in range(GB):
                        last = t.matmul(PY[e % 2][:, j, :], A[s % 4][:, j * P:(j + 1) * P], WD[:, s, :],
                                        start=(c == 0 and j == 0), stop=(c == HB - 1), skip_group_check=True)
                    last.then_inc(Z["dn_ready"], 1)

                def biases(g, par):
                    pe.wait_ge(Z["gt_ready"], g + 1)
                    at_least(pe, Z["x_added"], g)
                    for j in range(GB):
                        last = t.matmul(PB[:, j, :], GFT[par][:, j * P:(j + 1) * P], B2[:], start=True, stop=True)
                    last.then_inc(Z["b_ready"], 1)

                def gates_turn(g, par):
                    pe.wait_ge(Z["gs_ready"], g + 1)
                    at_least(pe, Z["gt_ready"], g)
                    for j in range(GB):
                        last = t.transpose(PTF[:, j * P:(j + 1) * P], GF[par][:, j, :], R.ident[:])
                    last.then_inc(Z["gt_psum"], 1)

                def group(g, par, first, last):
                    for s in range(N):
                        up(g, s)
                        if s >= 2:
                            down(g, s - 2)
                        elif not first:
                            down(g - 1, N - 2 + s)
                        if not two and s == 3:
                            gates_turn(g, par)
                        if not two and s == 7:
                            biases(g, par)
                    if last:
                        down(g, N - 2)
                        down(g, N - 1)

                groups_loop(pe, group)


def store_phase(nc, R, I, out):
    with ExitStack() as stack:
        sb, ps, sem = allocator(nc, stack)
        stored, summed = sem("stored"), sem("summed")
        view = out.rearrange("b t d -> t b d")
        parts = [slice(i * NB // 8, (i + 1) * NB // 8) for i in range(8)]
        with nc.Block() as block:
            @block.vector
            def _(dve):
                for q in parts:
                    if R.kept is not None:
                        nc.vector.tensor_tensor(R.x[:, q, :], R.x[:, q, :], R.kept[:, q, :], ALU.add).then_inc(summed, 1)

            @block.sync
            def _(sp):
                for i, q in enumerate(parts):
                    if R.kept is not None:
                        sp.wait_ge(summed, i + 1)
                    sp.dma_start(view[:, q, :], R.x[:, q, :]).then_inc(stored, 16)
                sp.wait_ge(stored, 16 * len(parts))


def build(nc, I, out, only=None):
    with ExitStack() as stack:
        sb, ps, sem = allocator(nc, stack)
        R = Namespace()
        R.x = sb("x", [P, NB, D])
        R.stats = sb("stats", [P, NB, 6])
        R.ident = sb("ident", [P, P])
        R.ident_bf = sb("ident_bf", [P, P], BF16)
        R.ones = sb("ones", [P, P])
        R.ones_bf = sb("ones_bf", [P, P], BF16)
        R.stats_done = sem("stats_done")
        R.kept = None
        load_phase(nc, R, I)
        phases = [
            lambda: attention_phase(nc, R, I, "a0", I["L0_xattn_Wq"], I["L0_xattn_Wk"], I["L0_xattn_Wv"], I["L0_xattn_Wo"],
                                    I["L0_xattn_bq"], I["L0_xattn_bk"], I["L0_xattn_bv"], I["L0_xattn_bo"], hepos=True, pad=I["pad"]),
            lambda: gated_rows_phase(nc, R, I, "f0", "proto"),
            lambda: attention_phase(nc, R, I, "a1", I["L1_xattn_wq"], I["L1_xattn_wk"], I["L1_xattn_wv"], I["L1_xattn_wo"],
                                    I["L1_xattn_bq"], I["L1_xattn_bk"], I["L1_xattn_bv"], I["L1_xattn_bo"]),
            lambda: gated_rows_phase(nc, R, I, "f1", "shared"),
            lambda: attention_phase(nc, R, I, "a2", I["L2_xattn_W_q"], I["L2_xattn_W_k"], I["L2_xattn_W_v"], I["L2_xattn_W_o"],
                                    I["L2_xattn_b_q"], I["L2_xattn_b_k"], I["L2_xattn_b_v"], I["L2_xattn_b_o"], mask=I["mask"]),
            lambda: gated_outputs_phase(nc, R, I, "f2", "capacity"),
            lambda: attention_phase(nc, R, I, "a3", I["L3_xattn_Wq"], I["L3_xattn_Wk"], I["L3_xattn_Wv"], I["L3_xattn_Wo"],
                                    causal=I["causal_ctx"]),
            lambda: renorm_phase(nc, R, sb("y", [P, NB, D])),
            lambda: attention_phase(nc, R, I, "s3", I["L3_ffn_wq"], I["L3_ffn_wk"], I["L3_ffn_wv"], I["L3_ffn_wo"],
                                    bo=I["L3_ffn_bo"], own_keys=True, causal=I["causal_own"],
                                    ln=(I["L3_ffn_ln1_scale"], I["L3_ffn_ln1_shift"])),
            lambda: gated_outputs_phase(nc, R, I, "f3", "swiglu"),
        ]
        chosen = range(len(phases)) if only is None else only
        for i in chosen:
            phases[i]()
        store_phase(nc, R, I, out)


def laid_out(inputs):
    a = {k: np.asarray(v) for k, v in inputs.items()}
    c = np.ascontiguousarray
    order = np.arange(KC).reshape(KCLS, STRIDE).T.reshape(-1)
    r = {
        "x": c(a["x"].transpose(1, 0, 2)),
        "ctxT": c(a["ctx_1024"][:, order, :].transpose(2, 0, 1)),
        "pad": c(a["mask_BxS2_bf0"][:, order].reshape(1, -1)),
        "mask": c(a["mask_1x1xSxS2_ik0"][0, 0][:, order]),
        "temp": a["L0_ffn_temp"].reshape(1, 1),
        "ln2_scale": a["L3_ffn_ln2_scale"], "ln2_shift": a["L3_ffn_ln2_shift"],
    }
    for n in ("Wq", "bq", "Wk", "bk", "Wv", "bv", "Wo", "bo"):
        r[f"L0_xattn_{n}"] = a[f"L0_xattn_{n}"]
        if n[0] == "W":
            r[f"L3_xattn_{n}"] = c(a[f"L3_xattn_{n}"].T)
    for n in ("q", "k", "v", "o"):
        r[f"L1_xattn_w{n}"] = c(a[f"L1_xattn_w{n}"].T)
        r[f"L1_xattn_b{n}"] = a[f"L1_xattn_b{n}"]
        r[f"L2_xattn_W_{n}"] = a[f"L2_xattn_W_{n}"]
        r[f"L2_xattn_b_{n}"] = a[f"L2_xattn_b_{n}"]
        r[f"L3_ffn_w{n}"] = a[f"L3_ffn_w{n}"]
    for n in ("bo", "ln1_scale", "ln1_shift"):
        r[f"L3_ffn_{n}"] = a[f"L3_ffn_{n}"]

    def blocks(w):
        return c(w.reshape(-1, P, D).transpose(1, 0, 2))

    r["f0_router"] = c(a["L0_ffn_prototypes"].T)
    r["f0_up"] = c(a["L0_ffn_B"].reshape(-1, D).T)
    r["f0_down"] = blocks(a["L0_ffn_A"].transpose(0, 2, 1).reshape(-1, D))
    r["f0_bias"] = a["L0_ffn_bias"]
    r["f1_router"] = c(a["L1_ffn_router_w"].T)
    up = np.concatenate([a["L1_ffn_shared_up"], a["L1_ffn_routed_up"]])
    down = np.concatenate([a["L1_ffn_shared_down"], a["L1_ffn_routed_down"]])
    r["f1_up"] = c(up.reshape(-1, D).T)
    r["f1_down"] = blocks(down.transpose(0, 2, 1).reshape(-1, D))
    r["f2_router"] = a["L2_ffn_wg"]
    r["f2_w1"] = c(a["L2_ffn_w1"].transpose(1, 0, 2).reshape(D, -1))
    r["f2_wd"] = blocks(a["L2_ffn_w2"].reshape(-1, D))
    r["f2_b1"] = c(a["L2_ffn_b1"].reshape(-1, P).T)
    r["f2_b2"] = a["L2_ffn_b2"]
    r["f3_router"] = a["L3_ffn_gate_w"]
    for n in ("w1", "w2"):
        r[f"f3_{n}"] = c(a[f"L3_ffn_{n}"].transpose(1, 0, 2).reshape(D, -1))
    r["f3_wd"] = blocks(a["L3_ffn_w3"].reshape(-1, D))

    bf = mybir.dt.np(BF16)
    place = np.arange(P)
    r["ident"] = np.eye(P, dtype=np.float32)
    r["ident_bf"] = np.eye(P).astype(bf)
    r["tri"] = (place[:, None] <= place[None, :]).astype(bf)
    r["classes"] = (np.arange(KC)[:, None] // KCLS == np.arange(32)[None, :] // HD).astype(np.float32)
    r["causal_ctx"] = np.where(order[None, :] > place[:, None], FAR, 0).astype(bf)
    r["causal_own"] = np.where(place[None, :] > place[:, None], FAR, 0).astype(bf)
    for e in (8, 16, 32):
        r[f"rank{e}"] = (e - np.arange(e, dtype=np.float32)).reshape(1, e)
    for n, e, blocks_, rows in (("f0", 32, 4, 16), ("f1", 16, 8, 64)):
        owner = np.arange(blocks_ * P).reshape(blocks_, P) // rows
        term = np.tile(np.arange(e), 3)
        term = np.concatenate([term, np.full(96 - 3 * e, -1)])
        r[f"{n}_sel"] = (term[:, None, None] == owner[None]).astype(bf)
    return r


def kernel(**inputs):
    import concourse.bacc as bacc
    from concourse.bass_utils import run_bass_kernel_spmd

    nc = bacc.Bacc("TRN2", target_bir_lowering=False, num_devices=1)
    arrays, I = {}, {}
    for name, a in laid_out(inputs).items():
        arrays["in_" + name] = a
        I[name] = nc.dram_tensor("in_" + name, a.shape, mybir.dt.from_np(a.dtype), kind="ExternalInput").ap()
    out = nc.dram_tensor("out_x", (NB, P, D), F32, kind="ExternalOutput").ap()
    build(nc, I, out)
    result = run_bass_kernel_spmd(nc, [arrays], core_ids=[0])
    return result.results[0]["out_x"]
```

```python
from contextlib import ExitStack

import concourse.bass as bass
import numpy as np
from concourse import mybir

F32 = mybir.dt.float32
BF16 = mybir.dt.bfloat16
F32R = mybir.dt.float32r
U8 = mybir.dt.uint8
I32 = mybir.dt.int32
ALU = mybir.AluOpType
ACT = mybir.ActivationFunctionType
AX = mybir.AxisListType

P = 128
D = 128
NB = 64
GB = 4
NG = NB // GB
GT = GB * P
NH = 16
HD = D // NH
KC = 120
STRIDE = 4
KCLS = KC // STRIDE
PARTS = 8
EPS = 1e-5
SCALE = float(HD) ** -0.5
FAR = -1.0e30


def at_least(eng, sem, value):
    if isinstance(value, int) and value <= 0:
        return
    eng.wait_ge(sem, value)


class Namespace:
    pass


def allocator(nc, stack):
    numbers = []

    def zero_semaphores():
        numbers.sort()
        runs = []
        for n in numbers:
            if runs and runs[-1].stop == n:
                runs[-1] = range(runs[-1].start, n + 1)
            else:
                runs.append(range(n, n + 1))
        for run in runs:
            nc.gpsimd.sem_clear(run)
        nc.all_engine_barrier()

    stack.callback(zero_semaphores)

    def sb(name, shape, dt=F32):
        return stack.enter_context(nc.sbuf_tensor(name, shape, dt))

    def ps(name, shape, dt=F32):
        return stack.enter_context(nc.psum_tensor(name, shape, dt))

    def sem(name):
        handle = stack.enter_context(nc.semaphore(name))
        numbers.append(handle.num)
        return handle

    return sb, ps, sem


def groups_loop(eng, body, peel=1):
    for g in range(peel):
        body(g, g % 2, g == 0, False)
    with eng.Fori(peel, NG - 2, 2) as g:
        body(g, 1, False, False)
        body(g + 1, 0, False, False)
    body(NG - 1, 1, False, True)


def pairs_loop(eng, end, body):
    body(0)
    with eng.Fori(2, end - 1, 2) as g:
        body(g)


class Norm:

    def __init__(self, nc, R, sb, sem, name):
        self.nc, self.R = nc, R
        self.mean = sb(name + "_mean", [P, NB])
        self.rstd = sb(name + "_rstd", [P, NB])
        self.work = sb(name + "_work", [P, 4, NB])
        self.steps = sem(name + "_norm_steps")
        self.var_ready = sem(name + "_var_ready")
        self.std_ready = sem(name + "_std_ready")

    def vector(self, dve):
        s = self.R.stats
        w = self.work
        v = self.nc.vector
        v.tensor_tensor(w[:, 0, :], s[:, :, 1], s[:, :, 4], ALU.add).then_inc(self.steps, 1)
        v.tensor_tensor(w[:, 1, :], s[:, :, 1], s[:, :, 4], ALU.subtract).then_inc(self.steps, 1)
        v.tensor_tensor(w[:, 2, :], s[:, :, 2], s[:, :, 5], ALU.add).then_inc(self.steps, 1)
        dve.wait_ge(self.steps, 3)
        v.tensor_scalar(self.mean[:], w[:, 0, :], 0.5, None, ALU.mult).then_inc(self.steps, 1)
        v.tensor_tensor(w[:, 3, :], w[:, 1, :], w[:, 1, :], ALU.mult).then_inc(self.steps, 1)
        dve.wait_ge(self.steps, 5)
        v.scalar_tensor_tensor(w[:, 0, :], w[:, 3, :], D / 4.0, w[:, 2, :], ALU.mult, ALU.add).then_inc(self.steps, 1)
        dve.wait_ge(self.steps, 6)
        v.tensor_scalar(w[:, 1, :], w[:, 0, :], 1.0 / D, EPS, ALU.mult, ALU.add).then_inc(self.var_ready, 1)
        dve.wait_ge(self.std_ready, 1)
        v.reciprocal(self.rstd[:], w[:, 2, :]).then_inc(self.steps, 1)
        dve.wait_ge(self.steps, 7)

    def scalar(self, act):
        act.wait_ge(self.var_ready, 1)
        self.nc.scalar.activation(self.work[:, 2, :], self.work[:, 1, :], ACT.Sqrt).then_inc(self.std_ready, 1)

    def apply(self, dve, g, h):
        for j in range(GB):
            b = g * GB + j
            last = self.nc.vector.tensor_scalar(h[:, j, :], self.R.x[:, b, :],
                                                self.mean[:, bass.ds(b, 1)], self.rstd[:, bass.ds(b, 1)],
                                                ALU.subtract, ALU.mult)
        return last

    def apply_one(self, dve, g, j, h):
        b = g * GB + j
        return self.nc.vector.tensor_scalar(h[:, j, :], self.R.x[:, b, :], self.mean[:, bass.ds(b, 1)],
                                            self.rstd[:, bass.ds(b, 1)], ALU.subtract, ALU.mult)


def residual(nc, R, dve, sem, g, out, done):
    xg = R.x[:, bass.ds(g * GB, GB), :]
    nc.vector.tensor_tensor(xg, xg, out, ALU.add).then_inc(sem, 1)
    dve.wait_ge(sem, done)
    for j in range(GB):
        b = g * GB + j
        nc.vector.bn_stats(R.stats[:, b, :], R.x[:, b, :]).then_inc(R.stats_done, 1)


def load_phase(nc, R, I):
    with ExitStack() as stack:
        sb, ps, sem = allocator(nc, stack)
        x_in = [sem(f"load_x{i}") for i in range(4)]
        const_in = sem("load_const")
        with nc.Block() as block:
            @block.sync
            def _(sp):
                for i in range(4):
                    q = slice(i * NB // 4, (i + 1) * NB // 4)
                    sp.dma_start(R.x[:, q, :], I["x"][:, q, :]).then_inc(x_in[i], 16)
                sp.dma_start(R.ident[:], I["ident"]).then_inc(const_in, 16)
                sp.dma_start(R.ident_bf[:], I["ident_bf"]).then_inc(const_in, 16)
                sp.wait_ge(const_in, 32)

            @block.vector
            def _(dve):
                nc.vector.memset(R.ones[:], 1.0)
                nc.vector.memset(R.ones_bf[:], 1.0)
                for b in range(NB):
                    if b % (NB // 4) == 0:
                        dve.wait_ge(x_in[b // (NB // 4)], 16)
                    nc.vector.bn_stats(R.stats[:, b, :], R.x[:, b, :]).then_inc(R.stats_done, 1)


def renorm_phase(nc, R, out):
    view = out.rearrange("b t d -> t b d")
    with ExitStack() as stack:
        sb, ps, sem = allocator(nc, stack)
        norm = Norm(nc, R, sb, sem, "renorm")
        y_ready = sem("y_ready")
        kept = [sem(f"kept{i}") for i in range(PARTS)]
        with nc.Block() as block:
            @block.sync
            def _(sp):
                for i in range(PARTS):
                    q = slice(i * NB // PARTS, (i + 1) * NB // PARTS)
                    sp.dma_start(view[:, q, :], R.x[:, q, :]).then_inc(kept[i], 16)
                for i in range(PARTS):
                    sp.wait_ge(kept[i], 16)

            @block.scalar
            def _(act):
                norm.scalar(act)

            @block.vector
            def _(dve):
                norm.vector(dve)

                def group(g):
                    norm.apply(dve, g, R.x[:, bass.ds(g * GB, GB), :]).then_inc(y_ready, 1)
                    dve.wait_ge(y_ready, g + 1)
                    for j in range(GB):
                        b = g * GB + j
                        nc.vector.bn_stats(R.stats[:, b, :], R.x[:, b, :]).then_inc(R.stats_done, 1)

                for i in range(PARTS):
                    dve.wait_ge(kept[i], 16)
                    with dve.Fori(i * NG // PARTS, (i + 1) * NG // PARTS) as g:
                        group(g)
    R.kept = True


def attention_phase(nc, R, I, name, wq, wk, wv, wo, bq=None, bk=None, bv=None, bo=None, hepos=False,
                    own_keys=False, mask=None, causal=None, pad=None, ln=None):
    packed = not hepos
    TR = 3 * 32
    LN_SLOTS = (0, 0, 0, 0) if own_keys else (1, 1, 2, 2)
    SUM_SLOT, STATS_SLOTS = 7, (10, 11, 14, 15)
    TURN, VALUES, RECIP, OUTPUT = (3, 4, 5, 7) if packed else (2, 3, 3, 4)
    TAKE_SLOT = 12
    KN = P if own_keys else KC
    U = 1 if hepos else 4
    S = GB * U
    W = 4 * KN
    steps_of = ["ht", "k", "q", "v"] if own_keys else ["k", "ht", "q", "v"]
    slot_of = dict(zip(steps_of, (0, 1, 2, 3) if U == 1 else (0, 3, 5, 13) if not own_keys else (1, 3, 5, 13)))
    with ExitStack() as stack:
        sb, ps, sem = allocator(nc, stack)
        n_ = lambda s: f"{name}_{s}"
        norm = Norm(nc, R, sb, sem, name)
        Wq, Wk, Wv, Wo = (sb(n_(s), [P, D]) for s in ("wq", "wk", "wv", "wo"))
        cols = sb(n_("cols"), [P, 6])
        bvb = sb(n_("bv"), [P, GB * D]) if bv is not None else None
        bor = sb(n_("bo"), [1, D])
        H = sb(n_("h"), [P, GB, D])
        HT = [sb(n_(f"ht{i}"), [P, GT]) for i in range(2)]
        QT = [sb(n_(f"qt{i}"), [P, GT]) for i in range(1 if packed else 2)]
        KT = [sb(n_(f"kt{i}"), [P, GB, KN]) for i in range(1 if packed else 2)]
        if packed:
            HIGH = {"k": sb(n_("kh"), [P, GB * KN], F32R), "q": sb(n_("qh"), [P, GT], F32R)}
            LOW = {"k": sb(n_("kl"), [P, GB * KN], F32R), "q": sb(n_("ql"), [P, GT], F32R)}
            K3 = sb(n_("k3"), [TR, 4, GB, KN])
            Q3 = sb(n_("q3"), [TR, 4, GT])
            QR = [sb(n_(f"qr{i}"), [TR, 4, GT], F32R) for i in range(2)]
            slots = sb(n_("slots"), [TR, 4])
        CTX = [sb(n_(f"ctx{i}"), [P, GB, KN]) for i in range(2)] if not own_keys else None
        KM = [sb(n_(f"km{i}"), [TR, 4, GB, W], F32R) if packed else sb(n_(f"km{i}"), [P, GB, U, W]) for i in range(2)]
        VW = D if hepos else NH * 32
        VM = [sb(n_(f"vm{i}"), [P, GB, VW]) for i in range(2)]
        DM = sb(n_("dm"), [P, 4, 32])
        PR = [sb(n_(f"p{i}"), [P, W]) for i in range(4)]
        PT = [sb(n_(f"pt{i}"), [P, 4 * P]) for i in range(4)]
        MX = [sb(n_(f"mx{i}"), [P, 16 if hepos else 4]) for i in range(2)]
        RD = sb(n_("rd"), [P, P])
        CT = [sb(n_(f"ct{i}"), [P, P]) for i in range(2)]
        SC = [ps(n_(f"sc{i}"), [P, 512]) for i in range(2)]
        TP = [ps(n_(f"tp{i}"), [P, 512]) for i in range(2)]
        PJ = ps(n_("pj"), [P, 512])
        ND = [ps(n_(f"nd{i}"), [P, 4, P]) for i in range(2)]
        OUT = ps(n_("out"), [P, GB, D])
        if pad is not None:
            padu = sb(n_("padu"), [1, NB * KC], U8)
            padb = sb(n_("padb"), [1, NB, KC], BF16)
        if mask is not None:
            mski = sb(n_("mski"), [P, KC], I32)
            keep = sb(n_("keep"), [P, KC])
            some = sb(n_("some"), [P, 1])
            diag = sb(n_("diag"), [P, P], BF16)
            qfac = sb(n_("qfac"), [P, P])
        if mask is not None or causal is not None:
            addm = sb(n_("addm"), [P, KN], BF16)

        v_biased = sem(n_("v_biased"))
        weights_in = sem(n_("weights_in"))
        prep = sem(n_("prep"))
        prep_pool = sem(n_("prep_pool"))
        f_psum = sem(n_("f_psum"))
        ctx_in = [sem(n_(f"ctx_in{i}")) for i in range(2)]
        h_ready, h_used = sem(n_("h_ready")), sem(n_("h_used"))
        psum_done = {s: sem(n_(f"{s}_psum")) for s in steps_of}
        ready = {s: sem(n_(f"{s}_ready")) for s in steps_of}
        km_in = [sem(n_(f"km_in{i}")) for i in range(2)]
        if packed:
            high_ready = {s: sem(n_(f"{s}_high_ready")) for s in "kq"}
            low_ready = {s: sem(n_(f"{s}_low_ready")) for s in "kq"}
            k3_in = [sem(n_(f"k3_in{i}")) for i in range(4)]
            q3_in = [sem(n_(f"q3_in{i}")) for i in range(4)]
            km_ready = [sem(n_(f"km_ready{i}")) for i in range(4)]
            qr_ready = [sem(n_(f"qr_ready{i}")) for i in range(4)]
        sc_ready, mx_ready, sub_ready, exp_ready = (sem(n_(s)) for s in ("sc_ready", "mx_ready", "sub_ready", "exp_ready"))
        tp_ready, pt_ready, pv_done = (sem(n_(s)) for s in ("tp_ready", "pt_ready", "pv_done"))
        rd_ready, ct_ready, o_done, x_added = (sem(n_(s)) for s in ("rd_ready", "ct_ready", "o_done", "x_added"))

        n_weights = 4 + sum(a is not None for a in (bq, bk, bo, mask, causal, pad)) + (GB if bv is not None else 0)
        n_weights += 2 * (ln is not None) + 1
        n_prep = (bq is not None) + (pad is not None) + (5 if mask is not None else 0)

        def diagonal(vm):
            a = vm[0:KN, :, :]
            return bass.AP(a.tensor, a.offset, [list(a.ap[0]), [128, GB * 4], [40, 4], [1, 8]])

        with nc.Block() as block:
            @block.sync
            def _(sp):
                for t, w in ((Wq, wq), (Wk, wk), (Wv, wv), (Wo, wo)):
                    sp.dma_start(t[:], w).then_inc(weights_in, 16)
                for c, v in ((0, bq), (1, bk)) + (((3, ln[0]), (4, ln[1])) if ln else ()):
                    if v is not None:
                        sp.dma_start(cols[:, c:c + 1], v.rearrange("(p a) -> p a", a=1)).then_inc(weights_in, 16)
                if bv is not None:
                    for j in range(GB):
                        sp.dma_start(bvb[:, j * D:(j + 1) * D],
                                     v_broadcast(bv)).then_inc(weights_in, 16)
                if bo is not None:
                    sp.dma_start(bor[:], bo.rearrange("(a p) -> a p", a=1)).then_inc(weights_in, 16)
                if mask is not None:
                    sp.dma_start(mski[:], mask).then_inc(weights_in, 16)
                if causal is not None:
                    sp.dma_start(addm[:], causal).then_inc(weights_in, 16)
                if pad is not None:
                    sp.dma_start(padu[:], pad).then_inc(weights_in, 16)
                if hepos:
                    sp.dma_start(DM[0:KC, 0, :], I["classes"]).then_inc(weights_in, 16)
                else:
                    sp.dma_start(slots[:], I["slots"]).then_inc(weights_in, 16)

                def ctx_load(g, par):
                    at_least(sp, psum_done["v"], g - 1)
                    sp.dma_start(CTX[par][:], I["ctxT"][:, bass.ds(g * GB, GB), :]).then_inc(ctx_in[par], 16)

                def stack_terms(g, par):
                    sp.wait_ge(low_ready["k"], g + 1)
                    for i in range(4):
                        at_least(sp, km_ready[i], g)
                        for term, part in enumerate((HIGH, LOW, HIGH)):
                            sp.dma_start(K3[32 * term:32 * term + 32, i, :, :].rearrange("p b k -> p (b k)"),
                                         part["k"][32 * i:32 * i + 32, :].bitcast(F32)).then_inc(k3_in[i], 16)
                    sp.wait_ge(low_ready["q"], g + 1)
                    for i in range(4):
                        at_least(sp, qr_ready[i], g)
                        for term, part in enumerate((HIGH, HIGH, LOW)):
                            sp.dma_start(Q3[32 * term:32 * term + 32, i, :],
                                         part["q"][32 * i:32 * i + 32, :].bitcast(F32)).then_inc(q3_in[i], 16)

                def spread(g, par, first):
                    if packed:
                        stack_terms(g, par)
                        return
                    sp.wait_ge(ready["k"], g + 1)
                    if first:
                        sp.wait_ge(prep_pool, 4)
                    for h in range(NH):
                        i, j = h % 4, h // 4
                        rows = slice(HD * h, HD * h + HD)
                        if hepos:
                            c = i
                            dst = KM[par][rows, :, 0, j * KC + c * KCLS:j * KC + (c + 1) * KCLS]
                            src = KT[par][rows, :, c * KCLS:(c + 1) * KCLS]
                        else:
                            dst = KM[par][rows, :, i, j * KN:(j + 1) * KN]
                            src = KT[par][rows, :, :]
                        sp.dma_start(dst, src).then_inc(km_in[par], 16)

                if own_keys:
                    groups_loop(sp, lambda g, par, first, last: stack_terms(g, par), 3)
                    return
                ctx_load(0, 0)
                ctx_load(1, 1)
                spread(0, 0, True)
                def pair(g):
                    ctx_load(g + 2, 0)
                    spread(g + 1, 1, False)
                    ctx_load(g + 3, 1)
                    spread(g + 2, 0, False)

                pairs_loop(sp, NG - 2, pair)
                spread(NG - 1, 1, False)

            @block.gpsimd
            def _(pool):
                for t in (KM if hepos else []) + VM:
                    nc.gpsimd.memset(t[:], 0.0).then_inc(prep_pool, 1)
                if not packed:
                    return
                nc.gpsimd.memset(DM[:], 0.0).then_inc(prep_pool, 1)
                pool.wait_ge(prep_pool, 3)
                for i in range(4):
                    nc.gpsimd.memset(DM[:, i, 8 * i:8 * i + 8], 1.0).then_inc(prep_pool, 1)
                pool.wait_ge(weights_in, 16 * n_weights)

                def low_part(step, g):
                    src = QT[0][:] if step == "q" else KT[0][:].rearrange("p b k -> p (b k)")
                    for i in range(4):
                        at_least(pool, (k3_in if step == "k" else q3_in)[i], 48 * g)
                    pool.wait_ge(high_ready[step], g + 1)
                    nc.gpsimd.tensor_tensor(LOW[step][:], src, HIGH[step][:].bitcast(F32),
                                            ALU.subtract).then_inc(low_ready[step], 1)

                def masked_keys(g, par, units):
                    at_least(pool, sc_ready, (g - 1) * S)
                    for i in units:
                        pool.wait_ge(k3_in[i], 48 * (g + 1))
                        nc.gpsimd.tensor_tensor(
                            KM[par][:, i, :, :].rearrange("p b (j k) -> p b j k", k=KN),
                            K3[:, i, :, :].unsqueeze(2).to_broadcast([TR, GB, 4, KN]),
                            slots[:].unsqueeze(1).unsqueeze(3).to_broadcast([TR, GB, 4, KN]),
                            ALU.mult).then_inc(km_ready[i], 1)

                def prepare(g, par):
                    low_part("k", g)
                    masked_keys(g, par, (0,))
                    low_part("q", g)
                    masked_keys(g, par, (1, 2, 3))

                def group(g, par, first, last):
                    if not last:
                        prepare(g + 1, 1 - par)

                prepare(0, 0)
                groups_loop(pool, group)

            @block.vector
            def _(dve):
                v = nc.vector
                norm.vector(dve)
                dve.wait_ge(weights_in, 16 * n_weights)
                done = 0
                if bq is not None:
                    v.tensor_scalar(cols[:, 2:3], cols[:, 0:1], SCALE, None, ALU.mult).then_inc(prep, 1)
                    done += 1
                if pad is not None:
                    v.tensor_scalar(padb[0:1, :, :], padu[0:1, :].rearrange("p (b k) -> p b k", k=KC), FAR, None,
                                    ALU.mult).then_inc(prep, 1)
                    done += 1
                if mask is not None:
                    v.tensor_scalar(keep[:], mski[:], 0.0, None, ALU.not_equal).then_inc(prep, 1)
                    v.tensor_scalar(addm[:], mski[:], 0.0, -1.0e9, ALU.is_equal, ALU.mult).then_inc(prep, 1)
                    done += 2
                    dve.wait_ge(prep, done)
                    v.tensor_reduce(some[:], keep[:], AX.X, ALU.max).then_inc(prep, 1)
                    dve.wait_ge(prep, done + 1)
                    v.tensor_scalar(diag[:], R.ident[:], some[:, 0:1], None, ALU.mult).then_inc(prep, 1)
                    dve.wait_ge(f_psum, 1)
                    v.tensor_scalar(qfac[:], OUT[:, 0, :], SCALE, None, ALU.mult).then_inc(prep, 1)
                    done += 3
                    dve.wait_ge(prep, done)

                def ln_group(g):
                    at_least(dve, psum_done["ht"], g)
                    norm.apply(dve, g, H).then_inc(h_ready, 1)

                def ln_sequence(g, j):
                    at_least(dve, psum_done["ht"], g)
                    ins = norm.apply_one(dve, g, j, H)
                    if j == GB - 1:
                        ins.then_inc(h_ready, 1)

                def q_evict(g, par):
                    dve.wait_ge(psum_done["q"], g + 1)
                    at_least(dve, low_ready["q"], g)
                    o = QT[0][:].rearrange("p (b t) -> p b t", b=GB)
                    i = PJ[:].rearrange("p (b t) -> p b t", b=GB)
                    f = qfac[:].unsqueeze(1).to_broadcast([P, GB, P])
                    v.scalar_tensor_tensor(o, i, cols[:, 0:1], f, ALU.add, ALU.mult).then_inc(ready["q"], 1)

                def v_evict(g, par, first):
                    dve.wait_ge(psum_done["v"], g + 1)
                    if first:
                        dve.wait_ge(prep_pool, 4 if hepos else 2)
                    src = PJ[0:KN, :]
                    if hepos:
                        o = VM[par][0:KN, :, :].rearrange("p b (i c) -> p (b i) c", c=32)
                        cm = DM[0:KN, 0, :].unsqueeze(1).to_broadcast([KN, GB * 4, 32])
                        s = src.rearrange("p (b c) -> p b c", c=32)
                        v.tensor_tensor(s, s, bvb[0:KN, :].rearrange("p (b c) -> p b c", c=32),
                                        ALU.add).then_inc(v_biased, 1)
                        dve.wait_ge(v_biased, g + 1)
                        v.tensor_tensor(o, s, cm, ALU.mult).then_inc(ready["v"], 1)
                    elif bv is not None:
                        v.tensor_tensor(diagonal(VM[par]), src.rearrange("p (b i d) -> p b i d", i=4, d=8),
                                        bvb[0:KN, :].rearrange("p (b i d) -> p b i d", i=4, d=8),
                                        ALU.add).then_inc(ready["v"], 1)
                    else:
                        v.tensor_copy(diagonal(VM[par]), src.rearrange("p (b i d) -> p b i d", i=4, d=8)
                                      ).then_inc(ready["v"], 1)

                def softmax_shift(g, s, between=()):
                    n = g * S + s
                    sc, mx = SC[s % 2], MX[s % 2]
                    k = KCLS if hepos else KN
                    heads = W // k
                    view = sc[:, 0:W].rearrange("p (h k) -> p h k", k=k)
                    dve.wait_ge(sc_ready, n + 1)
                    v.tensor_reduce(mx[:], view, AX.X, ALU.max).then_inc(mx_ready, 1)
                    for f in between:
                        f()
                    at_least(dve, tp_ready, n - 3)
                    dve.wait_ge(mx_ready, n + 1)
                    v.tensor_tensor(PR[s % 4][:].rearrange("p (h k) -> p h k", k=k), view,
                                    mx[:].unsqueeze(2).to_broadcast([P, heads, k]),
                                    ALU.subtract).then_inc(sub_ready, 1)

                def reciprocals(b, bt):
                    dve.wait_ge(pv_done, b * U + U)
                    at_least(dve, ct_ready, b)
                    v.reciprocal(RD[:], ND[bt % 2][:, 1, :]).then_inc(rd_ready, 1)

                def normalise(b, bt):
                    at_least(dve, o_done, b - 1)
                    dve.wait_ge(rd_ready, b + 1)
                    v.tensor_tensor(CT[bt % 2][:], ND[bt % 2][:, 0, :], RD[:], ALU.mult).then_inc(ct_ready, 1)

                def add_out(g):
                    dve.wait_ge(o_done, g * GB + GB)
                    residual(nc, R, dve, x_added, g, OUT[:], g + 1)

                def add_sum(g):
                    dve.wait_ge(o_done, g * GB + GB)
                    xg = R.x[:, bass.ds(g * GB, GB), :]
                    v.tensor_tensor(xg, xg, OUT[:], ALU.add).then_inc(x_added, 1)

                def statistics(g, j):
                    dve.wait_ge(x_added, g + 1)
                    b = g * GB + j
                    v.bn_stats(R.stats[:, b, :], R.x[:, b, :]).then_inc(R.stats_done, 1)

                def of_sequence(f, g, u):
                    f(g * GB + u // U, (u // U) % GB)

                def evicts(g, s, par):
                    if mask is not None and slot_of["q"] == s:
                        q_evict(g, par)
                    if slot_of["v"] == s:
                        v_evict(g, par, False)

                def work_at(g, s, par, first, last):
                    steps = []
                    u = s - RECIP
                    if (u + 1) % U == 0 and not (first and u < 0):
                        steps.append(lambda: of_sequence(reciprocals, g, u))
                        if U == 1:
                            steps.append(lambda: of_sequence(normalise, g, u))
                    if U > 1 and u % U == 0 and not (first and u <= 0):
                        steps.append(lambda: of_sequence(normalise, g, u - 1))
                    if not last:
                        if U > 1:
                            steps += [lambda j=j: ln_sequence(g + 1, j) for j in range(GB) if LN_SLOTS[j] == s]
                        steps.append(lambda: evicts(g + 1, s, 1 - par))
                    if not first:
                        if U == 1:
                            if s == 3:
                                steps.append(lambda: add_out(g - 1))
                        elif s == SUM_SLOT:
                            steps.append(lambda: add_sum(g - 1))
                        else:
                            steps += [lambda j=j: statistics(g - 1, j) for j in range(GB) if STATS_SLOTS[j] == s]
                    return steps

                def group(g, par, first, last):
                    for s in range(S):
                        work = work_at(g, s, par, first, last)
                        if U == 1 and s == 0 and not last:
                            ln_group(g + 1)
                        softmax_shift(g, s, () if U == 1 else work)
                        if U == 1:
                            for f in work:
                                f()
                    if last:
                        for u in range(S - RECIP, S):
                            if (u + 1) % U == 0:
                                of_sequence(reciprocals, g, u)
                                of_sequence(normalise, g, u)
                        add_out(g)

                ln_group(0)
                if mask is not None:
                    q_evict(0, 0)
                v_evict(0, 0, True)
                groups_loop(dve, group, 3 if U == 1 else 1)

            @block.scalar
            def _(act):
                a = nc.scalar
                norm.scalar(act)
                act.wait_ge(weights_in, 16 * n_weights)
                at_least(act, prep, n_prep)

                def high_part(step, g):
                    src = QT[0][:] if step == "q" else KT[0][:].rearrange("p b k -> p (b k)")
                    act.wait_ge(ready[step], g + 1)
                    for i in range(4):
                        at_least(act, (k3_in if step == "k" else q3_in)[i], 48 * g)
                    a.activation(HIGH[step][:], src, ACT.Copy).then_inc(high_ready[step], 1)

                def evict(step, g, par):
                    if step == "v" or (step == "q" and mask is not None):
                        return
                    act.wait_ge(psum_done[step], g + 1)
                    pj = PJ
                    if step == "ht":
                        if ln:
                            ins = a.activation(HT[par][:], pj[:], ACT.Identity, scale=cols[:, 3:4], bias=cols[:, 4:5])
                        else:
                            ins = a.activation(HT[par][:], pj[:], ACT.Copy)
                    elif step == "q":
                        if packed:
                            at_least(act, low_ready["q"], g)
                        q_out = QT[0 if packed else par][:]
                        if bq is not None:
                            ins = a.activation(q_out, pj[:], ACT.Identity, scale=SCALE, bias=cols[:, 2:3])
                        else:
                            ins = a.activation(q_out, pj[:], ACT.Copy, scale=SCALE)
                    else:
                        if packed:
                            at_least(act, low_ready["k"], g)
                        else:
                            at_least(act, km_in[par], km_count(g - 2, par))
                        k_in = pj[:, 0:W].rearrange("p (b k) -> p b k", k=KN)
                        k_out = KT[0 if packed else par][:]
                        if bk is not None:
                            ins = a.activation(k_out, k_in, ACT.Identity, bias=cols[:, 1:2])
                        else:
                            ins = a.activation(k_out, k_in, ACT.Copy)
                    ins.then_inc(ready[step], 1)

                def take_queries(g, par, i):
                    act.wait_ge(q3_in[i], 48 * (g + 1))
                    at_least(act, sc_ready, (g - 1) * S)
                    a.activation(QR[par][:, i, :], Q3[:, i, :], ACT.Copy).then_inc(qr_ready[i], 1)

                def exponentials(g, s):
                    n = g * S + s
                    act.wait_ge(sub_ready, n + 1)
                    a.activation(PR[s % 4][:], PR[s % 4][:], ACT.Exp).then_inc(exp_ready, 1)

                def turned(g, s):
                    n = g * S + s
                    act.wait_ge(tp_ready, n + 1)
                    at_least(act, pv_done, n - 3)
                    a.activation(PT[s % 4][0:KN, :], TP[s % 2][0:KN, :], ACT.Copy).then_inc(pt_ready, 1)

                def group(g, par, first, last):
                    for s in range(S):
                        if not (first and s < TURN):
                            turned(g, s - TURN)
                        exponentials(g, s)
                        if not last:
                            for step in steps_of:
                                if slot_of[step] == s:
                                    evict(step, g + 1, 1 - par)
                                    if packed and step in "kq":
                                        high_part(step, g + 1)
                            if packed and s >= TAKE_SLOT:
                                take_queries(g + 1, 1 - par, s - TAKE_SLOT)
                    if last:
                        for u in range(S - TURN, S):
                            turned(g, u)

                for step in steps_of:
                    evict(step, 0, 0)
                    if packed and step in "kq":
                        high_part(step, 0)
                if packed:
                    for i in range(4):
                        take_queries(0, 0, i)
                groups_loop(act, group, 3 if U == 1 else 1)

            @block.tensor
            def _(pe):
                t = nc.tensor
                pe.wait_ge(weights_in, 16 * n_weights)
                at_least(pe, prep, n_prep - 1 if mask is not None else n_prep)
                if mask is not None:
                    t.matmul(OUT[:, 0, :], R.ones_bf[:], diag[:], start=True, stop=True).then_inc(f_psum, 1)
                pe.wait_ge(prep_pool, 4 if hepos else 7)

                def project(step, g, par):
                    pj = PJ
                    n = steps_of.index(step)
                    at_least(pe, ready[steps_of[n - 1]], g + 1 if n else g)
                    if step == "ht":
                        pe.wait_ge(h_ready, g + 1)
                        for j in range(GB):
                            last = t.transpose(pj[:, j * P:(j + 1) * P], H[:, j, :], R.ident[:])
                    elif step == "q":
                        pe.wait_ge(ready["ht"], g + 1)
                        last = t.matmul(pj[:], Wq[:], HT[par][:], start=True, stop=True)
                    elif step == "k":
                        keys_there(g, par)
                        src = HT[par][:] if own_keys else CTX[par][:].rearrange("p b k -> p (b k)")
                        last = t.matmul(pj[:, 0:W], Wk[:], src, start=True, stop=True)
                    else:
                        keys_there(g, par)
                        for j in range(GB):
                            src = HT[par][:, j * P:(j + 1) * P] if own_keys else CTX[par][:, j, :]
                            last = t.matmul(pj[0:KN, j * D:(j + 1) * D], src, Wv[:], start=True, stop=True)
                    last.then_inc(psum_done[step], 1)

                def keys_there(g, par):
                    if own_keys:
                        pe.wait_ge(ready["ht"], g + 1)
                    else:
                        pe.wait_ge(ctx_in[par], ctx_count(g, par))

                def scores(g, s, par):
                    n = g * S + s
                    j, i = s // U, s % U
                    if packed and j == 0:
                        pe.wait_ge(km_ready[i], g + 1)
                        pe.wait_ge(qr_ready[i], g + 1)
                    if hepos and s == 0:
                        pe.wait_ge(km_in[par], km_count(g, par))
                        pe.wait_ge(ready["q"], g + 1)
                    at_least(pe, sub_ready, n - 1)
                    masked = addm_there = mask is not None or causal is not None or pad is not None
                    queries, keys = ((QR[par][:, i, j * P:(j + 1) * P], KM[par][:, i, j, :]) if packed else
                                     (QT[par][:, j * P:(j + 1) * P], KM[par][:, j, i, :]))
                    last = t.matmul(SC[s % 2][:, 0:W], queries, keys, start=True, stop=not masked)
                    if pad is not None:
                        b = g * GB + j
                        rows = padb[0:1, b, :].unsqueeze(1).to_broadcast([1, 4, KC])
                        last = t.matmul(SC[s % 2][:, 0:W], R.ones_bf[0:1, :], rows, start=False, stop=True)
                    elif masked:
                        last = t.matmul(SC[s % 2][:, 0:W], R.ident_bf[:],
                                        addm[:].unsqueeze(1).to_broadcast([P, 4, KN]), start=False, stop=True)
                    last.then_inc(sc_ready, 1)

                def turn(g, s):
                    n = g * S + s
                    pe.wait_ge(exp_ready, n + 1)
                    at_least(pe, pt_ready, n - 1)
                    for q in range(4):
                        last = t.transpose(TP[s % 2][0:KN, q * P:(q + 1) * P], PR[s % 4][:, q * KN:(q + 1) * KN],
                                           R.ident[:])
                    last.then_inc(tp_ready, 1)

                def values(g, s, par):
                    n = g * S + s
                    j, i = (s // U) % GB, s % U
                    if s % S == 0:
                        pe.wait_ge(ready["v"], g + s // S + 1)
                    pe.wait_ge(pt_ready, n + 1)
                    if i == 0:
                        at_least(pe, ct_ready, g * GB + s // U - 1)
                    for what in range(2):
                        for q in range(4):
                            if what == 1:
                                w = DM[0:KN, i, :]
                            elif hepos:
                                w = VM[par][0:KN, j, 32 * q:32 * q + 32]
                            else:
                                h = 4 * q + i
                                w = VM[par][0:KN, j, 32 * h:32 * h + 32]
                            last = t.matmul(ND[j % 2][32 * q:32 * q + 32, what, :], w,
                                            PT[s % 4][0:KN, q * P:(q + 1) * P],
                                            start=(what == 0 and i == 0), stop=(i == U - 1), skip_group_check=True,
                                            tile_position=(0, 32 * q))
                    last.then_inc(pv_done, 1)

                def output(g, b, bt):
                    pe.wait_ge(ct_ready, b + 1)
                    if bt == 0:
                        at_least(pe, x_added, g)
                    last = t.matmul(OUT[:, bt, :], CT[bt % 2][:], Wo[:], start=True, stop=bo is None)
                    if bo is not None:
                        last = t.matmul(OUT[:, bt, :], R.ones[0:1, :], bor[:], start=False, stop=True)
                    last.then_inc(o_done, 1)

                def behind(g, s, par, first):
                    if not (first and s < TURN) and s - TURN < S:
                        turn(g, s - TURN)
                    if not (first and s < VALUES) and s - VALUES < S:
                        values(g, s - VALUES, par if s >= VALUES else 1 - par)
                    u = s - OUTPUT
                    if not (first and u < 0) and (u + 1) % U == 0:
                        gg = g if u >= 0 else g - 1
                        output(gg, g * GB + u // U, (u // U) % GB)

                def group(g, par, first, last):
                    for s in range(S):
                        scores(g, s, par)
                        behind(g, s, par, first)
                        if not last:
                            for step in steps_of:
                                if slot_of[step] == s:
                                    project(step, g + 1, 1 - par)
                    if last:
                        for s in range(S, S + OUTPUT):
                            behind(g, s, par, False)

                for step in steps_of:
                    project(step, 0, 0)
                groups_loop(pe, group, 3 if U == 1 else 1)


def ctx_count(g, par):
    return (g + 2 - par) * 8


def km_count(g, par):
    return (g + 2 - par) * (8 * NH)


def v_broadcast(v):
    return v.rearrange("(a p) -> a p", a=1).to_broadcast([P, D])


class Experts:

    def __init__(self, nc, R, sb, sem, name, E):
        self.E = E
        self.ht = sb(name + "_htall", [P, NB * P])
        self.logits = sb(name + "_logits", [P, NB, E])
        self.gates = sb(name + "_gates", [P, NB, E])


def top_choices(nc, v, link, X, cur, scratch, rank, E, k, chosen, each=None):
    m, eq, r = scratch
    bc = lambda a: a.unsqueeze(2).to_broadcast([P, NB, E])
    for it in range(k):
        link(v.tensor_reduce(m[:], cur, AX.X, ALU.max))
        link(v.tensor_tensor(eq[:], cur, bc(m[:]), ALU.is_equal))
        link(v.tensor_tensor(eq[:], eq[:], rank[:].unsqueeze(1).to_broadcast([P, NB, E]), ALU.mult))
        link(v.tensor_reduce(r[:], eq[:], AX.X, ALU.max))
        one = each[it] if each is not None else eq[:]
        link(v.tensor_tensor(one, eq[:], bc(r[:]), ALU.is_equal))
        if it == 0:
            link(v.tensor_copy(chosen, one))
        else:
            link(v.tensor_tensor(chosen, chosen, one, ALU.add))
        if it < k - 1:
            link(v.scalar_tensor_tensor(cur, one, -3.0e38, cur, ALU.mult, ALU.add))


def routing_part(nc, R, I, name, X, kind, wr, loads, extra, splits=()):
    E = X.E
    TOP = {"proto": 2, "shared": 4, "capacity": 2, "swiglu": 2}[kind]
    with ExitStack() as stack:
        sb, ps, sem = allocator(nc, stack)
        n_ = lambda s: f"{name}r_{s}"
        norm = Norm(nc, R, sb, sem, n_("n"))
        WR = sb(n_("wr"), [P, E])
        rank = sb(n_("rank"), [P, E])
        H = [sb(n_(f"h{i}"), [P, GB, D]) for i in range(2)]
        HS = [sb(n_(f"hs{i}"), [P, GT]) for i in range(2)]
        m, r = sb(n_("m"), [P, NB]), sb(n_("r"), [P, NB])
        eq = sb(n_("eq"), [P, NB, E])
        ex = sb(n_("ex"), [P, NB, E])
        dist = sb(n_("dist"), [P, NB, E])
        TR = [ps(n_(f"tr{i}"), [P, 512]) for i in range(2)]
        LG = [ps(n_(f"lg{i}"), [P, GB, E]) for i in range(2)]
        small_in, big_in = sem(n_("small_in")), sem(n_("big_in"))
        raw = [sb(n_(f"raw{i}"), hi.shape) for i, (_, hi, _) in enumerate(splits)]
        raw_in = [sem(n_(f"raw_in{i}")) for i in range(len(splits))]
        high_ready, low_ready = sem(n_("high_ready")), sem(n_("low_ready"))
        h_ready, tr_ready, hs_ready, lg_ready, l_ready = (sem(n_(s)) for s in
                                                         ("h_ready", "tr_ready", "hs_ready", "lg_ready", "l_ready"))
        ht_in, chain, act_step, pe_step = [sem(n_(f"ht_in{i}")) for i in range(2)], sem(n_("chain")), sem(n_("act_step")), sem(n_("pe_step"))
        act_go, pe_go, scans, x2_ready = (sem(n_(s)) for s in ("act_go", "pe_go", "scans", "x2_ready"))
        if kind == "proto":
            psq = sb(n_("psq"), [P, E])
            protoT2 = sb(n_("protoT2"), [P, E])
            x2 = sb(n_("x2"), [P, NB])
            junk = sb(n_("junk"), [P, 2, GB, D])
            temp = sb(n_("temp"), [P, 2])
            PQ = ps(n_("pq"), [P, E])
        if kind == "swiglu":
            lnc = sb(n_("lnc"), [P, 2])
        if kind == "capacity":
            one = [sb(n_(f"one{i}"), [P, NB, E]) for i in range(2)]
            oneb = [sb(n_(f"oneb{i}"), [P, NB, E], BF16) for i in range(2)]
            tri = sb(n_("tri"), [P, P], BF16)
            total = [sb(n_(f"total{i}"), [P, NB, E]) for i in range(2)]
            run = [sb(n_(f"run{i}"), [P, NB, E]) for i in range(2)]
            ones64 = sb(n_("ones64"), [P, NB])
            CUM = [ps(n_(f"cum{i}"), [P, NB * E]) for i in range(2)]
            TOT = [ps(n_("tot0"), [P, NB * E]), ps(n_("tot1"), [P, NB * E])]
        n_small = 2 + {"proto": 1, "shared": 0, "capacity": 1, "swiglu": 2}[kind]

        with nc.Block() as block:
            @block.sync
            def _(sp):
                sp.dma_start(WR[:], wr).then_inc(small_in, 16)
                sp.dma_start(rank[:], extra["rank"].to_broadcast([P, E])).then_inc(small_in, 16)
                if kind == "proto":
                    sp.dma_start(temp[:, 0:1], extra["temp"].to_broadcast([P, 1])).then_inc(small_in, 16)
                if kind == "swiglu":
                    for c in range(2):
                        sp.dma_start(lnc[:, c:c + 1], extra["ln"][c].rearrange("(p a) -> p a", a=1)).then_inc(small_in, 16)
                if kind == "capacity":
                    sp.dma_start(tri[:], I["tri"]).then_inc(small_in, 16)
                for i, (w, hi, lo) in enumerate(splits):
                    sp.dma_start(raw[i][:], w).then_inc(raw_in[i], 16)
                for t, w in loads:
                    sp.dma_start(t, w).then_inc(big_in, 16)

                def keep(g, par):
                    sp.wait_ge(hs_ready, g + 1)
                    sp.dma_start(X.ht[:, bass.ds(g * GT, GT)], HS[par][:]).then_inc(ht_in[par], 16)

                def pair(g):
                    keep(g, 0)
                    keep(g + 1, 1)

                pairs_loop(sp, NG, pair)
                for i in range(2):
                    sp.wait_ge(ht_in[i], 8 * NG)
                sp.wait_ge(big_in, 16 * len(loads))

            @block.gpsimd
            def _(pool):
                for i, (w, hi, lo) in enumerate(splits):
                    pool.wait_ge(raw_in[i], 16)
                    nc.gpsimd.tensor_copy(hi[:], raw[i][:]).then_inc(high_ready, 1)
                    pool.wait_ge(high_ready, i + 1)
                    nc.gpsimd.tensor_tensor(lo[:], raw[i][:], hi[:].bitcast(F32), ALU.subtract).then_inc(low_ready, 1)

            @block.tensor
            def _(pe):
                t = nc.tensor
                pe.wait_ge(small_in, 16 * n_small)
                if kind == "proto":
                    pe.wait_ge(chain, 1)
                    t.matmul(PQ[:], R.ones[:], protoT2[:], start=True, stop=True).then_inc(pe_step, 1)

                def turn(g, par):
                    pe.wait_ge(h_ready, g + 1)
                    at_least(pe, hs_ready, g - 1)
                    for j in range(GB):
                        last = t.transpose(TR[par][:, j * P:(j + 1) * P], H[par][:, j, :], R.ident[:])
                    last.then_inc(tr_ready, 1)

                def scores(g, par):
                    pe.wait_ge(hs_ready, g + 1)
                    at_least(pe, l_ready, g - 1)
                    for j in range(GB):
                        last = t.matmul(LG[par][:, j, :], HS[par][:, j * P:(j + 1) * P], WR[:], start=True, stop=True)
                    last.then_inc(lg_ready, 1)

                turn(0, 0)
                def pair(g):
                    turn(g + 1, 1)
                    scores(g, 0)
                    turn(g + 2, 0)
                    scores(g + 1, 1)

                pairs_loop(pe, NG - 2, pair)
                turn(NG - 1, 1)
                scores(NG - 2, 0)
                scores(NG - 1, 1)
                if kind == "capacity":
                    for i in range(2):
                        pe.wait_ge(pe_go, i + 1)
                        flat = oneb[i][:].rearrange("p b e -> p (b e)")
                        t.matmul(CUM[i][:], tri[:], flat, start=True, stop=True)
                        t.matmul(TOT[i][:], R.ones_bf[:], flat, start=True, stop=True).then_inc(pe_step, 1)

            @block.scalar
            def _(act):
                a = nc.scalar
                norm.scalar(act)
                act.wait_ge(small_in, 16 * n_small)

                def hs(g, par):
                    act.wait_ge(tr_ready, g + 1)
                    at_least(act, ht_in[par], (g - par) * 8)
                    at_least(act, lg_ready, g - 1)
                    if kind == "swiglu":
                        ins = a.activation(HS[par][:], TR[par][:], ACT.Identity, scale=lnc[:, 0:1], bias=lnc[:, 1:2])
                    else:
                        ins = a.activation(HS[par][:], TR[par][:], ACT.Copy)
                    ins.then_inc(hs_ready, 1)

                def lg(g, par):
                    act.wait_ge(lg_ready, g + 1)
                    a.activation(X.logits[:, bass.ds(g * GB, GB), :], LG[par][:], ACT.Copy).then_inc(l_ready, 1)

                hs(0, 0)
                def pair(g):
                    hs(g + 1, 1)
                    lg(g, 0)
                    hs(g + 2, 0)
                    lg(g + 1, 1)

                pairs_loop(act, NG - 2, pair)
                hs(NG - 1, 1)
                lg(NG - 2, 0)
                lg(NG - 1, 1)
                if kind == "proto":
                    act.wait_ge(act_go, 1)
                    a.activation(dist[:], dist[:], ACT.Sqrt).then_inc(act_step, 1)
                    act.wait_ge(act_go, 2)
                    a.activation(ex[:], ex[:], ACT.Exp, scale=temp[:, 1:2]).then_inc(act_step, 1)
                else:
                    act.wait_ge(act_go, 1)
                    a.activation(ex[:], ex[:], ACT.Exp).then_inc(act_step, 1)

            @block.vector
            def _(dve):
                v = nc.vector
                count = [0]

                def link(ins):
                    count[0] += 1
                    ins.then_inc(chain, 1)
                    dve.wait_ge(chain, count[0])

                norm.vector(dve)
                dve.wait_ge(small_in, 16 * n_small)
                if kind == "proto":
                    link(v.tensor_tensor(protoT2[:], WR[:], WR[:], ALU.mult))
                    dve.wait_ge(pe_step, 1)
                    link(v.tensor_copy(psq[:], PQ[:]))
                    link(v.tensor_scalar(temp[:, 1:2], temp[:, 0:1], -1.0, None, ALU.mult))
                    link(v.tensor_tensor(temp[:, 0:1], temp[:, 0:1], temp[:, 1:2], ALU.max))
                    link(v.tensor_scalar(temp[:, 0:1], temp[:, 0:1], 0.1, None, ALU.max))
                    link(v.reciprocal(temp[:, 1:2], temp[:, 0:1]))
                    link(v.tensor_scalar(temp[:, 1:2], temp[:, 1:2], -1.0, None, ALU.mult))

                def ln_group(g, par):
                    at_least(dve, tr_ready, g - 1)
                    norm.apply(dve, g, H[par]).then_inc(h_ready, 1)
                    if kind == "proto":
                        dve.wait_ge(h_ready, g + 1)
                        at_least(dve, x2_ready, (g - 1) * GB)
                        for j in range(GB):
                            b = g * GB + j
                            v.scalar_tensor_tensor(junk[:, par, j, :], H[par][:, j, :], 1.0, H[par][:, j, :], ALU.mult, ALU.mult,
                                                   accum_out=x2[:, bass.ds(b, 1)]).then_inc(x2_ready, 1)

                def pair(g):
                    ln_group(g, 0)
                    ln_group(g + 1, 1)

                pairs_loop(dve, NG, pair)
                dve.wait_ge(l_ready, NG)
                bc = lambda a: a.unsqueeze(2).to_broadcast([P, NB, E])
                L = X.logits
                scratch = (m, eq, r)
                if kind == "proto":
                    dve.wait_ge(x2_ready, NB)
                    link(v.tensor_copy(eq[:], psq[:].unsqueeze(1).to_broadcast([P, NB, E])))
                    link(v.tensor_tensor(eq[:], eq[:], bc(x2[:]), ALU.add))
                    link(v.scalar_tensor_tensor(L[:], L[:], -2.0, eq[:], ALU.mult, ALU.add))
                    v.tensor_scalar(dist[:], L[:], 0.0, None, ALU.max).then_inc(chain, 1)
                    count[0] += 1
                    link(v.tensor_scalar(eq[:], L[:], 0.0, -1.0, ALU.max, ALU.mult))
                    v.tensor_copy(L[:], eq[:]).then_inc(act_go, 1)
                    dve.wait_ge(act_go, 1)
                    top_choices(nc, v, link, X, L[:], scratch, rank, E, TOP, X.gates[:])
                    dve.wait_ge(act_step, 1)
                    link(v.tensor_reduce(m[:], dist[:], AX.X, ALU.min))
                    v.tensor_tensor(ex[:], dist[:], bc(m[:]), ALU.subtract).then_inc(act_go, 1)
                    dve.wait_ge(act_step, 2)
                else:
                    link(v.tensor_reduce(m[:], L[:], AX.X, ALU.max))
                    v.tensor_tensor(ex[:], L[:], bc(m[:]), ALU.subtract).then_inc(act_go, 1)
                    dve.wait_ge(act_go, 1)
                    top_choices(nc, v, link, X, L[:], scratch, rank, E, TOP, X.gates[:],
                                [o[:] for o in one] if kind == "capacity" else None)
                    dve.wait_ge(act_step, 1)
                G = X.gates[:]
                if kind == "shared":
                    link(v.tensor_reduce(m[:], ex[:], AX.X, ALU.add))
                    link(v.tensor_tensor(G, G, ex[:], ALU.mult))
                else:
                    link(v.tensor_tensor(G, G, ex[:], ALU.mult))
                    link(v.tensor_reduce(m[:], G, AX.X, ALU.add))
                link(v.reciprocal(r[:], m[:]))
                link(v.tensor_tensor(G, G, bc(r[:]), ALU.mult))
                if kind == "capacity":
                    link(v.memset(ones64[:], 1.0))
                    for i in range(2):
                        v.tensor_copy(oneb[i][:], one[i][:]).then_inc(pe_go, 1)
                    for i in range(2):
                        dve.wait_ge(pe_step, i + 1)
                        link(v.tensor_copy(total[i][:], TOT[i][:].rearrange("p (b e) -> p b e", e=E)))
                        for e in range(E):
                            ins = v.tensor_tensor_scan(run[i][:, :, e], ones64[:], total[i][:, :, e], 0.0, ALU.mult,
                                                       ALU.add)
                            if e == E - 1:
                                link(ins)
                            else:
                                ins.then_inc(scans, 1)
                        dve.wait_ge(scans, (E - 1) * (i + 1))
                        link(v.tensor_tensor(total[i][:], run[i][:], total[i][:], ALU.subtract))
                        link(v.tensor_tensor(total[i][:], CUM[i][:].rearrange("p (b e) -> p b e", e=E), total[i][:],
                                             ALU.add))
                        if i == 1:
                            link(v.tensor_tensor(total[1][:], total[1][:],
                                                 run[0][:, NB - 1, :].unsqueeze(1).to_broadcast([P, NB, E]), ALU.add))
                        link(v.scalar_tensor_tensor(one[i][:], total[i][:], float(extra["cap"]) + 0.5, one[i][:],
                                                    ALU.is_lt, ALU.mult))
                    link(v.tensor_tensor(one[0][:], one[0][:], one[1][:], ALU.add))
                    link(v.tensor_tensor(G, G, one[0][:], ALU.mult))


def gated_rows_phase(nc, R, I, name, kind):
    E = 32 if kind == "proto" else 16
    BL = 4 if kind == "proto" else 9
    UNG = 0 if kind == "proto" else 1
    AR = 4 if kind == "proto" else 3
    TERMS = 96 // E
    K3 = TERMS * E
    with ExitStack() as stack:
        sb, ps, sem = allocator(nc, stack)
        n_ = lambda s: f"{name}_{s}"
        X = Experts(nc, R, sb, sem, name, E)
        UP = sb(n_("up"), [P, BL * P])
        DN = sb(n_("dn"), [P, BL, D])
        SEL = sb(n_("sel"), [K3, BL - UNG, P], BF16)
        loads = [(UP[:], I[n_("up")]), (DN[:], I[n_("down")]), (SEL[:], I[n_("sel")])]
        if kind == "proto":
            BI = sb(n_("bias"), [E, D])
            loads.append((BI[:], I[n_("bias")]))
        extra = {"rank": I[f"rank{E}"], "temp": I["temp"] if kind == "proto" else None}
        routing_part(nc, R, I, name, X, kind, I[n_("router")], loads, extra)

        g3 = sb(n_("g3"), [P, NB, TERMS, E], BF16)
        rest = sb(n_("rest"), [P, NB, E])
        GS = [sb(n_(f"gs{i}"), [P, GB, K3], BF16) for i in range(2)]
        G3T = [sb(n_(f"g3t{i}"), [K3, GT], BF16) for i in range(2)]
        if kind == "proto":
            GF = [sb(n_(f"gf{i}"), [P, GB, E]) for i in range(2)]
            GFT = [sb(n_(f"gft{i}"), [E, GT]) for i in range(2)]
        A = [sb(n_(f"a{i}"), [P, GT]) for i in range(2)]
        AG = [sb(n_(f"ag{i}"), [P, GT]) for i in range(AR)]
        PU = [ps(n_(f"pu{i}"), [P, 512]) for i in range(2)]
        PG = [ps(n_(f"pg{i}"), [P, 512]) for i in range(2)]
        PO = [ps(n_(f"po{i}"), [P, GB, D]) for i in range(2)]
        PT3 = ps(n_("pt3"), [K3, GT], BF16)
        PTF = ps(n_("ptf"), [E, GT]) if kind == "proto" else None
        names = ("split", "gs_ready", "gt_psum", "gt_ready", "up_ready", "ge_ready", "a_ready", "ag_ready", "ag0_ready",
                 "dn_ready", "x_added", "zeroed")
        Z = {s: sem(n_(s)) for s in names}
        func = ACT.Copy if kind == "proto" else ACT.Gelu
        GBL = BL - UNG

        with nc.Block() as block:
            @block.gpsimd
            def _(pool):
                pool.wait_ge(Z["split"], 5)
                if TERMS > 3:
                    pool.wait_ge(Z["zeroed"], 1)

                def stage(g, par):
                    at_least(pool, Z["gt_psum"], g - 1)
                    src = g3[:, bass.ds(g * GB, GB), :, :].rearrange("p b t e -> p b (t e)")
                    ins = nc.gpsimd.tensor_copy(GS[par][:], src)
                    if kind == "proto":
                        ins.then_inc(Z["gs_ready"], 1)
                        ins = nc.gpsimd.tensor_copy(GF[par][:], X.gates[:, bass.ds(g * GB, GB), :])
                    ins.then_inc(Z["gs_ready"], 1)

                def pair(g):
                    stage(g, 0)
                    stage(g + 1, 1)

                pairs_loop(pool, NG, pair)

            @block.vector
            def _(dve):
                v = nc.vector
                if TERMS > 3:
                    v.memset(g3[:, :, 3:TERMS, :], 0.0).then_inc(Z["zeroed"], 1)
                v.tensor_copy(g3[:, :, 0, :], X.gates[:]).then_inc(Z["split"], 1)
                dve.wait_ge(Z["split"], 1)
                v.tensor_tensor(rest[:], X.gates[:], g3[:, :, 0, :], ALU.subtract).then_inc(Z["split"], 1)
                dve.wait_ge(Z["split"], 2)
                v.tensor_copy(g3[:, :, 1, :], rest[:]).then_inc(Z["split"], 1)
                dve.wait_ge(Z["split"], 3)
                v.tensor_tensor(rest[:], rest[:], g3[:, :, 1, :], ALU.subtract).then_inc(Z["split"], 1)
                dve.wait_ge(Z["split"], 4)
                v.tensor_copy(g3[:, :, 2, :], rest[:]).then_inc(Z["split"], 1)

                def gate(g, c, par):
                    if c < UNG:
                        return
                    n = g * BL + c
                    gn = g * GBL + c - UNG
                    q = par * BL + c
                    dve.wait_ge(Z["a_ready"], gn + 1)
                    dve.wait_ge(Z["ge_ready"], gn + 1)
                    at_least(dve, Z["dn_ready"], n - AR + 1)
                    v.tensor_tensor(AG[q % AR][:], A[(par * GBL + c - UNG) % 2][:], PG[(par * GBL + c - UNG) % 2][:],
                                    ALU.mult).then_inc(Z["ag_ready"], 1)

                def group(g, par, first, last):
                    for c in range(BL):
                        gate(g, c, par)
                        if c == 2 and not first:
                            add(g - 1, 1 - par)
                    if last:
                        add(g, par)

                def add(g, par):
                    dve.wait_ge(Z["dn_ready"], g * BL + BL)
                    residual(nc, R, dve, Z["x_added"], g, PO[par][:], g + 1)

                groups_loop(dve, group, 3)

            @block.scalar
            def _(act):
                a = nc.scalar

                def gates_in(g, par):
                    act.wait_ge(Z["gt_psum"], g + 1)
                    ins = a.activation(G3T[par][:], PT3[:], ACT.Copy)
                    if kind == "proto":
                        ins.then_inc(Z["gt_ready"], 1)
                        ins = a.activation(GFT[par][:], PTF[:], ACT.Copy)
                    ins.then_inc(Z["gt_ready"], 1)

                def rows(g, c, par):
                    n = g * BL + c
                    q = par * BL + c
                    act.wait_ge(Z["up_ready"], n + 1)
                    if c < UNG:
                        at_least(act, Z["dn_ready"], n - AR + 1)
                        a.activation(AG[q % AR][:], PU[q % 2][:], func).then_inc(Z["ag0_ready"], 1)
                    else:
                        gn = g * GBL + c - UNG
                        at_least(act, Z["ag_ready"], gn - 1)
                        a.activation(A[(par * GBL + c - UNG) % 2][:], PU[q % 2][:], func).then_inc(Z["a_ready"], 1)

                def group(g, par, first, last):
                    for c in range(BL):
                        rows(g, c, par)
                        if c == 1 and not last:
                            gates_in(g + 1, 1 - par)

                gates_in(0, 0)
                groups_loop(act, group, 3)

            @block.tensor
            def _(pe):
                t = nc.tensor

                def gates_turn(g, par):
                    many = 2 if kind == "proto" else 1
                    pe.wait_ge(Z["gs_ready"], (g + 1) * many)
                    at_least(pe, Z["gt_ready"], g * many)
                    for j in range(GB):
                        last = t.transpose(PT3[:, j * P:(j + 1) * P], GS[par][:, j, :], R.ident_bf[:])
                    if kind == "proto":
                        for j in range(GB):
                            last = t.transpose(PTF[:, j * P:(j + 1) * P], GF[par][:, j, :], R.ident[:])
                    last.then_inc(Z["gt_psum"], 1)

                def up(g, c, par):
                    n = g * BL + c
                    q = par * BL + c
                    if UNG:
                        if c == 0:
                            at_least(pe, Z["a_ready"], g * GBL - 1)
                        elif c == 1:
                            at_least(pe, Z["a_ready"], g * GBL)
                        elif c == 2:
                            pe.wait_ge(Z["ag0_ready"], g + 1)
                        else:
                            at_least(pe, Z["a_ready"], g * GBL + c - 2)
                    else:
                        at_least(pe, Z["a_ready"], n - 1)
                    t.matmul(PU[q % 2][:], UP[:, c * P:(c + 1) * P], X.ht[:, bass.ds(g * GT, GT)], start=True,
                             stop=True).then_inc(Z["up_ready"], 1)
                    if c >= UNG:
                        gn = g * GBL + c - UNG
                        if c == UNG:
                            pe.wait_ge(Z["gt_ready"], (g + 1) * (2 if kind == "proto" else 1))
                        at_least(pe, Z["ag_ready"], gn - 1)
                        t.matmul(PG[(par * GBL + c - UNG) % 2][:], SEL[:, c - UNG, :], G3T[par][:], start=True,
                                 stop=True).then_inc(Z["ge_ready"], 1)

                def down(g, c, par):
                    q = par * BL + c
                    if c == 0:
                        at_least(pe, Z["x_added"], g - 1)
                    if c < UNG:
                        pe.wait_ge(Z["ag0_ready"], g + 1)
                    else:
                        pe.wait_ge(Z["ag_ready"], g * GBL + c - UNG + 1)
                    if c == 0 and kind == "proto":
                        for j in range(GB):
                            t.matmul(PO[par][:, j, :], GFT[par][:, j * P:(j + 1) * P], BI[:], start=(j == 0), stop=False,
                                     skip_group_check=True)
                    for j in range(GB):
                        last = t.matmul(PO[par][:, j, :], AG[q % AR][:, j * P:(j + 1) * P], DN[:, c, :],
                                        start=(c == 0 and j == 0 and kind != "proto"), stop=(c == BL - 1),
                                        skip_group_check=True)
                    last.then_inc(Z["dn_ready"], 1)

                def group(g, par, first, last):
                    for c in range(BL):
                        up(g, c, par)
                        if c >= 2:
                            down(g, c - 2, par)
                        elif not first:
                            down(g - 1, BL - 2 + c, 1 - par)
                        if c == 0 and not last:
                            gates_turn(g + 1, 1 - par)
                    if last:
                        down(g, BL - 2, par)
                        down(g, BL - 1, par)

                gates_turn(0, 0)
                groups_loop(pe, group, 3)


def three_passes(t, out, w_hi, w_lo, a_hi, a_lo, start=True, stop=True, before_lo=None):
    t.matmul(out, w_hi, a_hi, start=start, stop=False)
    t.matmul(out, w_lo, a_hi, start=False, stop=False)
    if before_lo is not None:
        before_lo()
    return t.matmul(out, w_hi, a_lo, start=False, stop=stop)


def gated_outputs_phase(nc, R, I, name, kind):
    E = 8
    HB = 4 if kind == "capacity" else 2
    N = E * HB
    two = kind == "swiglu"
    LAG = 3 if two else 2
    SUM_UNIT, TURN_UNIT, SPLIT_UNIT = 5, 8, 10
    ADDS = E - 1
    K3 = 96
    with ExitStack() as stack:
        sb, ps, sem = allocator(nc, stack)
        n_ = lambda s: f"{name}_{s}"
        X = Experts(nc, R, sb, sem, name, E)
        pieces = [("w1", N * P), ("wd", N * D)] + ([("w2", N * P)] if two else [])
        HI = {w: sb(n_(w + "hi"), [P, cols], F32R) for w, cols in pieces}
        LO = {w: sb(n_(w + "lo"), [P, cols], F32R) for w, cols in pieces}
        SEL = sb(n_("sel"), [K3, E, P], BF16)
        loads = [(SEL[:], I[n_("sel")])]
        if not two:
            B1, B2 = sb(n_("b1"), [P, N]), sb(n_("b2"), [P, E])
            loads += [(B1[:], I[n_("b1")]), (B2[:], I[n_("b2")])]
        extra = {"rank": I["rank8"], "cap": 2 * NB * P // E, "ln": (I["ln2_scale"], I["ln2_shift"]) if two else None}
        splits = [(I[n_(w)], HI[w], LO[w]) for w, _ in pieces]
        routing_part(nc, R, I, name, X, kind, I[n_("router")], loads, extra, splits)

        g3 = sb(n_("g3"), [P, NB, 3, E], BF16)
        rest = X.logits
        GS = [sb(n_(f"gs{i}"), [P, GB, K3]) for i in range(2)]
        G3T = [sb(n_(f"g3t{i}"), [K3, GT], BF16) for i in range(2)]
        XH = [sb(n_(f"xh{i}"), [P, GT], F32R) for i in range(2)]
        XL = [sb(n_(f"xl{i}"), [P, GT], F32R) for i in range(2)]
        A = [sb(n_(f"a{i}"), [P, GT]) for i in range(2)]
        AH = [sb(n_(f"ah{i}"), [P, GT], F32R) for i in range(4)]
        AL = [sb(n_(f"al{i}"), [P, GT], F32R) for i in range(4)]
        S = [sb(n_(f"s{i}"), [P, GT]) for i in range(2)] if two else None
        YG = [sb(n_(f"yg{i}"), [P, GT]) for i in range(2)]
        YA = [sb(n_(f"ya{i}"), [P, GT]) for i in range(2)]
        GX = [sb(n_(f"gx{i}"), [P, GT]) for i in range(2)]
        PU = [ps(n_(f"pu{i}"), [P, 512]) for i in range(2)]
        PV = [ps(n_(f"pv{i}"), [P, 512]) for i in range(2)] if two else None
        PY = [ps(n_(f"py{i}"), [P, GT]) for i in range(2)]
        PG = ps(n_("pg"), [P, GT])
        PT = ps(n_("pt"), [P, GB, D])
        Z = {s: sem(n_(s)) for s in ("split", "zeroed", "gs_ready", "gt_psum", "gt_ready", "xh_ready", "xl_ready",
                                     "up_ready", "s_ready", "a_ready", "hi_ready", "lo_ready", "dn_ready", "ge_ready",
                                     "gx_ready", "yg_ready", "ya_ready", "px_ready", "x_added")}

        def lagged(g, s, first, lag, f):
            if s >= lag:
                f(g, s - lag)
            elif not first:
                f(g - 1, N + s - lag)

        with nc.Block() as block:
            @block.gpsimd
            def _(pool):
                v = nc.gpsimd

                def stage(g, par):
                    at_least(pool, Z["gt_psum"], g - 1)
                    src = g3[:, bass.ds(g * GB, GB), :, :].rearrange("p b t e -> p b (t e)")
                    v.tensor_copy(GS[par][:, :, 0:3 * E], src).then_inc(Z["gs_ready"], 1)

                def group(g, par, first, last):
                    if not last:
                        stage(g + 1, 1 - par)
                    for e in range(1, E):
                        pool.wait_ge(Z["yg_ready"], g * E + e + 1)
                        if e == 1:
                            at_least(pool, Z["px_ready"], g - 1)
                            ins = v.tensor_tensor(YA[par][:], YG[0][:], YG[1][:], ALU.add)
                        else:
                            pool.wait_ge(Z["ya_ready"], g * ADDS + e - 1)
                            ins = v.tensor_tensor(YA[par][:], YA[par][:], YG[e % 2][:], ALU.add)
                        ins.then_inc(Z["ya_ready"], 1)

                for i in range(2):
                    v.memset(GS[i][:], 0.0).then_inc(Z["zeroed"], 1)
                pool.wait_ge(Z["zeroed"], 2)
                pool.wait_ge(Z["split"], 5)
                stage(0, 0)
                groups_loop(pool, group, 3)

            @block.vector
            def _(dve):
                v = nc.vector
                def split_inputs(g, par):
                    src = X.ht[:, bass.ds(g * GT, GT)]
                    at_least(dve, Z["up_ready"], (g - 1) * N)
                    v.tensor_copy(XH[par][:], src).then_inc(Z["xh_ready"], 1)
                    dve.wait_ge(Z["xh_ready"], g + 1)
                    v.tensor_tensor(XL[par][:], src, XH[par][:].bitcast(F32), ALU.subtract).then_inc(Z["xl_ready"], 1)

                def product(g, s):
                    n = g * N + s
                    dve.wait_ge(Z["s_ready"], n + 1)
                    dve.wait_ge(Z["up_ready"], n + 1)
                    at_least(dve, Z["lo_ready"], n - 1)
                    v.tensor_tensor(A[s % 2][:], S[s % 2][:], PV[s % 2][:], ALU.mult).then_inc(Z["a_ready"], 1)

                def high(g, s):
                    n = g * N + s
                    dve.wait_ge(Z["a_ready"], n + 1)
                    at_least(dve, Z["dn_ready"], n - 3)
                    v.tensor_copy(AH[s % 4][:], A[s % 2][:]).then_inc(Z["hi_ready"], 1)

                def low(g, s):
                    n = g * N + s
                    dve.wait_ge(Z["hi_ready"], n + 1)
                    at_least(dve, Z["dn_ready"], n - 3)
                    v.tensor_tensor(AL[s % 4][:], A[s % 2][:], AH[s % 4][:].bitcast(F32),
                                    ALU.subtract).then_inc(Z["lo_ready"], 1)

                def weigh(g, u):
                    if u % HB != HB - 1:
                        return
                    e = u // HB
                    dve.wait_ge(Z["gx_ready"], g * E + e + 1)
                    dve.wait_ge(Z["dn_ready"], g * N + u + 1)
                    at_least(dve, Z["ya_ready"], g * ADDS + (e - 1 if e < 2 else max(1, e - 2)))
                    if two:
                        ins = v.tensor_tensor(YG[e % 2][:], PY[e % 2][:], GX[e % 2][:], ALU.mult)
                    else:
                        ins = v.scalar_tensor_tensor(YG[e % 2][:], PY[e % 2][:], B2[:, e:e + 1], GX[e % 2][:], ALU.add, ALU.mult)
                    ins.then_inc(Z["yg_ready"], 1)

                def group(g, par, first, last):
                    for s in range(N):
                        if two:
                            product(g, s)
                            lagged(g, s, first, 1, low)
                        else:
                            high(g, s)
                            low(g, s)
                        lagged(g, s, first, LAG, weigh)
                        if s == SUM_UNIT and not first:
                            finish(g - 1)
                        if s == SPLIT_UNIT and not last:
                            split_inputs(g + 1, 1 - par)
                    if last:
                        if two:
                            low(g, N - 1)
                        for u in range(N - LAG, N):
                            weigh(g, u)
                        finish(g)

                def finish(g):
                    dve.wait_ge(Z["px_ready"], g + 1)
                    residual(nc, R, dve, Z["x_added"], g, PT[:], g + 1)

                split_inputs(0, 0)
                v.tensor_copy(g3[:, :, 0, :], X.gates[:]).then_inc(Z["split"], 1)
                dve.wait_ge(Z["split"], 1)
                v.tensor_tensor(rest[:], X.gates[:], g3[:, :, 0, :], ALU.subtract).then_inc(Z["split"], 1)
                dve.wait_ge(Z["split"], 2)
                v.tensor_copy(g3[:, :, 1, :], rest[:]).then_inc(Z["split"], 1)
                dve.wait_ge(Z["split"], 3)
                v.tensor_tensor(rest[:], rest[:], g3[:, :, 1, :], ALU.subtract).then_inc(Z["split"], 1)
                dve.wait_ge(Z["split"], 4)
                v.tensor_copy(g3[:, :, 2, :], rest[:]).then_inc(Z["split"], 1)
                groups_loop(dve, group)

            @block.scalar
            def _(act):
                a = nc.scalar

                def rows(g, s):
                    n = g * N + s
                    act.wait_ge(Z["up_ready"], n + 1)
                    if two:
                        at_least(act, Z["a_ready"], n - 1)
                        a.activation(S[s % 2][:], PU[s % 2][:], ACT.Silu).then_inc(Z["s_ready"], 1)
                    else:
                        at_least(act, Z["lo_ready"], n - 1)
                        a.activation(A[s % 2][:], PU[s % 2][:], ACT.Gelu, bias=B1[:, s:s + 1]).then_inc(Z["a_ready"], 1)

                def high(g, s):
                    n = g * N + s
                    act.wait_ge(Z["a_ready"], n + 1)
                    at_least(act, Z["dn_ready"], n - 3)
                    a.activation(AH[s % 4][:], A[s % 2][:], ACT.Copy).then_inc(Z["hi_ready"], 1)

                def gates_in(g, par):
                    act.wait_ge(Z["gt_psum"], g + 1)
                    at_least(act, Z["ge_ready"], (g - 1) * E)
                    a.activation(G3T[par][:], PT[0:K3, :, :].rearrange("p b t -> p (b t)"),
                                 ACT.Copy).then_inc(Z["gt_ready"], 1)

                def spread(g, u):
                    if u % HB != 0:
                        return
                    e = u // HB
                    act.wait_ge(Z["ge_ready"], g * E + e + 1)
                    at_least(act, Z["yg_ready"], g * E + e - 1)
                    a.activation(GX[e % 2][:], PG[:], ACT.Copy).then_inc(Z["gx_ready"], 1)

                def group(g, par, first, last):
                    for s in range(N):
                        rows(g, s)
                        if two:
                            lagged(g, s, first, 1, high)
                        lagged(g, s, first, LAG, spread)
                        if s == TURN_UNIT and not last:
                            gates_in(g + 1, 1 - par)
                    if last:
                        if two:
                            high(g, N - 1)
                        for u in range(N - LAG, N):
                            spread(g, u)

                gates_in(0, 0)
                groups_loop(act, group)

            @block.tensor
            def _(pe):
                t = nc.tensor

                def up(g, s, par):
                    n = g * N + s
                    at_least(pe, Z["a_ready"], n - 1)
                    if s == 0:
                        pe.wait_ge(Z["xh_ready"], g + 1)
                        pe.wait_ge(Z["xl_ready"], g + 1)
                    w = slice(s * P, (s + 1) * P)
                    last = three_passes(t, PU[s % 2][:], HI["w1"][:, w], LO["w1"][:, w], XH[par][:], XL[par][:])
                    if two:
                        last = three_passes(t, PV[s % 2][:], HI["w2"][:, w], LO["w2"][:, w], XH[par][:], XL[par][:])
                    last.then_inc(Z["up_ready"], 1)

                def down(g, s, par):
                    n = g * N + s
                    e, c = s // HB, s % HB
                    w = slice(s * D, (s + 1) * D)
                    pe.wait_ge(Z["hi_ready"], n + 1)
                    if c == 0:
                        at_least(pe, Z["yg_ready"], g * E + e - 1)
                        pe.wait_ge(Z["gt_ready"], g + 1)
                        at_least(pe, Z["gx_ready"], g * E + e)
                        t.matmul(PG[:], SEL[:, e, :], G3T[par][:], start=True, stop=True).then_inc(Z["ge_ready"], 1)
                    three_passes(t, PY[e % 2][:], HI["wd"][:, w], LO["wd"][:, w], AH[s % 4][:], AL[s % 4][:],
                                 start=(c == 0), stop=(c == HB - 1),
                                 before_lo=lambda: pe.wait_ge(Z["lo_ready"], n + 1)).then_inc(Z["dn_ready"], 1)

                def gates_turn(g, par):
                    pe.wait_ge(Z["gs_ready"], g + 1)
                    at_least(pe, Z["x_added"], g - 1)
                    for j in range(GB):
                        last = t.transpose(PT[0:K3, j, :], GS[par][:, j, :], R.ident[:])
                    last.then_inc(Z["gt_psum"], 1)

                def sums_turn(g, par, turned):
                    pe.wait_ge(Z["ya_ready"], (g + 1) * ADDS)
                    pe.wait_ge(Z["gt_ready"], turned)
                    for j in range(GB):
                        last = t.transpose(PT[:, j, :], YA[par][:, j * P:(j + 1) * P], R.ident[:])
                    last.then_inc(Z["px_ready"], 1)

                def group(g, par, first, last):
                    for s in range(N):
                        up(g, s, par)
                        if s >= LAG:
                            down(g, s - LAG, par)
                        elif not first:
                            down(g - 1, N + s - LAG, 1 - par)
                        if s == SUM_UNIT and not first:
                            sums_turn(g - 1, 1 - par, g + 1)
                        if s == TURN_UNIT and not last:
                            gates_turn(g + 1, 1 - par)
                    if last:
                        for u in range(N - LAG, N):
                            down(g, u, par)
                        sums_turn(g, par, g + 1)

                gates_turn(0, 0)
                groups_loop(pe, group)


def store_phase(nc, R, I, out):
    with ExitStack() as stack:
        sb, ps, sem = allocator(nc, stack)
        stored, summed = sem("stored"), sem("summed")
        view = out.rearrange("b t d -> t b d")
        parts = [slice(i * NB // PARTS, (i + 1) * NB // PARTS) for i in range(PARTS)]
        if R.kept:
            kept = [sb(f"kept_x{i}", [P, NB // PARTS, D]) for i in range(PARTS)]
            back = [sem(f"kept_back{i}") for i in range(PARTS)]
        with nc.Block() as block:
            @block.vector
            def _(dve):
                if R.kept:
                    for i, q in enumerate(parts):
                        dve.wait_ge(back[i], 16)
                        nc.vector.tensor_tensor(R.x[:, q, :], R.x[:, q, :], kept[i][:], ALU.add).then_inc(summed, 1)

            @block.sync
            def _(sp):
                if R.kept:
                    for i, q in enumerate(parts):
                        sp.dma_start(kept[i][:], view[:, q, :]).then_inc(back[i], 16)
                for i, q in enumerate(parts):
                    if R.kept:
                        sp.wait_ge(summed, i + 1)
                    sp.dma_start(view[:, q, :], R.x[:, q, :]).then_inc(stored, 16)
                sp.wait_ge(stored, 16 * PARTS)


def build(nc, I, out, only=None):
    with ExitStack() as stack:
        sb, ps, sem = allocator(nc, stack)
        R = Namespace()
        R.x = sb("x", [P, NB, D])
        R.stats = sb("stats", [P, NB, 6])
        R.ident = sb("ident", [P, P])
        R.ident_bf = sb("ident_bf", [P, P], BF16)
        R.ones = sb("ones", [P, P])
        R.ones_bf = sb("ones_bf", [P, P], BF16)
        R.stats_done = sem("stats_done")
        R.kept = False
        load_phase(nc, R, I)
        phases = [
            lambda: attention_phase(nc, R, I, "a0", I["L0_xattn_Wq"], I["L0_xattn_Wk"], I["L0_xattn_Wv"], I["L0_xattn_Wo"],
                                    I["L0_xattn_bq"], I["L0_xattn_bk"], I["L0_xattn_bv"], I["L0_xattn_bo"], hepos=True, pad=I["pad"]),
            lambda: gated_rows_phase(nc, R, I, "f0", "proto"),
            lambda: attention_phase(nc, R, I, "a1", I["L1_xattn_wq"], I["L1_xattn_wk"], I["L1_xattn_wv"], I["L1_xattn_wo"],
                                    I["L1_xattn_bq"], I["L1_xattn_bk"], I["L1_xattn_bv"], I["L1_xattn_bo"]),
            lambda: gated_rows_phase(nc, R, I, "f1", "shared"),
            lambda: attention_phase(nc, R, I, "a2", I["L2_xattn_W_q"], I["L2_xattn_W_k"], I["L2_xattn_W_v"], I["L2_xattn_W_o"],
                                    I["L2_xattn_b_q"], I["L2_xattn_b_k"], I["L2_xattn_b_v"], I["L2_xattn_b_o"], mask=I["mask"]),
            lambda: gated_outputs_phase(nc, R, I, "f2", "capacity"),
            lambda: attention_phase(nc, R, I, "a3", I["L3_xattn_Wq"], I["L3_xattn_Wk"], I["L3_xattn_Wv"], I["L3_xattn_Wo"],
                                    causal=I["causal_ctx"]),
            lambda: renorm_phase(nc, R, out),
            lambda: attention_phase(nc, R, I, "s3", I["L3_ffn_wq"], I["L3_ffn_wk"], I["L3_ffn_wv"], I["L3_ffn_wo"],
                                    bo=I["L3_ffn_bo"], own_keys=True, causal=I["causal_own"],
                                    ln=(I["L3_ffn_ln1_scale"], I["L3_ffn_ln1_shift"])),
            lambda: gated_outputs_phase(nc, R, I, "f3", "swiglu"),
        ]
        chosen = range(len(phases)) if only is None else only
        for i in chosen:
            phases[i]()
        store_phase(nc, R, I, out)


def laid_out(inputs):
    a = {k: np.asarray(v) for k, v in inputs.items()}
    c = np.ascontiguousarray
    order = np.arange(KC).reshape(KCLS, STRIDE).T.reshape(-1)
    r = {
        "x": c(a["x"].transpose(1, 0, 2)),
        "ctxT": c(a["ctx_1024"][:, order, :].transpose(2, 0, 1)),
        "pad": c(a["mask_BxS2_bf0"][:, order].reshape(1, -1)),
        "mask": c(a["mask_1x1xSxS2_ik0"][0, 0][:, order]),
        "temp": a["L0_ffn_temp"].reshape(1, 1),
        "ln2_scale": a["L3_ffn_ln2_scale"], "ln2_shift": a["L3_ffn_ln2_shift"],
    }
    for n in ("Wq", "bq", "Wk", "bk", "Wv", "bv", "Wo", "bo"):
        r[f"L0_xattn_{n}"] = a[f"L0_xattn_{n}"]
        if n[0] == "W":
            r[f"L3_xattn_{n}"] = c(a[f"L3_xattn_{n}"].T)
    for n in ("q", "k", "v", "o"):
        r[f"L1_xattn_w{n}"] = c(a[f"L1_xattn_w{n}"].T)
        r[f"L1_xattn_b{n}"] = a[f"L1_xattn_b{n}"]
        r[f"L2_xattn_W_{n}"] = a[f"L2_xattn_W_{n}"]
        r[f"L2_xattn_b_{n}"] = a[f"L2_xattn_b_{n}"]
        r[f"L3_ffn_w{n}"] = a[f"L3_ffn_w{n}"]
    for n in ("bo", "ln1_scale", "ln1_shift"):
        r[f"L3_ffn_{n}"] = a[f"L3_ffn_{n}"]
    unit_order = np.arange(D).reshape(4, 4, HD).transpose(1, 0, 2).reshape(-1)
    for n in ("L1_xattn_wq", "L1_xattn_wk", "L1_xattn_bq", "L1_xattn_bk", "L2_xattn_W_q", "L2_xattn_W_k",
              "L2_xattn_b_q", "L2_xattn_b_k", "L3_xattn_Wq", "L3_xattn_Wk", "L3_ffn_wq", "L3_ffn_wk"):
        r[n] = c(r[n][..., unit_order])

    def blocks(w):
        return c(w.reshape(-1, P, D).transpose(1, 0, 2))

    r["f0_router"] = c(a["L0_ffn_prototypes"].T)
    r["f0_up"] = c(a["L0_ffn_B"].reshape(-1, D).T)
    r["f0_down"] = blocks(a["L0_ffn_A"].transpose(0, 2, 1).reshape(-1, D))
    r["f0_bias"] = a["L0_ffn_bias"]
    r["f1_router"] = c(a["L1_ffn_router_w"].T)
    up = np.concatenate([a["L1_ffn_shared_up"], a["L1_ffn_routed_up"]])
    down = np.concatenate([a["L1_ffn_shared_down"], a["L1_ffn_routed_down"]])
    r["f1_up"] = c(up.reshape(-1, D).T)
    r["f1_down"] = blocks(down.transpose(0, 2, 1).reshape(-1, D))
    r["f2_router"] = a["L2_ffn_wg"]
    r["f2_w1"] = c(a["L2_ffn_w1"].transpose(1, 0, 2).reshape(D, -1))
    r["f2_wd"] = c(blocks(a["L2_ffn_w2"].reshape(-1, D)).reshape(P, -1))
    r["f2_b1"] = c(a["L2_ffn_b1"].reshape(-1, P).T)
    r["f2_b2"] = c(a["L2_ffn_b2"].T)
    r["f3_router"] = a["L3_ffn_gate_w"]
    for n in ("w1", "w2"):
        r[f"f3_{n}"] = c(a[f"L3_ffn_{n}"].transpose(1, 0, 2).reshape(D, -1))
    r["f3_wd"] = c(blocks(a["L3_ffn_w3"].reshape(-1, D)).reshape(P, -1))

    bf = mybir.dt.np(BF16)
    place = np.arange(P)
    r["ident"] = np.eye(P, dtype=np.float32)
    r["ident_bf"] = np.eye(P).astype(bf)
    r["tri"] = (place[:, None] <= place[None, :]).astype(bf)
    r["slots"] = (np.arange(96)[:, None] % 32 // HD == np.arange(4)[None, :]).astype(np.float32)
    r["classes"] = (np.arange(KC)[:, None] // KCLS == np.arange(32)[None, :] // HD).astype(np.float32)
    r["causal_ctx"] = np.where(order[None, :] > place[:, None], FAR, 0).astype(bf)
    r["causal_own"] = np.where(place[None, :] > place[:, None], FAR, 0).astype(bf)
    for e in (8, 16, 32):
        r[f"rank{e}"] = (e - np.arange(e, dtype=np.float32)).reshape(1, e)
    for n, e, blocks_, rows in (("f0", 32, 4, 16), ("f1", 16, 8, 64), ("f2", 8, 8, P), ("f3", 8, 8, P)):
        owner = np.arange(blocks_ * P).reshape(blocks_, P) // rows
        term = np.tile(np.arange(e), 3)
        term = np.concatenate([term, np.full(96 - 3 * e, -1)])
        r[f"{n}_sel"] = (term[:, None, None] == owner[None]).astype(bf)
    return r


def kernel(**inputs):
    import concourse.bacc as bacc
    from concourse.bass_utils import run_bass_kernel_spmd

    nc = bacc.Bacc("TRN2", target_bir_lowering=False, num_devices=1)
    arrays, I = {}, {}
    for name, a in laid_out(inputs).items():
        arrays["in_" + name] = a
        I[name] = nc.dram_tensor("in_" + name, a.shape, mybir.dt.from_np(a.dtype), kind="ExternalInput").ap()
    out = nc.dram_tensor("out_x", (NB, P, D), F32, kind="ExternalOutput").ap()
    build(nc, I, out)
    result = run_bass_kernel_spmd(nc, [arrays], core_ids=[0])
    return result.results[0]["out_x"]
```

```python
from contextlib import ExitStack

import concourse.bass as bass
import numpy as np
from concourse import mybir

F32 = mybir.dt.float32
BF16 = mybir.dt.bfloat16
F32R = mybir.dt.float32r
U8 = mybir.dt.uint8
I32 = mybir.dt.int32
ALU = mybir.AluOpType
ACT = mybir.ActivationFunctionType
AX = mybir.AxisListType

P = 128
D = 128
NB = 64
GB = 4
NG = NB // GB
GT = GB * P
NH = 16
HD = D // NH
KC = 120
STRIDE = 4
KCLS = KC // STRIDE
PARTS = 8
EPS = 1e-5
SCALE = float(HD) ** -0.5
FAR = -1.0e30


def at_least(eng, sem, value):
    if isinstance(value, int) and value <= 0:
        return
    eng.wait_ge(sem, value)


class Namespace:
    pass


def allocator(nc, stack):
    numbers = []

    def zero_semaphores():
        numbers.sort()
        runs = []
        for n in numbers:
            if runs and runs[-1].stop == n:
                runs[-1] = range(runs[-1].start, n + 1)
            else:
                runs.append(range(n, n + 1))
        for run in runs:
            nc.gpsimd.sem_clear(run)
        nc.all_engine_barrier()

    stack.callback(zero_semaphores)

    def sb(name, shape, dt=F32):
        return stack.enter_context(nc.sbuf_tensor(name, shape, dt))

    def ps(name, shape, dt=F32):
        return stack.enter_context(nc.psum_tensor(name, shape, dt))

    def sem(name):
        handle = stack.enter_context(nc.semaphore(name))
        numbers.append(handle.num)
        return handle

    return sb, ps, sem


def groups_loop(eng, body, peel=1):
    for g in range(peel):
        body(g, g % 2, g == 0, False)
    with eng.Fori(peel, NG - 2, 2) as g:
        body(g, 1, False, False)
        body(g + 1, 0, False, False)
    body(NG - 1, 1, False, True)


def pairs_loop(eng, end, body):
    body(0)
    with eng.Fori(2, end - 1, 2) as g:
        body(g)


class Norm:

    def __init__(self, nc, R, sb, sem, name):
        self.nc, self.R = nc, R
        self.mean = sb(name + "_mean", [P, NB])
        self.rstd = sb(name + "_rstd", [P, NB])
        self.work = sb(name + "_work", [P, 4, NB])
        self.steps = sem(name + "_norm_steps")
        self.var_ready = sem(name + "_var_ready")
        self.std_ready = sem(name + "_std_ready")

    def vector(self, dve):
        s = self.R.stats
        w = self.work
        v = self.nc.vector
        v.tensor_tensor(w[:, 0, :], s[:, :, 1], s[:, :, 4], ALU.add).then_inc(self.steps, 1)
        v.tensor_tensor(w[:, 1, :], s[:, :, 1], s[:, :, 4], ALU.subtract).then_inc(self.steps, 1)
        v.tensor_tensor(w[:, 2, :], s[:, :, 2], s[:, :, 5], ALU.add).then_inc(self.steps, 1)
        dve.wait_ge(self.steps, 3)
        v.tensor_scalar(self.mean[:], w[:, 0, :], 0.5, None, ALU.mult).then_inc(self.steps, 1)
        v.tensor_tensor(w[:, 3, :], w[:, 1, :], w[:, 1, :], ALU.mult).then_inc(self.steps, 1)
        dve.wait_ge(self.steps, 5)
        v.scalar_tensor_tensor(w[:, 0, :], w[:, 3, :], D / 4.0, w[:, 2, :], ALU.mult, ALU.add).then_inc(self.steps, 1)
        dve.wait_ge(self.steps, 6)
        v.tensor_scalar(w[:, 1, :], w[:, 0, :], 1.0 / D, EPS, ALU.mult, ALU.add).then_inc(self.var_ready, 1)
        dve.wait_ge(self.std_ready, 1)
        v.reciprocal(self.rstd[:], w[:, 2, :]).then_inc(self.steps, 1)
        dve.wait_ge(self.steps, 7)

    def scalar(self, act):
        act.wait_ge(self.var_ready, 1)
        self.nc.scalar.activation(self.work[:, 2, :], self.work[:, 1, :], ACT.Sqrt).then_inc(self.std_ready, 1)

    def apply(self, dve, g, h):
        for j in range(GB):
            b = g * GB + j
            last = self.nc.vector.tensor_scalar(h[:, j, :], self.R.x[:, b, :],
                                                self.mean[:, bass.ds(b, 1)], self.rstd[:, bass.ds(b, 1)],
                                                ALU.subtract, ALU.mult)
        return last

    def apply_one(self, dve, g, j, h):
        b = g * GB + j
        return self.nc.vector.tensor_scalar(h[:, j, :], self.R.x[:, b, :], self.mean[:, bass.ds(b, 1)],
                                            self.rstd[:, bass.ds(b, 1)], ALU.subtract, ALU.mult)


def residual(nc, R, dve, sem, g, out, done):
    xg = R.x[:, bass.ds(g * GB, GB), :]
    nc.vector.tensor_tensor(xg, xg, out, ALU.add).then_inc(sem, 1)
    dve.wait_ge(sem, done)
    for j in range(GB):
        b = g * GB + j
        nc.vector.bn_stats(R.stats[:, b, :], R.x[:, b, :]).then_inc(R.stats_done, 1)


def load_phase(nc, R, I):
    with ExitStack() as stack:
        sb, ps, sem = allocator(nc, stack)
        x_in = [sem(f"load_x{i}") for i in range(4)]
        const_in = sem("load_const")
        with nc.Block() as block:
            @block.sync
            def _(sp):
                for i in range(4):
                    q = slice(i * NB // 4, (i + 1) * NB // 4)
                    sp.dma_start(R.x[:, q, :], I["x"][:, q, :]).then_inc(x_in[i], 16)
                sp.dma_start(R.ident[:], I["ident"]).then_inc(const_in, 16)
                sp.dma_start(R.ident_bf[:], I["ident_bf"]).then_inc(const_in, 16)
                sp.wait_ge(const_in, 32)

            @block.vector
            def _(dve):
                nc.vector.memset(R.ones[:], 1.0)
                nc.vector.memset(R.ones_bf[:], 1.0)
                for b in range(NB):
                    if b % (NB // 4) == 0:
                        dve.wait_ge(x_in[b // (NB // 4)], 16)
                    nc.vector.bn_stats(R.stats[:, b, :], R.x[:, b, :]).then_inc(R.stats_done, 1)


def renorm_phase(nc, R, out):
    view = out.rearrange("b t d -> t b d")
    with ExitStack() as stack:
        sb, ps, sem = allocator(nc, stack)
        norm = Norm(nc, R, sb, sem, "renorm")
        shift = sb("renorm_shift", [P, NB])
        y_ready, shift_ready = sem("y_ready"), sem("shift_ready")
        kept = [sem(f"kept{i}") for i in range(PARTS)]
        with nc.Block() as block:
            @block.sync
            def _(sp):
                for i in range(PARTS):
                    q = slice(i * NB // PARTS, (i + 1) * NB // PARTS)
                    sp.dma_start(view[:, q, :], R.x[:, q, :]).then_inc(kept[i], 16)
                for i in range(PARTS):
                    sp.wait_ge(kept[i], 16)

            @block.scalar
            def _(act):
                norm.scalar(act)
                act.wait_ge(shift_ready, 1)
                for i in range(PARTS):
                    act.wait_ge(kept[i], 16)
                    for b in range(i * NB // PARTS, (i + 1) * NB // PARTS):
                        nc.scalar.activation(R.x[:, b, :], R.x[:, b, :], ACT.Identity, scale=norm.rstd[:, b:b + 1],
                                             bias=shift[:, b:b + 1]).then_inc(y_ready, 1)

            @block.vector
            def _(dve):
                norm.vector(dve)
                nc.vector.scalar_tensor_tensor(shift[:], norm.mean[:], -1.0, norm.rstd[:], ALU.mult,
                                               ALU.mult).then_inc(shift_ready, 1)
                for b in range(NB):
                    dve.wait_ge(y_ready, b + 1)
                    nc.vector.bn_stats(R.stats[:, b, :], R.x[:, b, :]).then_inc(R.stats_done, 1)


def attention_phase(nc, R, I, name, wq, wk, wv, wo, bq=None, bk=None, bv=None, bo=None, hepos=False,
                    own_keys=False, mask=None, causal=None, pad=None, ln=None):
    packed = not hepos
    TR = 3 * 32
    LN_SLOTS = (0, 0, 0, 0) if own_keys else (1, 1, 2, 2)
    SUM_SLOT, STATS_SLOTS = 7, (10, 11, 14, 15)
    TURN, VALUES, RECIP, OUTPUT = (2, 4, 5, 7) if packed else (2, 3, 3, 4)
    TAKE_SLOT = 12
    KN = P if own_keys else KC
    U = 1 if hepos else 4
    S = GB * U
    W = 4 * KN
    steps_of = ["ht", "k", "q", "v"] if own_keys else ["k", "ht", "q", "v"]
    slot_of = dict(zip(steps_of, (0, 1, 2, 3) if U == 1 else (0, 4, 8 if mask is not None else 7, 13) if not own_keys else (1, 4, 8, 13)))
    with ExitStack() as stack:
        sb, ps, sem = allocator(nc, stack)
        n_ = lambda s: f"{name}_{s}"
        norm = Norm(nc, R, sb, sem, name)
        Wq, Wk, Wv, Wo = (sb(n_(s), [P, D]) for s in ("wq", "wk", "wv", "wo"))
        cols = sb(n_("cols"), [P, 6])
        bvb = sb(n_("bv"), [P, GB * D]) if bv is not None else None
        if bo is not None:
            bor = sb(n_("bo"), [1, D])
            bo_terms = sb(n_("bo_terms"), [1, 3, D], BF16)
            bo3 = sb(n_("bo3"), [P, D], BF16)
        H = sb(n_("h"), [P, GB, D])
        HT = [sb(n_(f"ht{i}"), [P, GT]) for i in range(2)]
        QT = [sb(n_(f"qt{i}"), [P, GT]) for i in range(1 if packed else 2)]
        KT = [sb(n_(f"kt{i}"), [P, GB, KN]) for i in range(1 if packed else 2)]
        if packed:
            HIGH = {"k": sb(n_("kh"), [P, GB * KN], F32R), "q": sb(n_("qh"), [P, GT], F32R)}
            LOW = {"k": sb(n_("kl"), [P, GB * KN], F32R), "q": sb(n_("ql"), [P, GT], F32R)}
            K3 = sb(n_("k3"), [TR, 4, GB, KN])
            Q3 = sb(n_("q3"), [TR, 4, GT])
            QR = [sb(n_(f"qr{i}"), [TR, 4, GT], F32R) for i in range(2)]
        CTX = [sb(n_(f"ctx{i}"), [P, GB, KN]) for i in range(2)] if not own_keys else None
        slots = sb(n_("slots"), [TR, 4] if packed else [P, 4, STRIDE])
        KM = [sb(n_(f"km{i}"), [TR, 4, GB, W], F32R) if packed else sb(n_(f"km{i}"), [P, GB, U, W]) for i in range(2)]
        VW = D if hepos else NH * 32
        VM = [sb(n_(f"vm{i}"), [P, GB, VW]) for i in range(2)]
        DM = sb(n_("dm"), [P, 4, 32])
        PR = [sb(n_(f"p{i}"), [P, W]) for i in range(4)]
        PT = [sb(n_(f"pt{i}"), [P, 4 * P]) for i in range(4)]
        MX = [sb(n_(f"mx{i}"), [P, 16 if hepos else 4]) for i in range(2)]
        RD = sb(n_("rd"), [P, P])
        CT = [sb(n_(f"ct{i}"), [P, P]) for i in range(2)]
        SC = [ps(n_(f"sc{i}"), [P, 512]) for i in range(2)]
        TP = [ps(n_(f"tp{i}"), [P, 512]) for i in range(2)]
        PJ = ps(n_("pj"), [P, 512])
        ND = [ps(n_(f"nd{i}"), [P, 4, P]) for i in range(2)]
        OUT = ps(n_("out"), [P, GB, D])
        if pad is not None:
            padu = sb(n_("padu"), [1, NB * KC], U8)
            padb = sb(n_("padb"), [1, NB, KC], BF16)
        if mask is not None:
            mski = sb(n_("mski"), [P, KC], I32)
            keep = sb(n_("keep"), [P, KC])
            some = sb(n_("some"), [P, 1])
            diag = sb(n_("diag"), [P, P], BF16)
            qfac = sb(n_("qfac"), [P, P])
        if mask is not None or causal is not None:
            addm = sb(n_("addm"), [P, KN], BF16)

        v_biased = sem(n_("v_biased"))
        weights_in = sem(n_("weights_in"))
        bo_split, bo3_zero, bo3_in = (sem(n_(s)) for s in ("bo_split", "bo3_zero", "bo3_in"))
        keys_first_in = sem(n_("keys_first_in"))
        prep = sem(n_("prep"))
        prep_pool = sem(n_("prep_pool"))
        f_psum = sem(n_("f_psum"))
        ctx_in = [sem(n_(f"ctx_in{i}")) for i in range(2)]
        h_ready, h_used = sem(n_("h_ready")), sem(n_("h_used"))
        psum_done = {s: sem(n_(f"{s}_psum")) for s in steps_of}
        ready = {s: sem(n_(f"{s}_ready")) for s in steps_of}
        km_ready = [sem(n_(f"km_ready{i}")) for i in range(4)]
        if packed:
            high_ready = {s: sem(n_(f"{s}_high_ready")) for s in "kq"}
            low_ready = {s: sem(n_(f"{s}_low_ready")) for s in "kq"}
            k3_in = [sem(n_(f"k3_in{i}")) for i in range(4)]
            q3_in = [sem(n_(f"q3_in{i}")) for i in range(4)]
            qr_ready = [sem(n_(f"qr_ready{i}")) for i in range(4)]
        sc_ready, mx_ready, sub_ready, exp_ready = (sem(n_(s)) for s in ("sc_ready", "mx_ready", "sub_ready", "exp_ready"))
        tp_ready, pt_ready, pv_done = (sem(n_(s)) for s in ("tp_ready", "pt_ready", "pv_done"))
        rd_ready, ct_ready, o_done, x_added = (sem(n_(s)) for s in ("rd_ready", "ct_ready", "o_done", "x_added"))

        n_first = 2 + (bk is not None)
        n_weights = 3 + sum(a is not None for a in (bq, bo, mask, causal, pad)) + (GB if bv is not None else 0)
        n_weights += 2 * (ln is not None) + hepos
        n_prep = (bq is not None) + (pad is not None) + (5 if mask is not None else 0)

        def class_keys(pool, g, par):
            pool.wait_ge(ready["k"], g + 1)
            at_least(pool, sc_ready, (g - 1) * S)
            for j in range(4):
                nc.gpsimd.tensor_tensor(
                    KM[par][:, :, 0, j * KC:(j + 1) * KC].rearrange("p b (c k) -> p b c k", k=KCLS),
                    KT[par][:].rearrange("p b (c k) -> p b c k", k=KCLS),
                    slots[:, j, :].unsqueeze(1).unsqueeze(3).to_broadcast([P, GB, STRIDE, KCLS]),
                    ALU.mult).then_inc(km_ready[j], 1)

        def masked_keys(eng, v, g, par, units):
            at_least(eng, sc_ready, (g - 1) * S)
            for i in units:
                eng.wait_ge(k3_in[i], 48 * (g + 1))
                v.tensor_tensor(KM[par][:, i, :, :].rearrange("p b (j k) -> p b j k", k=KN),
                                K3[:, i, :, :].unsqueeze(2).to_broadcast([TR, GB, 4, KN]),
                                slots[:].unsqueeze(1).unsqueeze(3).to_broadcast([TR, GB, 4, KN]),
                                ALU.mult).then_inc(km_ready[i], 1)

        def diagonal(vm):
            a = vm[0:KN, :, :]
            return bass.AP(a.tensor, a.offset, [list(a.ap[0]), [128, GB * 4], [40, 4], [1, 8]])

        with nc.Block() as block:
            @block.sync
            def _(sp):
                def ctx_load(g, par):
                    at_least(sp, psum_done["v"], g - 1)
                    sp.dma_start(CTX[par][:], I["ctxT"][:, bass.ds(g * GB, GB), :]).then_inc(ctx_in[par], 16)

                sp.dma_start(Wk[:], wk).then_inc(keys_first_in, 16)
                if bk is not None:
                    sp.dma_start(cols[:, 1:2], bk.rearrange("(p a) -> p a", a=1)).then_inc(keys_first_in, 16)
                sp.dma_start(slots[:], I["slots" if packed else "slot_classes"]).then_inc(keys_first_in, 16)
                if not own_keys:
                    ctx_load(0, 0)
                for t, w in ((Wq, wq), (Wv, wv), (Wo, wo)):
                    sp.dma_start(t[:], w).then_inc(weights_in, 16)
                for c, v in ((0, bq),) + (((3, ln[0]), (4, ln[1])) if ln else ()):
                    if v is not None:
                        sp.dma_start(cols[:, c:c + 1], v.rearrange("(p a) -> p a", a=1)).then_inc(weights_in, 16)
                if bv is not None:
                    for j in range(GB):
                        sp.dma_start(bvb[:, j * D:(j + 1) * D],
                                     v_broadcast(bv)).then_inc(weights_in, 16)
                if bo is not None:
                    sp.dma_start(bor[:], bo.rearrange("(a p) -> a p", a=1)).then_inc(weights_in, 16)
                if mask is not None:
                    sp.dma_start(mski[:], mask).then_inc(weights_in, 16)
                if causal is not None:
                    sp.dma_start(addm[:], causal).then_inc(weights_in, 16)
                if pad is not None:
                    sp.dma_start(padu[:], pad).then_inc(weights_in, 16)
                if hepos:
                    sp.dma_start(DM[0:KC, 0, :], I["classes"]).then_inc(weights_in, 16)

                def stack_terms(g, par):
                    sp.wait_ge(low_ready["k"], g + 1)
                    for i in range(4):
                        at_least(sp, km_ready[i], g)
                        for term, part in enumerate((HIGH, LOW, HIGH)):
                            sp.dma_start(K3[32 * term:32 * term + 32, i, :, :].rearrange("p b k -> p (b k)"),
                                         part["k"][32 * i:32 * i + 32, :].bitcast(F32)).then_inc(k3_in[i], 16)
                    sp.wait_ge(low_ready["q"], g + 1)
                    for i in range(4):
                        at_least(sp, qr_ready[i], g)
                        for term, part in enumerate((HIGH, HIGH, LOW)):
                            sp.dma_start(Q3[32 * term:32 * term + 32, i, :],
                                         part["q"][32 * i:32 * i + 32, :].bitcast(F32)).then_inc(q3_in[i], 16)

                if bo is not None:
                    sp.wait_ge(bo_split, 5)
                    sp.wait_ge(bo3_zero, 1)
                    for i in range(3):
                        sp.dma_start(bo3[i:i + 1, :], bo_terms[:, i, :]).then_inc(bo3_in, 16)
                if own_keys:
                    groups_loop(sp, lambda g, par, first, last: stack_terms(g, par), 3)
                    return
                ctx_load(1, 1)
                if hepos:
                    def pair(g):
                        ctx_load(g + 2, 0)
                        ctx_load(g + 3, 1)

                    pairs_loop(sp, NG - 2, pair)
                    return
                stack_terms(0, 0)

                def pair(g):
                    ctx_load(g + 2, 0)
                    stack_terms(g + 1, 1)
                    ctx_load(g + 3, 1)
                    stack_terms(g + 2, 0)

                pairs_loop(sp, NG - 2, pair)
                stack_terms(NG - 1, 1)

            @block.gpsimd
            def _(pool):
                if bo is not None:
                    nc.gpsimd.memset(bo3[:], 0.0).then_inc(bo3_zero, 1)
                for t in VM:
                    nc.gpsimd.memset(t[:], 0.0).then_inc(prep_pool, 1)
                if hepos:
                    pool.wait_ge(keys_first_in, 16 * n_first)
                    class_keys(pool, 0, 0)
                    groups_loop(pool, lambda g, par, first, last: None if last else class_keys(pool, g + 1, 1 - par))
                    return
                nc.gpsimd.memset(DM[:], 0.0).then_inc(prep_pool, 1)
                pool.wait_ge(prep_pool, 3)
                for i in range(4):
                    nc.gpsimd.memset(DM[:, i, 8 * i:8 * i + 8], 1.0).then_inc(prep_pool, 1)
                pool.wait_ge(keys_first_in, 16 * n_first)

                def low_part(step, g):
                    src = QT[0][:] if step == "q" else KT[0][:].rearrange("p b k -> p (b k)")
                    for i in range(4):
                        at_least(pool, (k3_in if step == "k" else q3_in)[i], 48 * g)
                    pool.wait_ge(high_ready[step], g + 1)
                    nc.gpsimd.tensor_tensor(LOW[step][:], src, HIGH[step][:].bitcast(F32),
                                            ALU.subtract).then_inc(low_ready[step], 1)

                def prepare(g, par, others=(1, 2, 3)):
                    low_part("k", g)
                    masked_keys(pool, nc.gpsimd, g, par, (0,))
                    low_part("q", g)
                    masked_keys(pool, nc.gpsimd, g, par, others)

                def group(g, par, first, last):
                    if not last:
                        prepare(g + 1, 1 - par)

                prepare(0, 0, (2,))
                groups_loop(pool, group)

            @block.vector
            def _(dve):
                v = nc.vector
                norm.vector(dve)
                dve.wait_ge(weights_in, 16 * n_weights)
                done = 0
                if bq is not None:
                    v.tensor_scalar(cols[:, 2:3], cols[:, 0:1], SCALE, None, ALU.mult).then_inc(prep, 1)
                    done += 1
                if pad is not None:
                    v.tensor_scalar(padb[0:1, :, :], padu[0:1, :].rearrange("p (b k) -> p b k", k=KC), FAR, None,
                                    ALU.mult).then_inc(prep, 1)
                    done += 1
                if mask is not None:
                    v.tensor_scalar(keep[:], mski[:], 0.0, None, ALU.not_equal).then_inc(prep, 1)
                    v.tensor_scalar(addm[:], mski[:], 0.0, -1.0e9, ALU.is_equal, ALU.mult).then_inc(prep, 1)
                    done += 2
                    dve.wait_ge(prep, done)
                    v.tensor_reduce(some[:], keep[:], AX.X, ALU.max).then_inc(prep, 1)
                    dve.wait_ge(prep, done + 1)
                    v.tensor_scalar(diag[:], R.ident[:], some[:, 0:1], None, ALU.mult).then_inc(prep, 1)
                    dve.wait_ge(f_psum, 1)
                    v.tensor_scalar(qfac[:], OUT[:, 0, :], SCALE, None, ALU.mult).then_inc(prep, 1)
                    done += 3
                    dve.wait_ge(prep, done)

                def ln_group(g):
                    at_least(dve, psum_done["ht"], g)
                    norm.apply(dve, g, H).then_inc(h_ready, 1)

                def ln_sequence(g, j):
                    at_least(dve, psum_done["ht"], g)
                    ins = norm.apply_one(dve, g, j, H)
                    if j == GB - 1:
                        ins.then_inc(h_ready, 1)

                def q_evict(g, par):
                    dve.wait_ge(psum_done["q"], g + 1)
                    at_least(dve, low_ready["q"], g)
                    o = QT[0][:].rearrange("p (b t) -> p b t", b=GB)
                    i = PJ[:].rearrange("p (b t) -> p b t", b=GB)
                    f = qfac[:].unsqueeze(1).to_broadcast([P, GB, P])
                    v.scalar_tensor_tensor(o, i, cols[:, 0:1], f, ALU.add, ALU.mult).then_inc(ready["q"], 1)

                def v_evict(g, par, first):
                    dve.wait_ge(psum_done["v"], g + 1)
                    if first:
                        dve.wait_ge(prep_pool, 2)
                    src = PJ[0:KN, :]
                    if hepos:
                        o = VM[par][0:KN, :, :].rearrange("p b (i c) -> p (b i) c", c=32)
                        cm = DM[0:KN, 0, :].unsqueeze(1).to_broadcast([KN, GB * 4, 32])
                        s = src.rearrange("p (b c) -> p b c", c=32)
                        v.tensor_tensor(s, s, bvb[0:KN, :].rearrange("p (b c) -> p b c", c=32),
                                        ALU.add).then_inc(v_biased, 1)
                        dve.wait_ge(v_biased, g + 1)
                        v.tensor_tensor(o, s, cm, ALU.mult).then_inc(ready["v"], 1)
                    else:
                        v.tensor_tensor(diagonal(VM[par]), src.rearrange("p (b i d) -> p b i d", i=4, d=8),
                                        bvb[0:KN, :].rearrange("p (b i d) -> p b i d", i=4, d=8),
                                        ALU.add).then_inc(ready["v"], 1)

                def softmax_shift(g, s, between=()):
                    n = g * S + s
                    sc, mx = SC[s % 2], MX[s % 2]
                    k = KCLS if hepos else KN
                    heads = W // k
                    view = sc[:, 0:W].rearrange("p (h k) -> p h k", k=k)
                    dve.wait_ge(sc_ready, n + 1)
                    v.tensor_reduce(mx[:], view, AX.X, ALU.max).then_inc(mx_ready, 1)
                    for f in between:
                        f()
                    at_least(dve, tp_ready, n - 3)
                    dve.wait_ge(mx_ready, n + 1)
                    v.tensor_tensor(PR[s % 4][:].rearrange("p (h k) -> p h k", k=k), view,
                                    mx[:].unsqueeze(2).to_broadcast([P, heads, k]),
                                    ALU.subtract).then_inc(sub_ready, 1)

                def reciprocals(b, bt):
                    dve.wait_ge(pv_done, b * U + U)
                    at_least(dve, ct_ready, b)
                    v.reciprocal(RD[:], ND[bt % 2][:, 1, :]).then_inc(rd_ready, 1)

                def normalise(b, bt):
                    at_least(dve, o_done, b - 1)
                    dve.wait_ge(rd_ready, b + 1)
                    v.tensor_tensor(CT[bt % 2][:], ND[bt % 2][:, 0, :], RD[:], ALU.mult).then_inc(ct_ready, 1)

                def add_out(g):
                    dve.wait_ge(o_done, g * GB + GB)
                    residual(nc, R, dve, x_added, g, OUT[:], g + 1)

                def add_sum(g):
                    dve.wait_ge(o_done, g * GB + GB)
                    xg = R.x[:, bass.ds(g * GB, GB), :]
                    v.tensor_tensor(xg, xg, OUT[:], ALU.add).then_inc(x_added, 1)

                def statistics(g, j):
                    dve.wait_ge(x_added, g + 1)
                    b = g * GB + j
                    v.bn_stats(R.stats[:, b, :], R.x[:, b, :]).then_inc(R.stats_done, 1)

                def of_sequence(f, g, u):
                    f(g * GB + u // U, (u // U) % GB)

                def evicts(g, s, par):
                    if mask is not None and slot_of["q"] == s:
                        q_evict(g, par)
                    if bv is not None and slot_of["v"] == s:
                        v_evict(g, par, False)

                def work_at(g, s, par, first, last):
                    steps = []
                    u = s - RECIP
                    if (u + 1) % U == 0 and not (first and u < 0):
                        steps.append(lambda: of_sequence(reciprocals, g, u))
                        if U == 1:
                            steps.append(lambda: of_sequence(normalise, g, u))
                    if U > 1 and u % U == 0 and not (first and u <= 0):
                        steps.append(lambda: of_sequence(normalise, g, u - 1))
                    if not last:
                        if U > 1:
                            steps += [lambda j=j: ln_sequence(g + 1, j) for j in range(GB) if LN_SLOTS[j] == s]
                        steps.append(lambda: evicts(g + 1, s, 1 - par))
                    if not first:
                        if U == 1:
                            if s == 3:
                                steps.append(lambda: add_out(g - 1))
                        elif s == SUM_SLOT:
                            steps.append(lambda: add_sum(g - 1))
                        else:
                            steps += [lambda j=j: statistics(g - 1, j) for j in range(GB) if STATS_SLOTS[j] == s]
                    return steps

                def group(g, par, first, last):
                    for s in range(S):
                        work = work_at(g, s, par, first, last)
                        if U == 1 and s == 0 and not last:
                            ln_group(g + 1)
                        softmax_shift(g, s, () if U == 1 else work)
                        if U == 1:
                            for f in work:
                                f()
                    if last:
                        for u in range(S - RECIP, S):
                            if (u + 1) % U == 0:
                                of_sequence(reciprocals, g, u)
                                of_sequence(normalise, g, u)
                        add_out(g)

                ln_group(0)
                if bo is not None:
                    for i in range(3):
                        v.tensor_copy(bo_terms[:, i, :], bor[:]).then_inc(bo_split, 1)
                        if i < 2:
                            dve.wait_ge(bo_split, 2 * i + 1)
                            v.tensor_tensor(bor[:], bor[:], bo_terms[:, i, :], ALU.subtract).then_inc(bo_split, 1)
                            dve.wait_ge(bo_split, 2 * i + 2)
                if mask is not None:
                    q_evict(0, 0)
                if bv is not None:
                    v_evict(0, 0, True)
                if packed:
                    dve.wait_ge(keys_first_in, 16 * n_first)
                    masked_keys(dve, v, 0, 0, (1, 3))
                groups_loop(dve, group, 3 if U == 1 else 1)

            @block.scalar
            def _(act):
                a = nc.scalar
                norm.scalar(act)
                act.wait_ge(keys_first_in, 16 * n_first)

                def high_part(step, g):
                    src = QT[0][:] if step == "q" else KT[0][:].rearrange("p b k -> p (b k)")
                    act.wait_ge(ready[step], g + 1)
                    for i in range(4):
                        at_least(act, (k3_in if step == "k" else q3_in)[i], 48 * g)
                    a.activation(HIGH[step][:], src, ACT.Copy).then_inc(high_ready[step], 1)

                def evict(step, g, par):
                    if (step == "v" and bv is not None) or (step == "q" and mask is not None):
                        return
                    act.wait_ge(psum_done[step], g + 1)
                    pj = PJ
                    if step == "v":
                        at_least(act, pv_done, (g - 1) * S)
                        a.activation(diagonal(VM[par]), pj[0:KN, :].rearrange("p (b i d) -> p b i d", i=4, d=8),
                                     ACT.Copy).then_inc(ready[step], 1)
                        return
                    if step == "ht":
                        if ln:
                            ins = a.activation(HT[par][:], pj[:], ACT.Identity, scale=cols[:, 3:4], bias=cols[:, 4:5])
                        else:
                            ins = a.activation(HT[par][:], pj[:], ACT.Copy)
                    elif step == "q":
                        if packed:
                            at_least(act, low_ready["q"], g)
                        q_out = QT[0 if packed else par][:]
                        if bq is not None:
                            ins = a.activation(q_out, pj[:], ACT.Identity, scale=SCALE, bias=cols[:, 2:3])
                        else:
                            ins = a.activation(q_out, pj[:], ACT.Copy, scale=SCALE)
                    else:
                        if packed:
                            at_least(act, low_ready["k"], g)
                        else:
                            at_least(act, km_ready[3], g - 1)
                        k_in = pj[:, 0:W].rearrange("p (b k) -> p b k", k=KN)
                        k_out = KT[0 if packed else par][:]
                        if bk is not None:
                            ins = a.activation(k_out, k_in, ACT.Identity, bias=cols[:, 1:2])
                        else:
                            ins = a.activation(k_out, k_in, ACT.Copy)
                    ins.then_inc(ready[step], 1)

                def take_queries(g, par, i):
                    act.wait_ge(q3_in[i], 48 * (g + 1))
                    at_least(act, sc_ready, (g - 1) * S)
                    a.activation(QR[par][:, i, :], Q3[:, i, :], ACT.Copy).then_inc(qr_ready[i], 1)

                def exponentials(g, s):
                    n = g * S + s
                    act.wait_ge(sub_ready, n + 1)
                    a.activation(PR[s % 4][:], PR[s % 4][:], ACT.Exp).then_inc(exp_ready, 1)

                def turned(g, s):
                    n = g * S + s
                    act.wait_ge(tp_ready, n + 1)
                    at_least(act, pv_done, n - 3)
                    a.activation(PT[s % 4][0:KN, :], TP[s % 2][0:KN, :], ACT.Copy).then_inc(pt_ready, 1)

                def group(g, par, first, last):
                    for s in range(S):
                        if not (first and s < TURN):
                            turned(g, s - TURN)
                        exponentials(g, s)
                        if not last:
                            for step in steps_of:
                                if slot_of[step] == s:
                                    evict(step, g + 1, 1 - par)
                                    if packed and step in "kq":
                                        high_part(step, g + 1)
                            if packed and s >= TAKE_SLOT:
                                take_queries(g + 1, 1 - par, s - TAKE_SLOT)
                    if last:
                        for u in range(S - TURN, S):
                            turned(g, u)

                for step in steps_of:
                    if step == "v" and bv is None:
                        act.wait_ge(prep_pool, 2)
                    if step == ("ht" if own_keys else "q"):
                        act.wait_ge(weights_in, 16 * n_weights)
                        at_least(act, prep, n_prep)
                    evict(step, 0, 0)
                    if packed and step in "kq":
                        high_part(step, 0)
                if packed:
                    for i in range(4):
                        take_queries(0, 0, i)
                groups_loop(act, group, 3 if U == 1 else 1)

            @block.tensor
            def _(pe):
                t = nc.tensor
                pe.wait_ge(keys_first_in, 16 * n_first)

                def project(step, g, par):
                    pj = PJ
                    n = steps_of.index(step)
                    at_least(pe, ready[steps_of[n - 1]], g + 1 if n else g)
                    if step == "ht":
                        pe.wait_ge(h_ready, g + 1)
                        for j in range(GB):
                            last = t.transpose(pj[:, j * P:(j + 1) * P], H[:, j, :], R.ident[:])
                    elif step == "q":
                        pe.wait_ge(ready["ht"], g + 1)
                        last = t.matmul(pj[:], Wq[:], HT[par][:], start=True, stop=True)
                    elif step == "k":
                        keys_there(g, par)
                        src = HT[par][:] if own_keys else CTX[par][:].rearrange("p b k -> p (b k)")
                        last = t.matmul(pj[:, 0:W], Wk[:], src, start=True, stop=True)
                    else:
                        keys_there(g, par)
                        for j in range(GB):
                            src = HT[par][:, j * P:(j + 1) * P] if own_keys else CTX[par][:, j, :]
                            last = t.matmul(pj[0:KN, j * D:(j + 1) * D], src, Wv[:], start=True, stop=True)
                    last.then_inc(psum_done[step], 1)

                def keys_there(g, par):
                    if own_keys:
                        pe.wait_ge(ready["ht"], g + 1)
                    else:
                        pe.wait_ge(ctx_in[par], ctx_count(g, par))

                def scores(g, s, par):
                    n = g * S + s
                    j, i = s // U, s % U
                    if packed and j == 0:
                        pe.wait_ge(km_ready[i], g + 1)
                        pe.wait_ge(qr_ready[i], g + 1)
                    if hepos and s == 0:
                        for slot in range(4):
                            pe.wait_ge(km_ready[slot], g + 1)
                        pe.wait_ge(ready["q"], g + 1)
                    at_least(pe, sub_ready, n - 1)
                    masked = mask is not None or causal is not None or pad is not None
                    queries, keys = ((QR[par][:, i, j * P:(j + 1) * P], KM[par][:, i, j, :]) if packed else
                                     (QT[par][:, j * P:(j + 1) * P], KM[par][:, j, i, :]))
                    last = t.matmul(SC[s % 2][:, 0:W], queries, keys, start=True, stop=not masked)
                    if pad is not None:
                        b = g * GB + j
                        rows = padb[0:1, b, :].unsqueeze(1).to_broadcast([1, 4, KC])
                        last = t.matmul(SC[s % 2][:, 0:W], R.ones_bf[0:1, :], rows, start=False, stop=True)
                    elif masked:
                        last = t.matmul(SC[s % 2][:, 0:W], R.ident_bf[:],
                                        addm[:].unsqueeze(1).to_broadcast([P, 4, KN]), start=False, stop=True)
                    last.then_inc(sc_ready, 1)

                def turn(g, s):
                    n = g * S + s
                    pe.wait_ge(exp_ready, n + 1)
                    at_least(pe, pt_ready, n - 1)
                    for q in range(4):
                        last = t.transpose(TP[s % 2][0:KN, q * P:(q + 1) * P], PR[s % 4][:, q * KN:(q + 1) * KN],
                                           R.ident[:])
                    last.then_inc(tp_ready, 1)

                def values(g, s, par):
                    n = g * S + s
                    j, i = (s // U) % GB, s % U
                    if s % S == 0:
                        pe.wait_ge(ready["v"], g + s // S + 1)
                    pe.wait_ge(pt_ready, n + 1)
                    if i == 0:
                        at_least(pe, ct_ready, g * GB + s // U - 1)
                    for what in range(2):
                        for q in range(4):
                            if what == 1:
                                w = DM[0:KN, i, :]
                            elif hepos:
                                w = VM[par][0:KN, j, 32 * q:32 * q + 32]
                            else:
                                h = 4 * q + i
                                w = VM[par][0:KN, j, 32 * h:32 * h + 32]
                            last = t.matmul(ND[j % 2][32 * q:32 * q + 32, what, :], w,
                                            PT[s % 4][0:KN, q * P:(q + 1) * P],
                                            start=(what == 0 and i == 0), stop=(i == U - 1), skip_group_check=True,
                                            tile_position=(0, 32 * q))
                    last.then_inc(pv_done, 1)

                def output(g, b, bt):
                    pe.wait_ge(ct_ready, b + 1)
                    if bt == 0:
                        at_least(pe, x_added, g)
                        if bo is not None:
                            t.matmul(OUT[:], R.ones_bf[:], bo3[:].unsqueeze(1).to_broadcast([P, GB, D]), start=True,
                                     stop=False, skip_group_check=True)
                    t.matmul(OUT[:, bt, :], CT[bt % 2][:], Wo[:], start=bo is None, stop=True,
                             skip_group_check=True).then_inc(o_done, 1)

                def behind(g, s, par, first):
                    if not (first and s < TURN) and s - TURN < S:
                        turn(g, s - TURN)
                    if not (first and s < VALUES) and s - VALUES < S:
                        values(g, s - VALUES, par if s >= VALUES else 1 - par)
                    u = s - OUTPUT
                    if not (first and u < 0) and (u + 1) % U == 0:
                        gg = g if u >= 0 else g - 1
                        output(gg, g * GB + u // U, (u // U) % GB)

                def group(g, par, first, last):
                    for s in range(S):
                        scores(g, s, par)
                        behind(g, s, par, first)
                        if not last:
                            for step in steps_of:
                                if slot_of[step] == s:
                                    project(step, g + 1, 1 - par)
                    if last:
                        for s in range(S, S + OUTPUT):
                            behind(g, s, par, False)

                project(steps_of[0], 0, 0)
                pe.wait_ge(weights_in, 16 * n_weights)
                at_least(pe, prep, n_prep - 1 if mask is not None else n_prep)
                if mask is not None:
                    t.matmul(OUT[:, 0, :], R.ones_bf[:], diag[:], start=True, stop=True).then_inc(f_psum, 1)
                for step in steps_of[1:]:
                    project(step, 0, 0)
                pe.wait_ge(prep_pool, 2 if hepos else 7)
                if bo is not None:
                    pe.wait_ge(bo3_in, 48)
                groups_loop(pe, group, 3 if U == 1 else 1)


def ctx_count(g, par):
    return (g + 2 - par) * 8


def v_broadcast(v):
    return v.rearrange("(a p) -> a p", a=1).to_broadcast([P, D])


class Experts:

    def __init__(self, nc, R, sb, sem, name, E):
        self.E = E
        self.ht = sb(name + "_htall", [P, NB * P])
        self.logits = sb(name + "_logits", [P, NB, E])
        self.gates = sb(name + "_gates", [P, NB, E])


def top_choices(nc, v, link, X, cur, scratch, rank, E, k, chosen, each=None):
    m, eq, r = scratch
    bc = lambda a: a.unsqueeze(2).to_broadcast([P, NB, E])
    for it in range(k):
        link(v.tensor_reduce(m[:], cur, AX.X, ALU.max))
        link(v.tensor_tensor(eq[:], cur, bc(m[:]), ALU.is_equal))
        link(v.tensor_tensor(eq[:], eq[:], rank[:].unsqueeze(1).to_broadcast([P, NB, E]), ALU.mult))
        link(v.tensor_reduce(r[:], eq[:], AX.X, ALU.max))
        one = each[it] if each is not None else eq[:]
        link(v.tensor_tensor(one, eq[:], bc(r[:]), ALU.is_equal))
        if it == 0:
            link(v.tensor_copy(chosen, one))
        else:
            link(v.tensor_tensor(chosen, chosen, one, ALU.add))
        if it < k - 1:
            link(v.scalar_tensor_tensor(cur, one, -3.0e38, cur, ALU.mult, ALU.add))


def routing_part(nc, R, I, name, X, kind, wr, loads, extra, splits=()):
    E = X.E
    TOP = {"proto": 2, "shared": 4, "capacity": 2, "swiglu": 2}[kind]
    with ExitStack() as stack:
        sb, ps, sem = allocator(nc, stack)
        n_ = lambda s: f"{name}r_{s}"
        norm = Norm(nc, R, sb, sem, n_("n"))
        WR = sb(n_("wr"), [P, E])
        rank = sb(n_("rank"), [P, E])
        H = [sb(n_(f"h{i}"), [P, GB, D]) for i in range(2)]
        HS = [sb(n_(f"hs{i}"), [P, GT]) for i in range(2)]
        m, r = sb(n_("m"), [P, NB]), sb(n_("r"), [P, NB])
        eq = sb(n_("eq"), [P, NB, E])
        ex = sb(n_("ex"), [P, NB, E])
        dist = sb(n_("dist"), [P, NB, E])
        TR = [ps(n_(f"tr{i}"), [P, 512]) for i in range(2)]
        LG = [ps(n_(f"lg{i}"), [P, GB, E]) for i in range(2)]
        small_in, big_in = sem(n_("small_in")), sem(n_("big_in"))
        raw = [sb(n_(f"raw{i}"), hi.shape) for i, (_, hi, _) in enumerate(splits)]
        raw_in = [sem(n_(f"raw_in{i}")) for i in range(len(splits))]
        high_ready, low_ready = sem(n_("high_ready")), sem(n_("low_ready"))
        h_ready, tr_ready, hs_ready, lg_ready, l_ready = (sem(n_(s)) for s in
                                                         ("h_ready", "tr_ready", "hs_ready", "lg_ready", "l_ready"))
        ht_in, chain, act_step, pe_step = [sem(n_(f"ht_in{i}")) for i in range(2)], sem(n_("chain")), sem(n_("act_step")), sem(n_("pe_step"))
        act_go, pe_go, scans, x2_ready = (sem(n_(s)) for s in ("act_go", "pe_go", "scans", "x2_ready"))
        if kind == "proto":
            psq = sb(n_("psq"), [P, E])
            protoT2 = sb(n_("protoT2"), [P, E])
            x2 = sb(n_("x2"), [P, NB])
            junk = sb(n_("junk"), [P, 2, GB, D])
            temp = sb(n_("temp"), [P, 2])
            PQ = ps(n_("pq"), [P, E])
        if kind == "swiglu":
            lnc = sb(n_("lnc"), [P, 2])
        if kind == "capacity":
            one = [sb(n_(f"one{i}"), [P, NB, E]) for i in range(2)]
            oneb = [sb(n_(f"oneb{i}"), [P, NB, E], BF16) for i in range(2)]
            tri = sb(n_("tri"), [P, P], BF16)
            total = [sb(n_(f"total{i}"), [P, NB, E]) for i in range(2)]
            run = [sb(n_(f"run{i}"), [P, NB, E]) for i in range(2)]
            ones64 = sb(n_("ones64"), [P, NB])
            CUM = [ps(n_(f"cum{i}"), [P, NB * E]) for i in range(2)]
            TOT = [ps(n_("tot0"), [P, NB * E]), ps(n_("tot1"), [P, NB * E])]
        n_small = 2 + {"proto": 1, "shared": 0, "capacity": 1, "swiglu": 2}[kind]

        with nc.Block() as block:
            @block.sync
            def _(sp):
                sp.dma_start(WR[:], wr).then_inc(small_in, 16)
                sp.dma_start(rank[:], extra["rank"].to_broadcast([P, E])).then_inc(small_in, 16)
                if kind == "proto":
                    sp.dma_start(temp[:, 0:1], extra["temp"].to_broadcast([P, 1])).then_inc(small_in, 16)
                if kind == "swiglu":
                    for c in range(2):
                        sp.dma_start(lnc[:, c:c + 1], extra["ln"][c].rearrange("(p a) -> p a", a=1)).then_inc(small_in, 16)
                if kind == "capacity":
                    sp.dma_start(tri[:], I["tri"]).then_inc(small_in, 16)
                for i, (w, hi, lo) in enumerate(splits):
                    sp.dma_start(raw[i][:], w).then_inc(raw_in[i], 16)
                for t, w in loads:
                    sp.dma_start(t, w).then_inc(big_in, 16)

                def keep(g, par):
                    sp.wait_ge(hs_ready, g + 1)
                    sp.dma_start(X.ht[:, bass.ds(g * GT, GT)], HS[par][:]).then_inc(ht_in[par], 16)

                def pair(g):
                    keep(g, 0)
                    keep(g + 1, 1)

                pairs_loop(sp, NG, pair)
                for i in range(2):
                    sp.wait_ge(ht_in[i], 8 * NG)
                sp.wait_ge(big_in, 16 * len(loads))

            @block.gpsimd
            def _(pool):
                for i, (w, hi, lo) in enumerate(splits):
                    pool.wait_ge(high_ready, i + 1)
                    nc.gpsimd.tensor_tensor(lo[:], raw[i][:], hi[:].bitcast(F32), ALU.subtract).then_inc(low_ready, 1)

            @block.tensor
            def _(pe):
                t = nc.tensor
                pe.wait_ge(small_in, 16 * n_small)
                if kind == "proto":
                    pe.wait_ge(chain, 1)
                    t.matmul(PQ[:], R.ones[:], protoT2[:], start=True, stop=True).then_inc(pe_step, 1)

                def turn(g, par):
                    pe.wait_ge(h_ready, g + 1)
                    at_least(pe, hs_ready, g - 1)
                    for j in range(GB):
                        last = t.transpose(TR[par][:, j * P:(j + 1) * P], H[par][:, j, :], R.ident[:])
                    last.then_inc(tr_ready, 1)

                def scores(g, par):
                    pe.wait_ge(hs_ready, g + 1)
                    at_least(pe, l_ready, g - 1)
                    for j in range(GB):
                        last = t.matmul(LG[par][:, j, :], HS[par][:, j * P:(j + 1) * P], WR[:], start=True, stop=True)
                    last.then_inc(lg_ready, 1)

                turn(0, 0)
                def pair(g):
                    turn(g + 1, 1)
                    scores(g, 0)
                    turn(g + 2, 0)
                    scores(g + 1, 1)

                pairs_loop(pe, NG - 2, pair)
                turn(NG - 1, 1)
                scores(NG - 2, 0)
                scores(NG - 1, 1)
                if kind == "capacity":
                    for i in range(2):
                        pe.wait_ge(pe_go, i + 1)
                        flat = oneb[i][:].rearrange("p b e -> p (b e)")
                        t.matmul(CUM[i][:], tri[:], flat, start=True, stop=True)
                        t.matmul(TOT[i][:], R.ones_bf[:], flat, start=True, stop=True).then_inc(pe_step, 1)

            @block.scalar
            def _(act):
                a = nc.scalar
                norm.scalar(act)
                act.wait_ge(small_in, 16 * n_small)

                def hs(g, par):
                    act.wait_ge(tr_ready, g + 1)
                    at_least(act, ht_in[par], (g - par) * 8)
                    at_least(act, lg_ready, g - 1)
                    if kind == "swiglu":
                        ins = a.activation(HS[par][:], TR[par][:], ACT.Identity, scale=lnc[:, 0:1], bias=lnc[:, 1:2])
                    else:
                        ins = a.activation(HS[par][:], TR[par][:], ACT.Copy)
                    ins.then_inc(hs_ready, 1)

                def lg(g, par):
                    act.wait_ge(lg_ready, g + 1)
                    a.activation(X.logits[:, bass.ds(g * GB, GB), :], LG[par][:], ACT.Copy).then_inc(l_ready, 1)

                hs(0, 0)
                def pair(g):
                    hs(g + 1, 1)
                    lg(g, 0)
                    hs(g + 2, 0)
                    lg(g + 1, 1)

                pairs_loop(act, NG - 2, pair)
                hs(NG - 1, 1)
                lg(NG - 2, 0)
                lg(NG - 1, 1)
                if kind == "proto":
                    act.wait_ge(act_go, 1)
                    a.activation(dist[:], dist[:], ACT.Sqrt).then_inc(act_step, 1)
                    act.wait_ge(act_go, 2)
                    a.activation(ex[:], ex[:], ACT.Exp, scale=temp[:, 1:2]).then_inc(act_step, 1)
                else:
                    act.wait_ge(act_go, 1)
                    a.activation(ex[:], ex[:], ACT.Exp).then_inc(act_step, 1)

            @block.vector
            def _(dve):
                v = nc.vector
                count = [0]

                def link(ins):
                    count[0] += 1
                    ins.then_inc(chain, 1)
                    dve.wait_ge(chain, count[0])

                norm.vector(dve)
                dve.wait_ge(small_in, 16 * n_small)
                if kind == "proto":
                    link(v.tensor_tensor(protoT2[:], WR[:], WR[:], ALU.mult))
                    dve.wait_ge(pe_step, 1)
                    link(v.tensor_copy(psq[:], PQ[:]))
                    link(v.tensor_scalar(temp[:, 1:2], temp[:, 0:1], -1.0, None, ALU.mult))
                    link(v.tensor_tensor(temp[:, 0:1], temp[:, 0:1], temp[:, 1:2], ALU.max))
                    link(v.tensor_scalar(temp[:, 0:1], temp[:, 0:1], 0.1, None, ALU.max))
                    link(v.reciprocal(temp[:, 1:2], temp[:, 0:1]))
                    link(v.tensor_scalar(temp[:, 1:2], temp[:, 1:2], -1.0, None, ALU.mult))

                def ln_group(g, par):
                    at_least(dve, tr_ready, g - 1)
                    norm.apply(dve, g, H[par]).then_inc(h_ready, 1)
                    if kind == "proto":
                        dve.wait_ge(h_ready, g + 1)
                        at_least(dve, x2_ready, (g - 1) * GB)
                        for j in range(GB):
                            b = g * GB + j
                            v.scalar_tensor_tensor(junk[:, par, j, :], H[par][:, j, :], 1.0, H[par][:, j, :], ALU.mult, ALU.mult,
                                                   accum_out=x2[:, bass.ds(b, 1)]).then_inc(x2_ready, 1)

                def pair(g):
                    ln_group(g, 0)
                    ln_group(g + 1, 1)

                pair(0)
                with dve.Fori(2, 5, 2) as g:
                    pair(g)
                at = 6
                for i, (w, hi, lo) in enumerate(splits):
                    dve.wait_ge(raw_in[i], 16)
                    v.tensor_copy(hi[:], raw[i][:]).then_inc(high_ready, 1)
                    pair(at)
                    at += 2
                with dve.Fori(at, NG - 1, 2) as g:
                    pair(g)
                dve.wait_ge(l_ready, NG)
                bc = lambda a: a.unsqueeze(2).to_broadcast([P, NB, E])
                L = X.logits
                scratch = (m, eq, r)
                if kind == "proto":
                    dve.wait_ge(x2_ready, NB)
                    link(v.tensor_copy(eq[:], psq[:].unsqueeze(1).to_broadcast([P, NB, E])))
                    link(v.tensor_tensor(eq[:], eq[:], bc(x2[:]), ALU.add))
                    link(v.scalar_tensor_tensor(L[:], L[:], -2.0, eq[:], ALU.mult, ALU.add))
                    v.tensor_scalar(dist[:], L[:], 0.0, None, ALU.max).then_inc(chain, 1)
                    count[0] += 1
                    link(v.tensor_scalar(eq[:], L[:], 0.0, -1.0, ALU.max, ALU.mult))
                    v.tensor_copy(L[:], eq[:]).then_inc(act_go, 1)
                    dve.wait_ge(act_go, 1)
                    top_choices(nc, v, link, X, L[:], scratch, rank, E, TOP, X.gates[:])
                    dve.wait_ge(act_step, 1)
                    link(v.tensor_reduce(m[:], dist[:], AX.X, ALU.min))
                    v.tensor_tensor(ex[:], dist[:], bc(m[:]), ALU.subtract).then_inc(act_go, 1)
                    dve.wait_ge(act_step, 2)
                else:
                    link(v.tensor_reduce(m[:], L[:], AX.X, ALU.max))
                    v.tensor_tensor(ex[:], L[:], bc(m[:]), ALU.subtract).then_inc(act_go, 1)
                    dve.wait_ge(act_go, 1)
                    top_choices(nc, v, link, X, L[:], scratch, rank, E, TOP, X.gates[:],
                                [o[:] for o in one] if kind == "capacity" else None)
                    dve.wait_ge(act_step, 1)
                G = X.gates[:]
                if kind == "shared":
                    link(v.tensor_reduce(m[:], ex[:], AX.X, ALU.add))
                    link(v.tensor_tensor(G, G, ex[:], ALU.mult))
                else:
                    link(v.tensor_tensor(G, G, ex[:], ALU.mult))
                    link(v.tensor_reduce(m[:], G, AX.X, ALU.add))
                link(v.reciprocal(r[:], m[:]))
                link(v.tensor_tensor(G, G, bc(r[:]), ALU.mult))
                if kind == "capacity":
                    link(v.memset(ones64[:], 1.0))
                    for i in range(2):
                        v.tensor_copy(oneb[i][:], one[i][:]).then_inc(pe_go, 1)
                    for i in range(2):
                        dve.wait_ge(pe_step, i + 1)
                        link(v.tensor_copy(total[i][:], TOT[i][:].rearrange("p (b e) -> p b e", e=E)))
                        for e in range(E):
                            ins = v.tensor_tensor_scan(run[i][:, :, e], ones64[:], total[i][:, :, e], 0.0, ALU.mult,
                                                       ALU.add)
                            if e == E - 1:
                                link(ins)
                            else:
                                ins.then_inc(scans, 1)
                        dve.wait_ge(scans, (E - 1) * (i + 1))
                        link(v.tensor_tensor(total[i][:], run[i][:], total[i][:], ALU.subtract))
                        link(v.tensor_tensor(total[i][:], CUM[i][:].rearrange("p (b e) -> p b e", e=E), total[i][:],
                                             ALU.add))
                        if i == 1:
                            link(v.tensor_tensor(total[1][:], total[1][:],
                                                 run[0][:, NB - 1, :].unsqueeze(1).to_broadcast([P, NB, E]), ALU.add))
                        link(v.scalar_tensor_tensor(one[i][:], total[i][:], float(extra["cap"]) + 0.5, one[i][:],
                                                    ALU.is_lt, ALU.mult))
                    link(v.tensor_tensor(one[0][:], one[0][:], one[1][:], ALU.add))
                    link(v.tensor_tensor(G, G, one[0][:], ALU.mult))


def three_passes(t, out, w_hi, w_lo, a_hi, a_lo, start=True, stop=True, before_lo=None):
    t.matmul(out, w_hi, a_hi, start=start, stop=False)
    t.matmul(out, w_lo, a_hi, start=False, stop=False)
    if before_lo is not None:
        before_lo()
    return t.matmul(out, w_hi, a_lo, start=False, stop=stop)


def gated_rows_phase(nc, R, I, name, kind):
    E = 32 if kind == "proto" else 16
    BL = 4 if kind == "proto" else 9
    UNG = 0 if kind == "proto" else 1
    AR = 4 if kind == "proto" else 6
    TERMS = 96 // E
    K3 = TERMS * E
    LAG = 2 if kind == "proto" else 3
    COPY_UNIT, SUM_UNIT, ADD_UNIT = (2, 3, 3) if kind == "proto" else (3, 4, 5)
    with ExitStack() as stack:
        sb, ps, sem = allocator(nc, stack)
        n_ = lambda s: f"{name}_{s}"
        X = Experts(nc, R, sb, sem, name, E)
        HI = {w: sb(n_(w + "hi"), [P, BL * P], F32R) for w in ("up", "down")}
        LO = {w: sb(n_(w + "lo"), [P, BL * P], F32R) for w in ("up", "down")}
        SEL = sb(n_("sel"), [K3, BL - UNG, P], BF16)
        loads = [(SEL[:], I[n_("sel")])]
        if kind == "proto":
            BI = sb(n_("bias"), [K3, D])
            BI3 = [sb(n_(f"bias{i}"), [K3, D], BF16) for i in range(3)]
            loads += [(BI[E * i:E * (i + 1), :], I[n_("bias")]) for i in range(TERMS)]
        extra = {"rank": I[f"rank{E}"], "temp": I["temp"] if kind == "proto" else None}
        splits = [(I[n_(w)], HI[w], LO[w]) for w in ("up", "down")]
        routing_part(nc, R, I, name, X, kind, I[n_("router")], loads, extra, splits)

        g3 = sb(n_("g3"), [P, NB, TERMS, E], BF16)
        rest = sb(n_("rest"), [P, NB, E])
        GS = [sb(n_(f"gs{i}"), [P, GB, K3], BF16) for i in range(2)]
        G3T = [sb(n_(f"g3t{i}"), [K3, GT], BF16) for i in range(2)]
        XH = [sb(n_(f"xh{i}"), [P, GT], F32R) for i in range(2)]
        XL = [sb(n_(f"xl{i}"), [P, GT], F32R) for i in range(2)]
        A = [sb(n_(f"a{i}"), [P, GT]) for i in range(2)]
        AG = [sb(n_(f"ag{i}"), [P, GT]) for i in range(2)]
        AH = [sb(n_(f"ah{i}"), [P, GT], F32R) for i in range(AR)]
        AL = [sb(n_(f"al{i}"), [P, GT], F32R) for i in range(AR)]
        YS = [sb(n_(f"ys{i}"), [P, GT]) for i in range(2)]
        PU = [ps(n_(f"pu{i}"), [P, 512]) for i in range(2)]
        PG = [ps(n_(f"pg{i}"), [P, 512]) for i in range(2)]
        PO = [ps(n_(f"po{i}"), [P, GT]) for i in range(2)]
        PT3 = ps(n_("pt3"), [K3, GT], BF16)
        PX = ps(n_("px"), [P, GB, D])
        names = ("split", "gs_ready", "gt_psum", "gt_ready", "xh_ready", "xl_ready", "up_ready", "ge_ready", "a_ready",
                 "ag_ready", "hi_ready", "lo_ready", "dn_ready", "ys_ready", "px_ready", "x_added", "zeroed", "bias_split")
        Z = {s: sem(n_(s)) for s in names}
        func = ACT.Copy if kind == "proto" else ACT.Gelu
        GBL = BL - UNG

        def lagged(g, c, par, first, lag, f):
            if c >= lag:
                f(g, c - lag, par)
            elif not first:
                f(g - 1, BL + c - lag, 1 - par)

        with nc.Block() as block:
            @block.gpsimd
            def _(pool):
                pool.wait_ge(Z["split"], 5)
                if TERMS > 3:
                    pool.wait_ge(Z["zeroed"], 1)

                def stage(g, par):
                    at_least(pool, Z["gt_psum"], g - 1)
                    src = g3[:, bass.ds(g * GB, GB), :, :].rearrange("p b t e -> p b (t e)")
                    nc.gpsimd.tensor_copy(GS[par][:], src).then_inc(Z["gs_ready"], 1)

                def pair(g):
                    stage(g, 0)
                    stage(g + 1, 1)

                pairs_loop(pool, NG, pair)

            @block.vector
            def _(dve):
                v = nc.vector

                def split_inputs(g, par):
                    src = X.ht[:, bass.ds(g * GT, GT)]
                    at_least(dve, Z["up_ready"], (g - 1) * BL)
                    v.tensor_copy(XH[par][:], src).then_inc(Z["xh_ready"], 1)
                    dve.wait_ge(Z["xh_ready"], g + 1)
                    v.tensor_tensor(XL[par][:], src, XH[par][:].bitcast(F32), ALU.subtract).then_inc(Z["xl_ready"], 1)

                split_inputs(0, 0)
                if TERMS > 3:
                    v.memset(g3[:, :, 3:TERMS, :], 0.0).then_inc(Z["zeroed"], 1)
                v.tensor_copy(g3[:, :, 0, :], X.gates[:]).then_inc(Z["split"], 1)
                dve.wait_ge(Z["split"], 1)
                v.tensor_tensor(rest[:], X.gates[:], g3[:, :, 0, :], ALU.subtract).then_inc(Z["split"], 1)
                dve.wait_ge(Z["split"], 2)
                v.tensor_copy(g3[:, :, 1, :], rest[:]).then_inc(Z["split"], 1)
                dve.wait_ge(Z["split"], 3)
                v.tensor_tensor(rest[:], rest[:], g3[:, :, 1, :], ALU.subtract).then_inc(Z["split"], 1)
                dve.wait_ge(Z["split"], 4)
                v.tensor_copy(g3[:, :, 2, :], rest[:]).then_inc(Z["split"], 1)
                if kind == "proto":
                    for i in range(3):
                        v.tensor_copy(BI3[i][:], BI[:]).then_inc(Z["bias_split"], 1)
                        dve.wait_ge(Z["bias_split"], 2 * i + 1)
                        v.tensor_tensor(BI[:], BI[:], BI3[i][:], ALU.subtract).then_inc(Z["bias_split"], 1)
                        dve.wait_ge(Z["bias_split"], 2 * i + 2)

                def gate(g, c, par):
                    n = g * BL + c
                    q = par * BL + c
                    dve.wait_ge(Z["a_ready"], n + 1)
                    at_least(dve, Z["lo_ready"], n - 1)
                    if c < UNG:
                        v.tensor_copy(AG[q % 2][:], A[q % 2][:]).then_inc(Z["ag_ready"], 1)
                        return
                    dve.wait_ge(Z["ge_ready"], g * GBL + c - UNG + 1)
                    v.tensor_tensor(AG[q % 2][:], A[q % 2][:], PG[(par * GBL + c - UNG) % 2][:],
                                    ALU.mult).then_inc(Z["ag_ready"], 1)

                def low(g, c, par):
                    n = g * BL + c
                    q = par * BL + c
                    dve.wait_ge(Z["hi_ready"], n + 1)
                    at_least(dve, Z["dn_ready"], n - AR + 1)
                    v.tensor_tensor(AL[q % AR][:], AG[q % 2][:], AH[q % AR][:].bitcast(F32),
                                    ALU.subtract).then_inc(Z["lo_ready"], 1)

                def add(g, par):
                    dve.wait_ge(Z["px_ready"], g + 1)
                    residual(nc, R, dve, Z["x_added"], g, PX[:], g + 1)

                def group(g, par, first, last):
                    for c in range(BL):
                        gate(g, c, par)
                        lagged(g, c, par, first, 1, low)
                        if c == 1 and not last:
                            split_inputs(g + 1, 1 - par)
                        if c == ADD_UNIT and not first:
                            add(g - 1, 1 - par)
                    if last:
                        low(g, BL - 1, par)
                        add(g, par)

                groups_loop(dve, group, 3)

            @block.scalar
            def _(act):
                a = nc.scalar

                def gates_in(g, par):
                    act.wait_ge(Z["gt_psum"], g + 1)
                    at_least(act, Z["ge_ready"], (g - 1) * GBL)
                    a.activation(G3T[par][:], PT3[:], ACT.Copy).then_inc(Z["gt_ready"], 1)

                def rows(g, c, par):
                    n = g * BL + c
                    q = par * BL + c
                    act.wait_ge(Z["up_ready"], n + 1)
                    at_least(act, Z["ag_ready"], n - 1)
                    a.activation(A[q % 2][:], PU[q % 2][:], func).then_inc(Z["a_ready"], 1)

                def high(g, c, par):
                    n = g * BL + c
                    q = par * BL + c
                    act.wait_ge(Z["ag_ready"], n + 1)
                    at_least(act, Z["dn_ready"], n - AR + 1)
                    a.activation(AH[q % AR][:], AG[q % 2][:], ACT.Copy).then_inc(Z["hi_ready"], 1)

                def sums(g, par):
                    act.wait_ge(Z["dn_ready"], (g + 1) * BL)
                    at_least(act, Z["px_ready"], g - 1)
                    a.activation(YS[par][:], PO[par][:], ACT.Copy).then_inc(Z["ys_ready"], 1)

                def group(g, par, first, last):
                    for c in range(BL):
                        rows(g, c, par)
                        lagged(g, c, par, first, 1, high)
                        if c == 0 and not last:
                            gates_in(g + 1, 1 - par)
                        if c == COPY_UNIT and not first:
                            sums(g - 1, 1 - par)
                    if last:
                        high(g, BL - 1, par)
                        sums(g, par)

                gates_in(0, 0)
                groups_loop(act, group, 3)

            @block.tensor
            def _(pe):
                t = nc.tensor

                def gates_turn(g, par):
                    pe.wait_ge(Z["gs_ready"], g + 1)
                    at_least(pe, Z["gt_ready"], g)
                    for j in range(GB):
                        last = t.transpose(PT3[:, j * P:(j + 1) * P], GS[par][:, j, :], R.ident_bf[:])
                    last.then_inc(Z["gt_psum"], 1)

                def up(g, c, par):
                    n = g * BL + c
                    q = par * BL + c
                    if c == 0:
                        pe.wait_ge(Z["xh_ready"], g + 1)
                        pe.wait_ge(Z["xl_ready"], g + 1)
                    at_least(pe, Z["a_ready"], n - 1)
                    w = slice(c * P, (c + 1) * P)
                    three_passes(t, PU[q % 2][:], HI["up"][:, w], LO["up"][:, w], XH[par][:],
                                 XL[par][:]).then_inc(Z["up_ready"], 1)
                    if c >= UNG:
                        if c == UNG:
                            pe.wait_ge(Z["gt_ready"], g + 1)
                        at_least(pe, Z["ag_ready"], n - 1 if c >= UNG + 2 else g * BL - 1 + c - UNG)
                        t.matmul(PG[(par * GBL + c - UNG) % 2][:], SEL[:, c - UNG, :], G3T[par][:], start=True,
                                 stop=True).then_inc(Z["ge_ready"], 1)

                def down(g, c, par):
                    n = g * BL + c
                    q = par * BL + c
                    if c == 0:
                        at_least(pe, Z["ys_ready"], g - 1)
                        if kind == "proto":
                            for i in (2, 1, 0):
                                t.matmul(PO[par][:], BI3[i][:], G3T[par][:], start=(i == 2), stop=False)
                    w = slice(c * P, (c + 1) * P)
                    pe.wait_ge(Z["hi_ready"], n + 1)
                    three_passes(t, PO[par][:], HI["down"][:, w], LO["down"][:, w], AH[q % AR][:], AL[q % AR][:],
                                 start=(c == 0 and kind != "proto"), stop=(c == BL - 1),
                                 before_lo=lambda: pe.wait_ge(Z["lo_ready"], n + 1)).then_inc(Z["dn_ready"], 1)

                def sums_turn(g, par):
                    pe.wait_ge(Z["ys_ready"], g + 1)
                    at_least(pe, Z["x_added"], g)
                    for j in range(GB):
                        last = t.transpose(PX[:, j, :], YS[par][:, j * P:(j + 1) * P], R.ident[:])
                    last.then_inc(Z["px_ready"], 1)

                def group(g, par, first, last):
                    for c in range(BL):
                        up(g, c, par)
                        lagged(g, c, par, first, LAG, down)
                        if c == 0 and not last:
                            gates_turn(g + 1, 1 - par)
                        if c == SUM_UNIT and not first:
                            sums_turn(g - 1, 1 - par)
                    if last:
                        for u in range(BL - LAG, BL):
                            down(g, u, par)
                        sums_turn(g, par)

                if kind == "proto":
                    pe.wait_ge(Z["bias_split"], 6)
                gates_turn(0, 0)
                groups_loop(pe, group, 3)


def gated_outputs_phase(nc, R, I, name, kind, out=None):
    E = 8
    HB = 4 if kind == "capacity" else 2
    N = E * HB
    two = kind == "swiglu"
    LAG = 3 if two else 2
    SUM_UNIT, TURN_UNIT, SPLIT_UNIT, PRESUM_UNIT = 5, 8, 10, 12
    ADDS = E - 1
    K3 = 96
    with ExitStack() as stack:
        sb, ps, sem = allocator(nc, stack)
        n_ = lambda s: f"{name}_{s}"
        X = Experts(nc, R, sb, sem, name, E)
        pieces = [("w1", N * P), ("wd", N * D)] + ([("w2", N * P)] if two else [])
        HI = {w: sb(n_(w + "hi"), [P, cols], F32R) for w, cols in pieces}
        LO = {w: sb(n_(w + "lo"), [P, cols], F32R) for w, cols in pieces}
        SEL = sb(n_("sel"), [K3, E, P], BF16)
        loads = [(SEL[:], I[n_("sel")])]
        if not two:
            B1, B2 = sb(n_("b1"), [P, N]), sb(n_("b2"), [P, E])
            loads += [(B1[:], I[n_("b1")]), (B2[:], I[n_("b2")])]
        extra = {"rank": I["rank8"], "cap": 2 * NB * P // E, "ln": (I["ln2_scale"], I["ln2_shift"]) if two else None}
        splits = [(I[n_(w)], HI[w], LO[w]) for w, _ in pieces]
        routing_part(nc, R, I, name, X, kind, I[n_("router")], loads, extra, splits)

        g3 = sb(n_("g3"), [P, NB, 3, E], BF16)
        rest = X.logits
        GS = [sb(n_(f"gs{i}"), [P, GB, K3]) for i in range(2)]
        G3T = [sb(n_(f"g3t{i}"), [K3, GT], BF16) for i in range(2)]
        XH = [sb(n_(f"xh{i}"), [P, GT], F32R) for i in range(2)]
        XL = [sb(n_(f"xl{i}"), [P, GT], F32R) for i in range(2)]
        A = [sb(n_(f"a{i}"), [P, GT]) for i in range(2)]
        AH = [sb(n_(f"ah{i}"), [P, GT], F32R) for i in range(4)]
        AL = [sb(n_(f"al{i}"), [P, GT], F32R) for i in range(4)]
        S = [sb(n_(f"s{i}"), [P, GT]) for i in range(2)] if two else None
        YG = [sb(n_(f"yg{i}"), [P, GT]) for i in range(2)]
        YA = [sb(n_(f"ya{i}"), [P, GT]) for i in range(2)]
        GX = [sb(n_(f"gx{i}"), [P, GT]) for i in range(2)]
        PU = [ps(n_(f"pu{i}"), [P, 512]) for i in range(2)]
        PV = [ps(n_(f"pv{i}"), [P, 512]) for i in range(2)] if two else None
        PY = [ps(n_(f"py{i}"), [P, GT]) for i in range(2)]
        PG = ps(n_("pg"), [P, GT])
        PT = ps(n_("pt"), [P, GB, D])
        Z = {s: sem(n_(s)) for s in ("split", "zeroed", "gs_ready", "gt_psum", "gt_ready", "xh_ready", "xl_ready",
                                     "up_ready", "s_ready", "a_ready", "hi_ready", "lo_ready", "dn_ready", "ge_ready",
                                     "gx_ready", "yg_ready", "ya_ready", "px_ready", "x_added", "presummed")}
        if out is not None:
            view = out.rearrange("b t d -> t b d")
            KEPT = [sb(n_(f"kept{i}"), [P, GB, D]) for i in range(2)]
            kept_in, stored = ([sem(n_(f"{s}{i}")) for i in range(2)] for s in ("kept_in", "stored"))

        def lagged(g, s, first, lag, f):
            if s >= lag:
                f(g, s - lag)
            elif not first:
                f(g - 1, N + s - lag)

        with nc.Block() as block:
            if out is not None:
                @block.sync
                def _(sp):
                    def load(g, par):
                        sp.dma_start(KEPT[par][:], view[:, bass.ds(g * GB, GB), :]).then_inc(kept_in[par], 16)

                    def store(g, par):
                        sp.wait_ge(Z["x_added"], g + 1)
                        sp.dma_start(view[:, bass.ds(g * GB, GB), :], KEPT[par][:]).then_inc(stored[par], 16)

                    def turn_over(g, par):
                        store(g, par)
                        sp.wait_ge(stored[par], ctx_count(g, par))
                        load(g + 2, par)

                    def pair(g):
                        turn_over(g, 0)
                        turn_over(g + 1, 1)

                    load(0, 0)
                    load(1, 1)
                    pairs_loop(sp, NG - 2, pair)
                    store(NG - 2, 0)
                    store(NG - 1, 1)
                    for i in range(2):
                        sp.wait_ge(stored[i], 8 * NG)

            @block.gpsimd
            def _(pool):
                v = nc.gpsimd

                def stage(g, par):
                    at_least(pool, Z["gt_psum"], g - 1)
                    src = g3[:, bass.ds(g * GB, GB), :, :].rearrange("p b t e -> p b (t e)")
                    v.tensor_copy(GS[par][:, :, 0:3 * E], src).then_inc(Z["gs_ready"], 1)

                def group(g, par, first, last):
                    if not last:
                        stage(g + 1, 1 - par)
                    for e in range(1, E):
                        pool.wait_ge(Z["yg_ready"], g * E + e + 1)
                        if e == 1:
                            at_least(pool, Z["px_ready"], g - 1)
                            ins = v.tensor_tensor(YA[par][:], YG[0][:], YG[1][:], ALU.add)
                        else:
                            pool.wait_ge(Z["ya_ready"], g * ADDS + e - 1)
                            ins = v.tensor_tensor(YA[par][:], YA[par][:], YG[e % 2][:], ALU.add)
                        ins.then_inc(Z["ya_ready"], 1)

                for i in range(2):
                    v.memset(GS[i][:], 0.0).then_inc(Z["zeroed"], 1)
                pool.wait_ge(Z["zeroed"], 2)
                pool.wait_ge(Z["split"], 5)
                stage(0, 0)
                groups_loop(pool, group, 3)

            @block.vector
            def _(dve):
                v = nc.vector
                def split_inputs(g, par):
                    src = X.ht[:, bass.ds(g * GT, GT)]
                    at_least(dve, Z["up_ready"], (g - 1) * N)
                    v.tensor_copy(XH[par][:], src).then_inc(Z["xh_ready"], 1)
                    dve.wait_ge(Z["xh_ready"], g + 1)
                    v.tensor_tensor(XL[par][:], src, XH[par][:].bitcast(F32), ALU.subtract).then_inc(Z["xl_ready"], 1)

                def product(g, s):
                    n = g * N + s
                    dve.wait_ge(Z["s_ready"], n + 1)
                    dve.wait_ge(Z["up_ready"], n + 1)
                    at_least(dve, Z["lo_ready"], n - 1)
                    v.tensor_tensor(A[s % 2][:], S[s % 2][:], PV[s % 2][:], ALU.mult).then_inc(Z["a_ready"], 1)

                def high(g, s):
                    n = g * N + s
                    dve.wait_ge(Z["a_ready"], n + 1)
                    at_least(dve, Z["dn_ready"], n - 3)
                    v.tensor_copy(AH[s % 4][:], A[s % 2][:]).then_inc(Z["hi_ready"], 1)

                def low(g, s):
                    n = g * N + s
                    dve.wait_ge(Z["hi_ready"], n + 1)
                    at_least(dve, Z["dn_ready"], n - 3)
                    v.tensor_tensor(AL[s % 4][:], A[s % 2][:], AH[s % 4][:].bitcast(F32),
                                    ALU.subtract).then_inc(Z["lo_ready"], 1)

                def weigh(g, u):
                    if u % HB != HB - 1:
                        return
                    e = u // HB
                    dve.wait_ge(Z["gx_ready"], g * E + e + 1)
                    dve.wait_ge(Z["dn_ready"], g * N + u + 1)
                    at_least(dve, Z["ya_ready"], g * ADDS + (e - 1 if e < 2 else max(1, e - 2)))
                    if two:
                        ins = v.tensor_tensor(YG[e % 2][:], PY[e % 2][:], GX[e % 2][:], ALU.mult)
                    else:
                        ins = v.scalar_tensor_tensor(YG[e % 2][:], PY[e % 2][:], B2[:, e:e + 1], GX[e % 2][:], ALU.add, ALU.mult)
                    ins.then_inc(Z["yg_ready"], 1)

                def presum(g, par):
                    dve.wait_ge(kept_in[par], ctx_count(g, par))
                    v.tensor_tensor(KEPT[par][:], KEPT[par][:], R.x[:, bass.ds(g * GB, GB), :],
                                    ALU.add).then_inc(Z["presummed"], 1)

                def group(g, par, first, last):
                    for s in range(N):
                        if out is not None and s == PRESUM_UNIT:
                            presum(g, par)
                        if two:
                            product(g, s)
                            lagged(g, s, first, 1, low)
                        else:
                            high(g, s)
                            low(g, s)
                        lagged(g, s, first, LAG, weigh)
                        if s == SUM_UNIT and not first:
                            finish(g - 1, 1 - par)
                        if s == SPLIT_UNIT and not last:
                            split_inputs(g + 1, 1 - par)
                    if last:
                        if two:
                            low(g, N - 1)
                        for u in range(N - LAG, N):
                            weigh(g, u)
                        finish(g, par)

                def finish(g, par):
                    dve.wait_ge(Z["px_ready"], g + 1)
                    if out is not None:
                        dve.wait_ge(Z["presummed"], g + 1)
                        v.tensor_tensor(KEPT[par][:], KEPT[par][:], PT[:], ALU.add).then_inc(Z["x_added"], 1)
                        return
                    residual(nc, R, dve, Z["x_added"], g, PT[:], g + 1)

                split_inputs(0, 0)
                v.tensor_copy(g3[:, :, 0, :], X.gates[:]).then_inc(Z["split"], 1)
                dve.wait_ge(Z["split"], 1)
                v.tensor_tensor(rest[:], X.gates[:], g3[:, :, 0, :], ALU.subtract).then_inc(Z["split"], 1)
                dve.wait_ge(Z["split"], 2)
                v.tensor_copy(g3[:, :, 1, :], rest[:]).then_inc(Z["split"], 1)
                dve.wait_ge(Z["split"], 3)
                v.tensor_tensor(rest[:], rest[:], g3[:, :, 1, :], ALU.subtract).then_inc(Z["split"], 1)
                dve.wait_ge(Z["split"], 4)
                v.tensor_copy(g3[:, :, 2, :], rest[:]).then_inc(Z["split"], 1)
                groups_loop(dve, group)

            @block.scalar
            def _(act):
                a = nc.scalar

                def rows(g, s):
                    n = g * N + s
                    act.wait_ge(Z["up_ready"], n + 1)
                    if two:
                        at_least(act, Z["a_ready"], n - 1)
                        a.activation(S[s % 2][:], PU[s % 2][:], ACT.Silu).then_inc(Z["s_ready"], 1)
                    else:
                        at_least(act, Z["lo_ready"], n - 1)
                        a.activation(A[s % 2][:], PU[s % 2][:], ACT.Gelu, bias=B1[:, s:s + 1]).then_inc(Z["a_ready"], 1)

                def high(g, s):
                    n = g * N + s
                    act.wait_ge(Z["a_ready"], n + 1)
                    at_least(act, Z["dn_ready"], n - 3)
                    a.activation(AH[s % 4][:], A[s % 2][:], ACT.Copy).then_inc(Z["hi_ready"], 1)

                def gates_in(g, par):
                    act.wait_ge(Z["gt_psum"], g + 1)
                    at_least(act, Z["ge_ready"], (g - 1) * E)
                    a.activation(G3T[par][:], PT[0:K3, :, :].rearrange("p b t -> p (b t)"),
                                 ACT.Copy).then_inc(Z["gt_ready"], 1)

                def spread(g, u):
                    if u % HB != 0:
                        return
                    e = u // HB
                    act.wait_ge(Z["ge_ready"], g * E + e + 1)
                    at_least(act, Z["yg_ready"], g * E + e - 1)
                    a.activation(GX[e % 2][:], PG[:], ACT.Copy).then_inc(Z["gx_ready"], 1)

                def group(g, par, first, last):
                    for s in range(N):
                        rows(g, s)
                        if two:
                            lagged(g, s, first, 1, high)
                        lagged(g, s, first, LAG, spread)
                        if s == TURN_UNIT and not last:
                            gates_in(g + 1, 1 - par)
                    if last:
                        if two:
                            high(g, N - 1)
                        for u in range(N - LAG, N):
                            spread(g, u)

                gates_in(0, 0)
                groups_loop(act, group)

            @block.tensor
            def _(pe):
                t = nc.tensor

                def up(g, s, par):
                    n = g * N + s
                    at_least(pe, Z["a_ready"], n - 1)
                    if s == 0:
                        pe.wait_ge(Z["xh_ready"], g + 1)
                        pe.wait_ge(Z["xl_ready"], g + 1)
                    w = slice(s * P, (s + 1) * P)
                    last = three_passes(t, PU[s % 2][:], HI["w1"][:, w], LO["w1"][:, w], XH[par][:], XL[par][:])
                    if two:
                        last = three_passes(t, PV[s % 2][:], HI["w2"][:, w], LO["w2"][:, w], XH[par][:], XL[par][:])
                    last.then_inc(Z["up_ready"], 1)

                def down(g, s, par):
                    n = g * N + s
                    e, c = s // HB, s % HB
                    w = slice(s * D, (s + 1) * D)
                    pe.wait_ge(Z["hi_ready"], n + 1)
                    if c == 0:
                        at_least(pe, Z["yg_ready"], g * E + e - 1)
                        pe.wait_ge(Z["gt_ready"], g + 1)
                        at_least(pe, Z["gx_ready"], g * E + e)
                        t.matmul(PG[:], SEL[:, e, :], G3T[par][:], start=True, stop=True).then_inc(Z["ge_ready"], 1)
                    three_passes(t, PY[e % 2][:], HI["wd"][:, w], LO["wd"][:, w], AH[s % 4][:], AL[s % 4][:],
                                 start=(c == 0), stop=(c == HB - 1),
                                 before_lo=lambda: pe.wait_ge(Z["lo_ready"], n + 1)).then_inc(Z["dn_ready"], 1)

                def gates_turn(g, par):
                    pe.wait_ge(Z["gs_ready"], g + 1)
                    at_least(pe, Z["x_added"], g - 1)
                    for j in range(GB):
                        last = t.transpose(PT[0:K3, j, :], GS[par][:, j, :], R.ident[:])
                    last.then_inc(Z["gt_psum"], 1)

                def sums_turn(g, par, turned):
                    pe.wait_ge(Z["ya_ready"], (g + 1) * ADDS)
                    pe.wait_ge(Z["gt_ready"], turned)
                    for j in range(GB):
                        last = t.transpose(PT[:, j, :], YA[par][:, j * P:(j + 1) * P], R.ident[:])
                    last.then_inc(Z["px_ready"], 1)

                def group(g, par, first, last):
                    for s in range(N):
                        up(g, s, par)
                        if s >= LAG:
                            down(g, s - LAG, par)
                        elif not first:
                            down(g - 1, N + s - LAG, 1 - par)
                        if s == SUM_UNIT and not first:
                            sums_turn(g - 1, 1 - par, g + 1)
                        if s == TURN_UNIT and not last:
                            gates_turn(g + 1, 1 - par)
                    if last:
                        for u in range(N - LAG, N):
                            down(g, u, par)
                        sums_turn(g, par, g + 1)

                gates_turn(0, 0)
                groups_loop(pe, group)


def build(nc, I, out):
    with ExitStack() as stack:
        sb, ps, sem = allocator(nc, stack)
        R = Namespace()
        R.x = sb("x", [P, NB, D])
        R.stats = sb("stats", [P, NB, 6])
        R.ident = sb("ident", [P, P])
        R.ident_bf = sb("ident_bf", [P, P], BF16)
        R.ones = sb("ones", [P, P])
        R.ones_bf = sb("ones_bf", [P, P], BF16)
        R.stats_done = sem("stats_done")
        load_phase(nc, R, I)
        attention_phase(nc, R, I, "a0", I["L0_xattn_Wq"], I["L0_xattn_Wk"], I["L0_xattn_Wv"], I["L0_xattn_Wo"],
                        I["L0_xattn_bq"], I["L0_xattn_bk"], I["L0_xattn_bv"], I["L0_xattn_bo"], hepos=True, pad=I["pad"])
        gated_rows_phase(nc, R, I, "f0", "proto")
        attention_phase(nc, R, I, "a1", I["L1_xattn_wq"], I["L1_xattn_wk"], I["L1_xattn_wv"], I["L1_xattn_wo"],
                        I["L1_xattn_bq"], I["L1_xattn_bk"], I["L1_xattn_bv"], I["L1_xattn_bo"])
        gated_rows_phase(nc, R, I, "f1", "shared")
        attention_phase(nc, R, I, "a2", I["L2_xattn_W_q"], I["L2_xattn_W_k"], I["L2_xattn_W_v"], I["L2_xattn_W_o"],
                        I["L2_xattn_b_q"], I["L2_xattn_b_k"], I["L2_xattn_b_v"], I["L2_xattn_b_o"], mask=I["mask"])
        gated_outputs_phase(nc, R, I, "f2", "capacity")
        attention_phase(nc, R, I, "a3", I["L3_xattn_Wq"], I["L3_xattn_Wk"], I["L3_xattn_Wv"], I["L3_xattn_Wo"],
                        causal=I["causal_ctx"])
        renorm_phase(nc, R, out)
        attention_phase(nc, R, I, "s3", I["L3_ffn_wq"], I["L3_ffn_wk"], I["L3_ffn_wv"], I["L3_ffn_wo"],
                        bo=I["L3_ffn_bo"], own_keys=True, causal=I["causal_own"],
                        ln=(I["L3_ffn_ln1_scale"], I["L3_ffn_ln1_shift"]))
        gated_outputs_phase(nc, R, I, "f3", "swiglu", out)


def laid_out(inputs):
    a = {k: np.asarray(v) for k, v in inputs.items()}
    c = np.ascontiguousarray
    order = np.arange(KC).reshape(KCLS, STRIDE).T.reshape(-1)
    r = {
        "x": c(a["x"].transpose(1, 0, 2)),
        "ctxT": c(a["ctx_1024"][:, order, :].transpose(2, 0, 1)),
        "pad": c(a["mask_BxS2_bf0"][:, order].reshape(1, -1)),
        "mask": c(a["mask_1x1xSxS2_ik0"][0, 0][:, order]),
        "temp": a["L0_ffn_temp"].reshape(1, 1),
        "ln2_scale": a["L3_ffn_ln2_scale"], "ln2_shift": a["L3_ffn_ln2_shift"],
    }
    for n in ("Wq", "bq", "Wk", "bk", "Wv", "bv", "Wo", "bo"):
        r[f"L0_xattn_{n}"] = a[f"L0_xattn_{n}"]
        if n[0] == "W":
            r[f"L3_xattn_{n}"] = c(a[f"L3_xattn_{n}"].T)
    for n in ("q", "k", "v", "o"):
        r[f"L1_xattn_w{n}"] = c(a[f"L1_xattn_w{n}"].T)
        r[f"L1_xattn_b{n}"] = a[f"L1_xattn_b{n}"]
        r[f"L2_xattn_W_{n}"] = a[f"L2_xattn_W_{n}"]
        r[f"L2_xattn_b_{n}"] = a[f"L2_xattn_b_{n}"]
        r[f"L3_ffn_w{n}"] = a[f"L3_ffn_w{n}"]
    for n in ("bo", "ln1_scale", "ln1_shift"):
        r[f"L3_ffn_{n}"] = a[f"L3_ffn_{n}"]
    unit_order = np.arange(D).reshape(4, 4, HD).transpose(1, 0, 2).reshape(-1)
    for n in ("L1_xattn_wq", "L1_xattn_wk", "L1_xattn_bq", "L1_xattn_bk", "L2_xattn_W_q", "L2_xattn_W_k",
              "L2_xattn_b_q", "L2_xattn_b_k", "L3_xattn_Wq", "L3_xattn_Wk", "L3_ffn_wq", "L3_ffn_wk"):
        r[n] = c(r[n][..., unit_order])

    def blocks(w):
        return c(w.reshape(-1, P, D).transpose(1, 0, 2))

    r["f0_router"] = c(a["L0_ffn_prototypes"].T)
    r["f0_up"] = c(a["L0_ffn_B"].reshape(-1, D).T)
    r["f0_down"] = c(blocks(a["L0_ffn_A"].transpose(0, 2, 1).reshape(-1, D)).reshape(P, -1))
    r["f0_bias"] = a["L0_ffn_bias"]
    r["f1_router"] = c(a["L1_ffn_router_w"].T)
    up = np.concatenate([a["L1_ffn_shared_up"], a["L1_ffn_routed_up"]])
    down = np.concatenate([a["L1_ffn_shared_down"], a["L1_ffn_routed_down"]])
    r["f1_up"] = c(up.reshape(-1, D).T)
    r["f1_down"] = c(blocks(down.transpose(0, 2, 1).reshape(-1, D)).reshape(P, -1))
    r["f2_router"] = a["L2_ffn_wg"]
    r["f2_w1"] = c(a["L2_ffn_w1"].transpose(1, 0, 2).reshape(D, -1))
    r["f2_wd"] = c(blocks(a["L2_ffn_w2"].reshape(-1, D)).reshape(P, -1))
    r["f2_b1"] = c(a["L2_ffn_b1"].reshape(-1, P).T)
    r["f2_b2"] = c(a["L2_ffn_b2"].T)
    r["f3_router"] = a["L3_ffn_gate_w"]
    for n in ("w1", "w2"):
        r[f"f3_{n}"] = c(a[f"L3_ffn_{n}"].transpose(1, 0, 2).reshape(D, -1))
    r["f3_wd"] = c(blocks(a["L3_ffn_w3"].reshape(-1, D)).reshape(P, -1))

    bf = mybir.dt.np(BF16)
    place = np.arange(P)
    r["ident"] = np.eye(P, dtype=np.float32)
    r["ident_bf"] = np.eye(P).astype(bf)
    r["tri"] = (place[:, None] <= place[None, :]).astype(bf)
    r["slots"] = (np.arange(96)[:, None] % 32 // HD == np.arange(4)[None, :]).astype(np.float32)
    head = np.arange(P) // HD
    r["slot_classes"] = ((head[:, None, None] // 4 == np.arange(4)[:, None]) &
                         (head[:, None, None] % 4 == np.arange(STRIDE))).astype(np.float32)
    r["classes"] = (np.arange(KC)[:, None] // KCLS == np.arange(32)[None, :] // HD).astype(np.float32)
    r["causal_ctx"] = np.where(order[None, :] > place[:, None], FAR, 0).astype(bf)
    r["causal_own"] = np.where(place[None, :] > place[:, None], FAR, 0).astype(bf)
    for e in (8, 16, 32):
        r[f"rank{e}"] = (e - np.arange(e, dtype=np.float32)).reshape(1, e)
    for n, e, blocks_, rows in (("f0", 32, 4, 16), ("f1", 16, 8, 64), ("f2", 8, 8, P), ("f3", 8, 8, P)):
        owner = np.arange(blocks_ * P).reshape(blocks_, P) // rows
        term = np.tile(np.arange(e), 3)
        term = np.concatenate([term, np.full(96 - 3 * e, -1)])
        r[f"{n}_sel"] = (term[:, None, None] == owner[None]).astype(bf)
    return r


def kernel(**inputs):
    import concourse.bacc as bacc
    from concourse.bass_utils import run_bass_kernel_spmd

    nc = bacc.Bacc("TRN2", target_bir_lowering=False, num_devices=1)
    arrays, I = {}, {}
    for name, a in laid_out(inputs).items():
        arrays["in_" + name] = a
        I[name] = nc.dram_tensor("in_" + name, a.shape, mybir.dt.from_np(a.dtype), kind="ExternalInput").ap()
    out = nc.dram_tensor("out_x", (NB, P, D), F32, kind="ExternalOutput").ap()
    build(nc, I, out)
    result = run_bass_kernel_spmd(nc, [arrays], core_ids=[0])
    return result.results[0]["out_x"]
```
